# Optimizing a Trainium2 kernel written in Bass

```python
import numpy as np
import jax
import jax.numpy as jnp

def _softmax(x, axis=-1):
    return jax.nn.softmax(x, axis=axis)

def _gelu(x):
    return jax.nn.gelu(x, approximate=True)

def _silu(x):
    return jax.nn.silu(x)

def _sigmoid(x):
    return jax.nn.sigmoid(x)

def _layernorm(x, axis=-1, eps=1e-05):
    m = jnp.mean(x, axis=axis, keepdims=True)
    v = jnp.var(x, axis=axis, keepdims=True)
    return (x - m) / jnp.sqrt(v + eps)

def _scatter_add(tgt, idx, src, axis=0):
    return tgt.at[idx].add(src)

def _segment_sum(src, seg, n):
    return jax.ops.segment_sum(src, seg, n)
kernel_name = 'mk_gnn_ffn_d4_gnn_r8_5af5a5'

def setup_inputs(seed: int=0):
    np.random.seed(seed)
    _w = jnp.asarray

    def _rec_inputs():
        import jax
        import jax.numpy as jnp
        _gk = jax.random.key(seed)
        x = -8.776e-05 + 1 * jax.random.normal(jax.random.fold_in(_gk, 1), (1250, 512), jnp.float32)
        src = jax.random.randint(jax.random.fold_in(_gk, 2), (20000,), 0, 1250, jnp.int32)
        dst = jnp.minimum((1250 * jax.random.uniform(jax.random.fold_in(_gk, 3), (20000,)) ** 2.0).astype(jnp.int32), 9999)
        _o = jnp.argsort(dst, stable=True)
        src = src[_o]
        dst = dst[_o]
        edge_attr_4 = 0.000126197 + 0.999763 * jax.random.normal(jax.random.fold_in(_gk, 13), (20000, 4), jnp.float32)
        return (x, src, dst, edge_attr_4)
    x, src, dst, edge_attr_4 = _rec_inputs()

    def _L0_gnn_setup():
        import jax, jax.numpy as jnp
        import numpy as np
        N = 1250
        E = 20000
        DIN = 512
        DOUT = 512
        key = jax.random.key(seed)
        k1, k2, k3 = jax.random.split(key, 3)
        x = jax.random.normal(k1, (N, DIN), dtype=jnp.float32)
        edge_index = jax.random.randint(k2, (2, E), 0, N, dtype=jnp.int32)
        W = jax.random.normal(k3, (DIN, DOUT), dtype=jnp.float32) * (1.0 / np.sqrt(DIN))
        b = jnp.zeros((DOUT,), dtype=jnp.float32)
        return {'x': x, 'edge_index': edge_index, 'W': W, 'b': b}
    _L0_gnn_all = _L0_gnn_setup()
    _L0_gnn_in = {k: v for k, v in _L0_gnn_all.items() if k in ('W', 'b')}
    del _L0_gnn_all

    def _L0_ffn_setup():
        import jax, jax.numpy as jnp
        import numpy as np
        DIM = 512
        NE = 8
        TOPK = 2
        CF = 1.2
        HID = 4 * DIM
        B, S = (8, 512)
        key = jax.random.key(seed)
        ks = jax.random.split(key, 4)
        s = 0.02
        return {'x': jax.random.normal(ks[0], (B, S, DIM), jnp.float32), 'gate_w': jax.random.normal(ks[1], (NE, DIM), jnp.float32) * s, 'gate_b': jnp.zeros((NE,), jnp.float32), 'w1': jax.random.normal(ks[2], (NE, DIM, HID), jnp.float32) * s, 'b1': jnp.zeros((NE, HID), jnp.float32), 'w2': jax.random.normal(ks[3], (NE, HID, DIM), jnp.float32) * s, 'b2': jnp.zeros((NE, DIM), jnp.float32)}
    _L0_ffn_all = _L0_ffn_setup()
    _L0_ffn_in = {k: v for k, v in _L0_ffn_all.items() if k in ('gate_w', 'gate_b', 'w1', 'b1', 'w2', 'b2')}
    del _L0_ffn_all

    def _L1_gnn_setup():
        import jax, jax.numpy as jnp
        import numpy as np
        N = 2500
        E = 40000
        IN = 512
        H = 4
        C = 128
        ED = 4
        NEG_SLOPE = 0.2
        BN_EPS = 1e-05

        def _edge_gat(x, edge_index, edge_attr, W, W_edge, att_src, att_dst, att_edge, bias, gamma, beta):
            n = x.shape[0]
            loop = jnp.arange(n, dtype=edge_index.dtype)
            src = jnp.concatenate([edge_index[0], loop])
            dst = jnp.concatenate([edge_index[1], loop])
            ea = jnp.concatenate([edge_attr, jnp.broadcast_to(edge_attr.mean(0), (n, edge_attr.shape[1]))], 0)
            h = (x @ W).reshape(n, H, C)
            a_src = (h * att_src[None]).sum(-1)
            a_dst = (h * att_dst[None]).sum(-1)
            e = (ea @ W_edge).reshape(-1, H, C)
            a_edge = (e * att_edge[None]).sum(-1)
            alpha = a_src[src] + a_dst[dst] + a_edge
            alpha = jax.nn.leaky_relu(alpha, NEG_SLOPE)
            amax = jax.lax.stop_gradient(jax.ops.segment_max(alpha, dst, num_segments=n))
            ex = jnp.exp(alpha - amax[dst])
            denom = jax.ops.segment_sum(ex, dst, num_segments=n)
            att = ex / (denom[dst] + 1e-16)
            msg = h[src] * att[:, :, None]
            out = jax.ops.segment_sum(msg, dst, num_segments=n).reshape(n, H * C) + bias
            mu = out.mean(0)
            var = out.var(0)
            return (out - mu) / jnp.sqrt(var + BN_EPS) * gamma + beta
        key = jax.random.key(seed)
        ks = jax.random.split(key, 10)
        x = jax.random.normal(ks[0], (N, IN), dtype=jnp.float32)
        edge_index = jax.random.randint(ks[1], (2, E), 0, N, dtype=jnp.int64)
        edge_attr = jax.random.normal(ks[2], (E, ED), dtype=jnp.float32)
        W = jax.random.normal(ks[3], (IN, H * C), dtype=jnp.float32) / np.sqrt(IN)
        W_edge = jax.random.normal(ks[4], (ED, H * C), dtype=jnp.float32) / np.sqrt(ED)
        att_src = jax.random.normal(ks[5], (H, C), dtype=jnp.float32) / np.sqrt(C)
        att_dst = jax.random.normal(ks[6], (H, C), dtype=jnp.float32) / np.sqrt(C)
        att_edge = jax.random.normal(ks[7], (H, C), dtype=jnp.float32) / np.sqrt(C)
        bias = jnp.zeros((H * C,), dtype=jnp.float32)
        gamma = jnp.ones((H * C,), dtype=jnp.float32)
        beta = jnp.zeros((H * C,), dtype=jnp.float32)
        return {'x': x, 'edge_index': edge_index, 'edge_attr': edge_attr, 'W': W, 'W_edge': W_edge, 'att_src': att_src, 'att_dst': att_dst, 'att_edge': att_edge, 'bias': bias, 'gamma': gamma, 'beta': beta}
    _L1_gnn_all = _L1_gnn_setup()
    _L1_gnn_in = {k: v for k, v in _L1_gnn_all.items() if k in ('W', 'W_edge', 'att_src', 'att_dst', 'att_edge', 'bias', 'gamma', 'beta')}
    del _L1_gnn_all

    def _L1_ffn_setup():
        import jax, jax.numpy as jnp
        import numpy as np
        B, S, D = (8, 512, 512)
        H = 256
        O = 512
        E = 8
        TOP_K = 1
        key = jax.random.key(seed)
        ks = jax.random.split(key, 8)
        sc = 0.02
        return {'x': jax.random.normal(ks[0], (B, S, D), dtype=jnp.float32), 'Wr': jax.random.normal(ks[1], (D, E), dtype=jnp.float32) * sc, 'br': jnp.zeros((E,), dtype=jnp.float32), 'W1': jax.random.normal(ks[2], (E, D, H), dtype=jnp.float32) * sc, 'b1': jnp.zeros((E, H), dtype=jnp.float32), 'W2': jax.random.normal(ks[3], (E, H, O), dtype=jnp.float32) * sc, 'b2': jnp.zeros((E, O), dtype=jnp.float32)}
    _L1_ffn_all = _L1_ffn_setup()
    _L1_ffn_in = {k: v for k, v in _L1_ffn_all.items() if k in ('Wr', 'br', 'W1', 'b1', 'W2', 'b2')}
    del _L1_ffn_all

    def _L2_gnn_setup():
        import jax, jax.numpy as jnp
        import numpy as np
        N_NODES = 1250
        N_EDGES = 20000
        IN_DIM = 512
        HID = 256
        HEADS = 4
        OUT_DIM = 512
        NEG_SLOPE = 0.2

        def _glorot(key, shape):
            fan_in, fan_out = (shape[0], shape[-1])
            lim = jnp.sqrt(6.0 / (fan_in + fan_out))
            return jax.random.uniform(key, shape, jnp.float32, -lim, lim)

        def gat_conv(x, src, dst, W, att_src, att_dst, bias):
            N = x.shape[0]
            h = (x @ W).reshape(N, HEADS, HID)
            a_src = jnp.sum(h * att_src, axis=-1)
            a_dst = jnp.sum(h * att_dst, axis=-1)
            e = jax.nn.leaky_relu(a_src[src] + a_dst[dst], NEG_SLOPE)
            m = jax.ops.segment_max(e, dst, num_segments=N)
            e = jnp.exp(e - m[dst])
            s = jax.ops.segment_sum(e, dst, num_segments=N)
            alpha = e / (s[dst] + 1e-16)
            msg = alpha[:, :, None] * h[src]
            out = jax.ops.segment_sum(msg, dst, num_segments=N)
            return out.reshape(N, HEADS * HID) + bias
        key = jax.random.key(seed)
        ks = jax.random.split(key, 16)
        x = jax.random.normal(ks[0], (N_NODES, IN_DIM), jnp.float32)
        edge_index = jax.random.randint(ks[1], (2, N_EDGES), 0, N_NODES, jnp.int64)
        W1 = _glorot(ks[2], (IN_DIM, HEADS * HID))
        att_src1 = _glorot(ks[3], (HEADS, HID))
        att_dst1 = _glorot(ks[4], (HEADS, HID))
        b1 = jnp.zeros((HEADS * HID,), jnp.float32)
        W2 = _glorot(ks[5], (HEADS * HID, HEADS * HID))
        att_src2 = _glorot(ks[6], (HEADS, HID))
        att_dst2 = _glorot(ks[7], (HEADS, HID))
        b2 = jnp.zeros((HEADS * HID,), jnp.float32)
        fcW = _glorot(ks[8], (HEADS * HID, OUT_DIM))
        fcb = jnp.zeros((OUT_DIM,), jnp.float32)
        return dict(x=x, edge_index=edge_index, W1=W1, att_src1=att_src1, att_dst1=att_dst1, b1=b1, W2=W2, att_src2=att_src2, att_dst2=att_dst2, b2=b2, fcW=fcW, fcb=fcb)
    _L2_gnn_all = _L2_gnn_setup()
    _L2_gnn_in = {k: v for k, v in _L2_gnn_all.items() if k in ('W1', 'att_src1', 'att_dst1', 'b1', 'W2', 'att_src2', 'att_dst2', 'b2', 'fcW', 'fcb')}
    del _L2_gnn_all

    def _L2_ffn_setup():
        import jax, jax.numpy as jnp
        import numpy as np
        B, S, D, F, E = (8, 512, 512, 256, 8)
        INIT_LAMBDA = 0.2
        LN_EPS = 1e-05
        LN_MERGE = 0.03
        key = jax.random.key(seed)
        ks = jax.random.split(key, 12)
        n = lambda k, shp, s=1.0: jax.random.normal(k, shp, dtype=jnp.float32) * s
        return {'hidden_states': n(ks[0], (B, S, D)), 'gfc1_w': n(ks[1], (D, D), 0.01), 'gfc1_b': jnp.zeros((D,), jnp.float32), 'gfc2_w': n(ks[2], (E, D), 0.01), 'gfc2_b': jnp.full((E,), INIT_LAMBDA, dtype=jnp.float32), 'W1': n(ks[3], (F, D), 0.02), 'b1': jnp.zeros((F,), jnp.float32), 'W2': n(ks[4], (D, F), 0.02), 'b2': jnp.zeros((D,), jnp.float32), 'ln_g': jnp.ones((D,), jnp.float32), 'ln_b': jnp.zeros((D,), jnp.float32), 'tv_W1': n(ks[5], (E, F, D), 0.02), 'tv_b1': n(ks[6], (E, F), 0.02), 'tv_W2': n(ks[7], (E, D, F), 0.02), 'tv_b2': n(ks[8], (E, D), 0.02), 'tv_ln_g': n(ks[9], (E, D), 0.02), 'tv_ln_b': n(ks[10], (E, D), 0.02)}
    _L2_ffn_all = _L2_ffn_setup()
    _L2_ffn_in = {k: v for k, v in _L2_ffn_all.items() if k in ('gfc1_w', 'gfc1_b', 'gfc2_w', 'gfc2_b', 'W1', 'b1', 'W2', 'b2', 'ln_g', 'ln_b', 'tv_W1', 'tv_b1', 'tv_W2', 'tv_b2', 'tv_ln_g', 'tv_ln_b')}
    del _L2_ffn_all

    def _L3_gnn_setup():
        import jax, jax.numpy as jnp
        import numpy as np
        N_NODES = 1250
        N_EDGES = 20000
        IN_DIM = 512
        OUT_DIM = 512
        LN_EPS = 1e-05
        key = jax.random.key(seed)
        k_x, k_src, k_ws, k_wn = jax.random.split(key, 4)
        x = jax.random.normal(k_x, (N_NODES, IN_DIM), dtype=jnp.float32)
        edge_src = jax.random.randint(k_src, (N_EDGES,), 0, N_NODES, dtype=jnp.int32)
        edge_dst = jnp.repeat(jnp.arange(N_NODES, dtype=jnp.int32), N_EDGES // N_NODES)
        deg = jnp.full((N_NODES,), float(N_EDGES // N_NODES), dtype=jnp.float32)
        scale = 1.0 / np.sqrt(IN_DIM)
        W_self = jax.random.normal(k_ws, (OUT_DIM, IN_DIM), dtype=jnp.float32) * scale
        W_neigh = jax.random.normal(k_wn, (OUT_DIM, IN_DIM), dtype=jnp.float32) * scale
        bias = jnp.zeros((OUT_DIM,), dtype=jnp.float32)
        gamma = jnp.ones((OUT_DIM,), dtype=jnp.float32)
        beta = jnp.zeros((OUT_DIM,), dtype=jnp.float32)
        return {'x': x, 'edge_src': edge_src, 'edge_dst': edge_dst, 'deg': deg, 'W_self': W_self, 'W_neigh': W_neigh, 'bias': bias, 'gamma': gamma, 'beta': beta}
    _L3_gnn_all = _L3_gnn_setup()
    _L3_gnn_in = {k: v for k, v in _L3_gnn_all.items() if k in ('W_self', 'W_neigh', 'bias', 'gamma', 'beta')}
    del _L3_gnn_all

    def _L3_ffn_setup():
        import jax, jax.numpy as jnp
        import numpy as np
        NUM_EXPERTS = 32
        GROUP_SIZE = 4
        NUM_GROUPS = NUM_EXPERTS // GROUP_SIZE
        C_CAP = 1.0
        key = jax.random.key(seed)
        ks = jax.random.split(key, 5)
        B, S, H = (16, 256, 512)
        D_FF = int(H * 4 * (2.0 / 3.0))
        x = jax.random.normal(ks[0], (B, S, H), dtype=jnp.float32)
        W_router = jax.random.normal(ks[1], (H, NUM_EXPERTS), dtype=jnp.float32) * (1.0 / np.sqrt(H))
        b_router = jnp.zeros((NUM_EXPERTS,), dtype=jnp.float32)
        W_up = jax.random.normal(ks[2], (NUM_GROUPS, H, D_FF), dtype=jnp.float32) * (1.0 / np.sqrt(H))
        b_up = jnp.zeros((NUM_GROUPS, D_FF), dtype=jnp.float32)
        W_down = jax.random.normal(ks[3], (NUM_EXPERTS, D_FF, H), dtype=jnp.float32) * (1.0 / np.sqrt(D_FF))
        b_down = jnp.zeros((NUM_EXPERTS, H), dtype=jnp.float32)
        return {'x': x, 'W_router': W_router, 'b_router': b_router, 'W_up': W_up, 'b_up': b_up, 'W_down': W_down, 'b_down': b_down}
    _L3_ffn_all = _L3_ffn_setup()
    _L3_ffn_in = {k: v for k, v in _L3_ffn_all.items() if k in ('W_router', 'b_router', 'W_up', 'b_up', 'W_down', 'b_down')}
    del _L3_ffn_all
    return {'x': x, 'src': src, 'dst': dst, 'edge_attr_4': edge_attr_4, 'L0_gnn_W': _L0_gnn_in['W'], 'L0_gnn_b': _L0_gnn_in['b'], 'L0_ffn_gate_w': _L0_ffn_in['gate_w'], 'L0_ffn_gate_b': _L0_ffn_in['gate_b'], 'L0_ffn_w1': _L0_ffn_in['w1'], 'L0_ffn_b1': _L0_ffn_in['b1'], 'L0_ffn_w2': _L0_ffn_in['w2'], 'L0_ffn_b2': _L0_ffn_in['b2'], 'L1_gnn_W': _L1_gnn_in['W'], 'L1_gnn_W_edge': _L1_gnn_in['W_edge'], 'L1_gnn_att_src': _L1_gnn_in['att_src'], 'L1_gnn_att_dst': _L1_gnn_in['att_dst'], 'L1_gnn_att_edge': _L1_gnn_in['att_edge'], 'L1_gnn_bias': _L1_gnn_in['bias'], 'L1_gnn_gamma': _L1_gnn_in['gamma'], 'L1_gnn_beta': _L1_gnn_in['beta'], 'L1_ffn_Wr': _L1_ffn_in['Wr'], 'L1_ffn_br': _L1_ffn_in['br'], 'L1_ffn_W1': _L1_ffn_in['W1'], 'L1_ffn_b1': _L1_ffn_in['b1'], 'L1_ffn_W2': _L1_ffn_in['W2'], 'L1_ffn_b2': _L1_ffn_in['b2'], 'L2_gnn_W1': _L2_gnn_in['W1'], 'L2_gnn_att_src1': _L2_gnn_in['att_src1'], 'L2_gnn_att_dst1': _L2_gnn_in['att_dst1'], 'L2_gnn_b1': _L2_gnn_in['b1'], 'L2_gnn_W2': _L2_gnn_in['W2'], 'L2_gnn_att_src2': _L2_gnn_in['att_src2'], 'L2_gnn_att_dst2': _L2_gnn_in['att_dst2'], 'L2_gnn_b2': _L2_gnn_in['b2'], 'L2_gnn_fcW': _L2_gnn_in['fcW'], 'L2_gnn_fcb': _L2_gnn_in['fcb'], 'L2_ffn_gfc1_w': _L2_ffn_in['gfc1_w'], 'L2_ffn_gfc1_b': _L2_ffn_in['gfc1_b'], 'L2_ffn_gfc2_w': _L2_ffn_in['gfc2_w'], 'L2_ffn_gfc2_b': _L2_ffn_in['gfc2_b'], 'L2_ffn_W1': _L2_ffn_in['W1'], 'L2_ffn_b1': _L2_ffn_in['b1'], 'L2_ffn_W2': _L2_ffn_in['W2'], 'L2_ffn_b2': _L2_ffn_in['b2'], 'L2_ffn_ln_g': _L2_ffn_in['ln_g'], 'L2_ffn_ln_b': _L2_ffn_in['ln_b'], 'L2_ffn_tv_W1': _L2_ffn_in['tv_W1'], 'L2_ffn_tv_b1': _L2_ffn_in['tv_b1'], 'L2_ffn_tv_W2': _L2_ffn_in['tv_W2'], 'L2_ffn_tv_b2': _L2_ffn_in['tv_b2'], 'L2_ffn_tv_ln_g': _L2_ffn_in['tv_ln_g'], 'L2_ffn_tv_ln_b': _L2_ffn_in['tv_ln_b'], 'L3_gnn_W_self': _L3_gnn_in['W_self'], 'L3_gnn_W_neigh': _L3_gnn_in['W_neigh'], 'L3_gnn_bias': _L3_gnn_in['bias'], 'L3_gnn_gamma': _L3_gnn_in['gamma'], 'L3_gnn_beta': _L3_gnn_in['beta'], 'L3_ffn_W_router': _L3_ffn_in['W_router'], 'L3_ffn_b_router': _L3_ffn_in['b_router'], 'L3_ffn_W_up': _L3_ffn_in['W_up'], 'L3_ffn_b_up': _L3_ffn_in['b_up'], 'L3_ffn_W_down': _L3_ffn_in['W_down'], 'L3_ffn_b_down': _L3_ffn_in['b_down']}

def reference(x, src, dst, edge_attr_4, L0_gnn_W, L0_gnn_b, L0_ffn_gate_w, L0_ffn_gate_b, L0_ffn_w1, L0_ffn_b1, L0_ffn_w2, L0_ffn_b2, L1_gnn_W, L1_gnn_W_edge, L1_gnn_att_src, L1_gnn_att_dst, L1_gnn_att_edge, L1_gnn_bias, L1_gnn_gamma, L1_gnn_beta, L1_ffn_Wr, L1_ffn_br, L1_ffn_W1, L1_ffn_b1, L1_ffn_W2, L1_ffn_b2, L2_gnn_W1, L2_gnn_att_src1, L2_gnn_att_dst1, L2_gnn_b1, L2_gnn_W2, L2_gnn_att_src2, L2_gnn_att_dst2, L2_gnn_b2, L2_gnn_fcW, L2_gnn_fcb, L2_ffn_gfc1_w, L2_ffn_gfc1_b, L2_ffn_gfc2_w, L2_ffn_gfc2_b, L2_ffn_W1, L2_ffn_b1, L2_ffn_W2, L2_ffn_b2, L2_ffn_ln_g, L2_ffn_ln_b, L2_ffn_tv_W1, L2_ffn_tv_b1, L2_ffn_tv_W2, L2_ffn_tv_b2, L2_ffn_tv_ln_g, L2_ffn_tv_ln_b, L3_gnn_W_self, L3_gnn_W_neigh, L3_gnn_bias, L3_gnn_gamma, L3_gnn_beta, L3_ffn_W_router, L3_ffn_b_router, L3_ffn_W_up, L3_ffn_b_up, L3_ffn_W_down, L3_ffn_b_down):
    import jax
    import jax.numpy as jnp

    def _L0_gnn_ref(x, edge_index, W, b):
        import jax, jax.numpy as jnp
        import numpy as np
        N = 1250
        E = 20000
        DIN = 512
        DOUT = 512
        n = x.shape[0]
        src, dst = (edge_index[0], edge_index[1])
        loop = jnp.arange(n, dtype=src.dtype)
        src = jnp.concatenate([src, loop])
        dst = jnp.concatenate([dst, loop])
        deg = jax.ops.segment_sum(jnp.ones_like(src, dtype=x.dtype), dst, num_segments=n)
        dinv = jnp.where(deg > 0, jax.lax.rsqrt(jnp.maximum(deg, 1e-12)), 0.0)
        norm = dinv[src] * dinv[dst]
        h = x @ W
        msg = h[src] * norm[:, None]
        out = jax.ops.segment_sum(msg, dst, num_segments=n) + b
        return jax.nn.relu(out)

    def _L0_ffn_ref(x, gate_w, gate_b, w1, b1, w2, b2):
        import jax, jax.numpy as jnp
        import numpy as np
        DIM = 512
        NE = 8
        TOPK = 2
        CF = 1.2
        HID = 4 * DIM
        B, S = (8, 512)
        Bq, Sq, D = x.shape
        T = Bq * Sq
        cap = int(CF * T / NE)
        xf = x.reshape(T, D)
        probs = jax.nn.softmax(xf @ gate_w.T + gate_b, axis=-1)
        topw, topi = jax.lax.top_k(probs, TOPK)
        onehot = jax.nn.one_hot(topi, NE, dtype=topw.dtype)
        w_te = jnp.einsum('tk,tke->te', topw, onehot)
        routed = onehot.sum(axis=1) > 0
        wm = jnp.where(routed, w_te, -1.0)
        sel_w, sel_idx = jax.lax.top_k(wm.T, cap)
        sel_w = jnp.maximum(sel_w, 0.0)
        xg = xf[sel_idx]
        h = jax.nn.gelu(jnp.einsum('ecd,edh->ech', xg, w1) + b1[:, None, :], approximate=False)
        out = jnp.einsum('ech,ehd->ecd', h, w2) + b2[:, None, :]
        weighted = out * sel_w[..., None]
        of = jnp.zeros((T, D), x.dtype).at[sel_idx.reshape(-1)].add(weighted.reshape(-1, D))
        return of.reshape(Bq, Sq, D)

    def _L1_gnn_ref(x, edge_index, edge_attr, W, W_edge, att_src, att_dst, att_edge, bias, gamma, beta):
        import jax, jax.numpy as jnp
        import numpy as np
        N = 2500
        E = 40000
        IN = 512
        H = 4
        C = 128
        ED = 4
        NEG_SLOPE = 0.2
        BN_EPS = 1e-05

        def _edge_gat(x, edge_index, edge_attr, W, W_edge, att_src, att_dst, att_edge, bias, gamma, beta):
            n = x.shape[0]
            loop = jnp.arange(n, dtype=edge_index.dtype)
            src = jnp.concatenate([edge_index[0], loop])
            dst = jnp.concatenate([edge_index[1], loop])
            ea = jnp.concatenate([edge_attr, jnp.broadcast_to(edge_attr.mean(0), (n, edge_attr.shape[1]))], 0)
            h = (x @ W).reshape(n, H, C)
            a_src = (h * att_src[None]).sum(-1)
            a_dst = (h * att_dst[None]).sum(-1)
            e = (ea @ W_edge).reshape(-1, H, C)
            a_edge = (e * att_edge[None]).sum(-1)
            alpha = a_src[src] + a_dst[dst] + a_edge
            alpha = jax.nn.leaky_relu(alpha, NEG_SLOPE)
            amax = jax.lax.stop_gradient(jax.ops.segment_max(alpha, dst, num_segments=n))
            ex = jnp.exp(alpha - amax[dst])
            denom = jax.ops.segment_sum(ex, dst, num_segments=n)
            att = ex / (denom[dst] + 1e-16)
            msg = h[src] * att[:, :, None]
            out = jax.ops.segment_sum(msg, dst, num_segments=n).reshape(n, H * C) + bias
            mu = out.mean(0)
            var = out.var(0)
            return (out - mu) / jnp.sqrt(var + BN_EPS) * gamma + beta
        return _edge_gat(x, edge_index, edge_attr, W, W_edge, att_src, att_dst, att_edge, bias, gamma, beta)

    def _L1_ffn_ref(x, Wr, br, W1, b1, W2, b2):
        import jax, jax.numpy as jnp
        import numpy as np
        B, S, D = (8, 512, 512)
        H = 256
        O = 512
        E = 8
        TOP_K = 1
        b, s, d = x.shape
        xf = x.reshape(-1, d)
        router_logits = xf @ Wr + br
        topk_logits, topk_idx = jax.lax.top_k(router_logits, TOP_K)
        topk_gates = jax.nn.softmax(topk_logits, axis=1)
        out = jnp.zeros((xf.shape[0], O), dtype=x.dtype)
        for k in range(TOP_K):
            idx_k = topk_idx[:, k]
            gate_k = topk_gates[:, k:k + 1]
            for e in range(E):
                h = jax.nn.relu(xf @ W1[e] + b1[e])
                oe = h @ W2[e] + b2[e]
                mask = (idx_k == e)[:, None]
                out = out + jnp.where(mask, gate_k * oe, 0.0)
        return out.reshape(b, s, O)

    def _L2_gnn_ref(x, edge_index, W1, att_src1, att_dst1, b1, W2, att_src2, att_dst2, b2, fcW, fcb):
        import jax, jax.numpy as jnp
        import numpy as np
        N_NODES = 1250
        N_EDGES = 20000
        IN_DIM = 512
        HID = 256
        HEADS = 4
        OUT_DIM = 512
        NEG_SLOPE = 0.2

        def _glorot(key, shape):
            fan_in, fan_out = (shape[0], shape[-1])
            lim = jnp.sqrt(6.0 / (fan_in + fan_out))
            return jax.random.uniform(key, shape, jnp.float32, -lim, lim)

        def gat_conv(x, src, dst, W, att_src, att_dst, bias):
            N = x.shape[0]
            h = (x @ W).reshape(N, HEADS, HID)
            a_src = jnp.sum(h * att_src, axis=-1)
            a_dst = jnp.sum(h * att_dst, axis=-1)
            e = jax.nn.leaky_relu(a_src[src] + a_dst[dst], NEG_SLOPE)
            m = jax.ops.segment_max(e, dst, num_segments=N)
            e = jnp.exp(e - m[dst])
            s = jax.ops.segment_sum(e, dst, num_segments=N)
            alpha = e / (s[dst] + 1e-16)
            msg = alpha[:, :, None] * h[src]
            out = jax.ops.segment_sum(msg, dst, num_segments=N)
            return out.reshape(N, HEADS * HID) + bias
        N = x.shape[0]
        loops = jnp.arange(N, dtype=edge_index.dtype)
        src = jnp.concatenate([edge_index[0], loops])
        dst = jnp.concatenate([edge_index[1], loops])
        h = gat_conv(x, src, dst, W1, att_src1, att_dst1, b1)
        h = jax.nn.relu(h)
        h = gat_conv(h, src, dst, W2, att_src2, att_dst2, b2)
        h = jax.nn.relu(h)
        return h @ fcW + fcb

    def _L2_ffn_ref(hidden_states, gfc1_w, gfc1_b, gfc2_w, gfc2_b, W1, b1, W2, b2, ln_g, ln_b, tv_W1, tv_b1, tv_W2, tv_b2, tv_ln_g, tv_ln_b):
        import jax, jax.numpy as jnp
        import numpy as np
        B, S, D, F, E = (8, 512, 512, 256, 8)
        INIT_LAMBDA = 0.2
        LN_EPS = 1e-05
        LN_MERGE = 0.03
        x = hidden_states
        gh = jax.nn.relu(jnp.einsum('bsd,hd->bsh', x, gfc1_w) + gfc1_b)
        g = (jnp.einsum('bsh,eh->bse', gh, gfc2_w) + gfc2_b).mean(axis=1)
        W1m = W1 + jnp.einsum('be,efd->bfd', g, tv_W1)
        b1m = b1 + g @ tv_b1
        W2m = W2 + jnp.einsum('be,edf->bdf', g, tv_W2)
        b2m = b2 + g @ tv_b2
        lng = ln_g + LN_MERGE * (tv_ln_g - ln_g).sum(axis=0)
        lnb = ln_b + LN_MERGE * (tv_ln_b - ln_b).sum(axis=0)
        h = jax.nn.relu(jnp.einsum('bsd,bfd->bsf', x, W1m) + b1m[:, None, :])
        out = jnp.einsum('bsf,bdf->bsd', h, W2m) + b2m[:, None, :]
        res = x + out
        mu = res.mean(axis=-1, keepdims=True)
        var = res.var(axis=-1, keepdims=True)
        return (res - mu) * jax.lax.rsqrt(var + LN_EPS) * lng + lnb

    def _L3_gnn_ref(x, edge_src, edge_dst, deg, W_self, W_neigh, bias, gamma, beta):
        import jax, jax.numpy as jnp
        import numpy as np
        N_NODES = 1250
        N_EDGES = 20000
        IN_DIM = 512
        OUT_DIM = 512
        LN_EPS = 1e-05
        n = x.shape[0]
        h_self = jnp.einsum('nd,od->no', x, W_self)
        neigh_sum = jax.ops.segment_sum(x[edge_src], edge_dst, num_segments=n)
        neigh_mean = neigh_sum / jnp.maximum(deg, 1.0)[:, None]
        h_neigh = jnp.einsum('nd,od->no', neigh_mean, W_neigh)
        h = h_self + h_neigh + bias
        mu = jnp.mean(h, axis=-1, keepdims=True)
        var = jnp.mean(jnp.square(h - mu), axis=-1, keepdims=True)
        h = (h - mu) * jax.lax.rsqrt(var + LN_EPS)
        return h * gamma + beta

    def _L3_ffn_ref(x, W_router, b_router, W_up, b_up, W_down, b_down):
        import jax, jax.numpy as jnp
        import numpy as np
        NUM_EXPERTS = 32
        GROUP_SIZE = 4
        NUM_GROUPS = NUM_EXPERTS // GROUP_SIZE
        C_CAP = 1.0
        B, S, H = x.shape
        bs = B * S
        E = NUM_EXPERTS
        k = min(int(bs * C_CAP) // E, bs)
        xf = x.reshape(bs, H)
        h = xf @ W_router + b_router
        Sm = jax.nn.softmax(h, axis=-1)
        G_ek, idx_ek = jax.lax.top_k(Sm.T, k)
        tokens = xf[idx_ek]
        D_FF = W_up.shape[-1]
        tok_g = tokens.reshape(NUM_GROUPS, GROUP_SIZE, k, H)
        up = jnp.einsum('gjkh,ghf->gjkf', tok_g, W_up) + b_up[:, None, None, :]
        act = jax.nn.silu(up).reshape(E, k, D_FF)
        Eout = jnp.einsum('ekf,efh->ekh', act, W_down) + b_down[:, None, :]
        weighted = G_ek[..., None] * Eout
        y = jnp.zeros((bs, H), dtype=x.dtype).at[idx_ek.reshape(-1)].add(weighted.reshape(-1, H))
        return y.reshape(B, S, H)
    edge_index = jnp.stack([src, dst])
    deg = jnp.maximum(jax.ops.segment_sum(jnp.ones(dst.shape, jnp.float32), dst, num_segments=1250), 1.0)
    x = x + _L0_gnn_ref(_layernorm(x, axis=-1), edge_index, L0_gnn_W, L0_gnn_b)
    x = x + _L0_ffn_ref(_layernorm(x, axis=-1)[None], L0_ffn_gate_w, L0_ffn_gate_b, L0_ffn_w1, L0_ffn_b1, L0_ffn_w2, L0_ffn_b2)[0]
    x = x + _L1_gnn_ref(_layernorm(x, axis=-1), edge_index, edge_attr_4, L1_gnn_W, L1_gnn_W_edge, L1_gnn_att_src, L1_gnn_att_dst, L1_gnn_att_edge, L1_gnn_bias, L1_gnn_gamma, L1_gnn_beta)
    x = x + _L1_ffn_ref(_layernorm(x, axis=-1)[None], L1_ffn_Wr, L1_ffn_br, L1_ffn_W1, L1_ffn_b1, L1_ffn_W2, L1_ffn_b2)[0]
    x = x + _L2_gnn_ref(_layernorm(x, axis=-1), edge_index, L2_gnn_W1, L2_gnn_att_src1, L2_gnn_att_dst1, L2_gnn_b1, L2_gnn_W2, L2_gnn_att_src2, L2_gnn_att_dst2, L2_gnn_b2, L2_gnn_fcW, L2_gnn_fcb)
    x = x + _L2_ffn_ref(_layernorm(x, axis=-1)[None], L2_ffn_gfc1_w, L2_ffn_gfc1_b, L2_ffn_gfc2_w, L2_ffn_gfc2_b, L2_ffn_W1, L2_ffn_b1, L2_ffn_W2, L2_ffn_b2, L2_ffn_ln_g, L2_ffn_ln_b, L2_ffn_tv_W1, L2_ffn_tv_b1, L2_ffn_tv_W2, L2_ffn_tv_b2, L2_ffn_tv_ln_g, L2_ffn_tv_ln_b)[0]
    x = x + _L3_gnn_ref(_layernorm(x, axis=-1), src, dst, deg, L3_gnn_W_self, L3_gnn_W_neigh, L3_gnn_bias, L3_gnn_gamma, L3_gnn_beta)
    x = x + _L3_ffn_ref(_layernorm(x, axis=-1)[None], L3_ffn_W_router, L3_ffn_b_router, L3_ffn_W_up, L3_ffn_b_up, L3_ffn_W_down, L3_ffn_b_down)[0]
    return x

_drawn_inputs = setup_inputs


def setup_inputs(seed=0):
    import zlib

    import numpy as np

    out = dict(_drawn_inputs(seed))
    spreads = {'L0_gnn_b': (0.0, 0.1),
     'L0_ffn_gate_b': (0.0, 0.293),
     'L0_ffn_b1': (0.0, 0.402),
     'L0_ffn_b2': (0.0, 0.1),
     'L1_gnn_bias': (0.0, 2.0),
     'L1_gnn_gamma': (1.0, 0.2),
     'L1_gnn_beta': (0.0, 0.1),
     'L1_ffn_br': (0.0, 0.1),
     'L1_ffn_b1': (0.0, 0.486),
     'L1_ffn_b2': (0.0, 0.1),
     'L2_gnn_b1': (0.0, 0.1),
     'L2_gnn_b2': (0.0, 0.1),
     'L2_gnn_fcb': (0.0, 0.1),
     'L2_ffn_gfc1_b': (0.0, 0.8),
     'L2_ffn_gfc2_b': (0.20000000298023224, 0.6),
     'L2_ffn_b1': (0.0, 0.793),
     'L2_ffn_b2': (0.0, 0.304),
     'L2_ffn_ln_g': (1.0, 0.2),
     'L2_ffn_ln_b': (0.0, 0.1),
     'L3_gnn_bias': (0.0, 0.1),
     'L3_gnn_gamma': (1.0, 0.2),
     'L3_gnn_beta': (0.0, 0.1),
     'L3_ffn_b_router': (0.0, 0.8),
     'L3_ffn_b_up': (0.0, 0.8),
     'L3_ffn_b_down': (0.0, 0.8)}
    factors = {'L2_gnn_att_dst1': 7.804,
     'L2_gnn_att_src2': 7.901,
     'L2_gnn_att_dst2': 27.34,
     'L2_ffn_gfc1_w': 8.0,
     'L2_ffn_gfc2_w': 8.0,
     'L2_ffn_tv_b1': 8.0,
     'L2_ffn_tv_b2': 8.0,
     'L2_ffn_tv_ln_g': 44.723,
     'L2_ffn_tv_ln_b': 58.755}
    for name, (base, spread) in spreads.items():
        noise = np.random.default_rng([zlib.crc32(name.encode()), seed]).standard_normal(out[name].shape)
        drawn = base * np.exp(spread * noise) if base else spread * noise
        out[name] = jnp.asarray(drawn.astype(out[name].dtype))
    for name, factor in factors.items():
        out[name] = (out[name] * factor).astype(out[name].dtype)
    return out
```

```python
from contextlib import ExitStack

import concourse.bass as bass
from concourse import mybir

F32 = mybir.dt.float32
BF16 = mybir.dt.bfloat16
F16 = mybir.dt.float16
I32 = mybir.dt.int32
U32 = mybir.dt.uint32
ALU = mybir.AluOpType
ACT = mybir.ActivationFunctionType
AX = mybir.AxisListType.X
ds = bass.ds

N, D, E = 1250, 512, 20000
TP, NT = 125, 10
KC = D // 128
EC = E // TP
BLK, CH = 512, 4
NB = (E + NT * (BLK - 1)) // BLK
NEG = -1.0e30
EPS = 1e-5
STAGES = 8


class Count:

    def __init__(self, nc, ctx, name, giver=None, credit=0):
        self.sem = ctx.enter_context(nc.semaphore(name))
        self.base, self.n, self.stack = credit, 0, []
        if credit:
            giver.sem_inc(self.sem, credit)

    def up(self, ins, k=1):
        ins.then_inc(self.sem, k)
        self.n += k
        return self.base + self.n

    def up_now(self, eng):
        eng.sem_inc(self.sem, 1)
        self.n += 1
        return self.base + self.n

    def now(self):
        return self.base + self.n

    def ago(self, m, turns=1):
        start, per = self.stack[-1]
        assert not isinstance(start, int) or start + m - turns * per > 0, (self.sem, "needs more credit")
        return self.base + (m - turns * per)

    def enter(self, i, per):
        self.stack.append((self.base + self.n, per))
        self.base, self.n = self.base + self.n + i * per, 0

    def leave(self, trips):
        start, per = self.stack.pop()
        assert self.n == per, (self.sem, "increments in a turn:", self.n, "declared:", per)
        self.base, self.n = start + trips * per, 0


class loop:

    def __init__(self, nc, trips, per):
        self.nc, self.trips, self.per = nc, trips, per

    def __enter__(self):
        self.f = self.nc.Fori(0, self.trips)
        i = self.f.__enter__()
        for c, k in self.per.items():
            c.enter(i, k)
        return i

    def __exit__(self, *a):
        r = self.f.__exit__(*a)
        if a[0] is None:
            for c in self.per:
                c.leave(self.trips)
        return r


def wait(eng, c, v):
    eng.wait_ge(c.sem, v)


def chain(eng, c, ins):
    wait(eng, c, c.up(ins))


def row(t, i):
    return t[:, ds(i, 1), :].rearrange("p a n -> p (a n)")


class Env:
    pass


def stage(nc, g):
    class S(ExitStack):
        def __exit__(self, *a):
            if a[0] is None:
                nc.all_engine_barrier()
                if self.counts:
                    nums = sorted(c.sem.num for c in self.counts)
                    first = [n for n in nums if n - 1 not in nums]
                    last = [n for n in nums if n + 1 not in nums]
                    for m, n in zip(first, last):
                        nc.gpsimd.sem_clear(range(m, n + 1))
                    nc.all_engine_barrier()
            return super().__exit__(*a)
    s = S()
    g.k += 1
    k = g.k
    s.sb = lambda name, shape, dt=F32: s.enter_context(nc.sbuf_tensor(f"{name}_{k}", shape, dt))
    s.counts = []

    def cnt(name, giver=None, credit=0):
        s.counts.append(Count(nc, s, f"{name}_{k}", giver, credit))
        return s.counts[-1]
    s.cnt = cnt
    s.dma_cnt = lambda name: Count(nc, g.ctx, f"{name}_{k}")
    return s


def bcast(ap, p):
    return ap.partition_broadcast(p)


def constants(nc, g, ctx, x):
    def sb(name, shape, dt=F32):
        return ctx.enter_context(nc.sbuf_tensor(name, shape, dt))
    g.X = sb("x_res", [TP, NT, D])
    g.ident = sb("ident", [128, 128])
    g.iota = sb("iota_nodes", [128, N], F16)
    g.iota_tp = sb("iota_tp", [128, TP])
    g.pcol = sb("partition_number", [128, 1])
    g.ones = sb("ones", [128, 128])
    g.zeros = sb("zeros_bf", [1, 512], BF16)
    g.deg = sb("degree", [TP, NT])
    g.PS = ctx.enter_context(nc.psum_tensor("psum", [128, 8, 512], F32))
    g.rec = sb("records", [128, NB * CH, 8])
    with stage(nc, g) as s:
        cp, cd = s.cnt("c_pool"), s.cnt("c_dma")
        cd.up(nc.sync.dma_start(g.X[:], x.rearrange("(t p) d -> p t d", p=TP)), 16)
        chain(nc.gpsimd, cp, nc.gpsimd.memset(g.ident[:], 0.0))
        cp.up(nc.gpsimd.affine_select(out=g.ident[:], in_=g.ident[:], compare_op=ALU.not_equal, fill=1.0,
                                      base=0, pattern=[[-1, 128]], channel_multiplier=1))
        cp.up(nc.gpsimd.iota(g.iota[:], [[1, N]], base=0, channel_multiplier=0,
                             allow_small_or_imprecise_dtypes=True))
        cp.up(nc.gpsimd.iota(g.iota_tp[:], [[1, TP]], base=0, channel_multiplier=0,
                             allow_small_or_imprecise_dtypes=True))
        cp.up(nc.gpsimd.iota(g.pcol[:], [[1, 1]], base=0, channel_multiplier=1,
                             allow_small_or_imprecise_dtypes=True))
        cp.up(nc.gpsimd.memset(g.ones[:], 1.0))
        cp.up(nc.gpsimd.memset(g.zeros[:], 0.0))
        wait(nc.gpsimd, cp, cp.now())
        wait(nc.sync, cd, cd.now())


def group_edges(nc, g, src, dst, edge_attr, W_edge, att_edge):
    dve, pe, pool, sp, act = nc.vector, nc.tensor, nc.gpsimd, nc.sync, nc.scalar
    with stage(nc, g) as s:
        v, d, p, q = s.cnt("v"), s.cnt("d"), s.cnt("p"), s.cnt("q")
        srci, dsti = s.sb("srci", [TP, EC], I32), s.sb("dsti", [TP, EC], I32)
        ea = s.sb("ea", [TP, EC, 4])
        we = s.sb("we", [TP, 4, D])
        att = s.sb("att", [TP, D])
        E8 = s.sb("edge_records", [TP, EC, 8])
        dstf = s.sb("dstf", [TP, EC])
        ge = s.sb("ge", [TP, NT + 1, EC])
        oh = s.sb("oh", [TP, NT, EC])
        cum = s.sb("cum", [TP, NT, EC])
        zero = s.sb("zero", [TP, NT, EC])
        tri = s.sb("tri", [TP, TP])
        cnt = s.sb("cnt", [TP, NT])
        tot = s.sb("tot", [TP, NT])
        toti = s.sb("toti", [TP, NT], I32)
        nblk = s.sb("nblk", [TP, NT])
        cblk = s.sb("cblk", [TP, NT])
        off = s.sb("off", [TP, NT])
        pos = s.sb("pos", [TP, EC])
        posi = s.sb("posi", [TP, EC], I32)
        V = s.sb("V", [TP, 16])
        vt = s.sb("vt", [TP, 4, D])
        am = s.sb("am", [TP, 4])
        pad = s.sb("pad", [128, NB * CH, 8])
        blkf = s.sb("blkf", [TP, NB])
        blkb = s.sb("blkb", [TP, NB])
        d.up(sp.dma_start(dsti[:], dst.rearrange("(p c) -> p c", c=EC)), 16)
        d.up(sp.dma_start(srci[:], src.rearrange("(p c) -> p c", c=EC)), 16)
        d.up(sp.dma_start(ea[:], edge_attr.rearrange("(p c) k -> p c k", c=EC)), 16)
        d.up(sp.dma_start(we[:], bcast(W_edge, TP)), 16)
        d.up(sp.dma_start(att[:], bcast(att_edge.rearrange("h c -> (h c)"), TP)), 16)
        chain(pool, p, pool.memset(tri[:], 1.0))
        p.up(pool.affine_select(out=tri[:], in_=tri[:], compare_op=ALU.is_gt, fill=0.0, base=0,
                                pattern=[[1, TP]], channel_multiplier=-1))
        chain(pool, p, pool.memset(pad[:], 0.0))
        p.up(pool.memset(pad[:, :, 1:2], -1.0))
        p.up(pool.iota(blkf[:], [[1, NB]], base=0, channel_multiplier=0, allow_small_or_imprecise_dtypes=True))
        wait(sp, p, p.now())
        pd = s.cnt("pads")
        pd.up(sp.dma_start(g.recd.rearrange("(c p) k -> p c k", p=128), pad[:]), 16)
        wait(dve, d, d.now())
        wait(dve, p, p.now())
        v.up(dve.memset(zero[:], 0.0))
        chain(dve, v, dve.tensor_copy(dstf[:], dsti[:]))
        chain(dve, v, dve.memset(E8[:], 0.0))
        v.up(dve.tensor_copy(E8[:, :, 0], srci[:]))
        for b in range(NT + 1):
            v.up(dve.tensor_scalar(ge[:, b, :], dstf[:], float(TP * b), None, ALU.is_ge))
        wait(dve, v, v.now())
        chain(dve, v, dve.tensor_tensor(oh[:], ge[:, 0:NT, :], ge[:, 1:NT + 1, :], ALU.subtract))
        chain(dve, v, dve.tensor_reduce(pos[:], ge[:, 1:NT, :].rearrange("p b c -> p c b"), AX, ALU.add))
        v.up(dve.scalar_tensor_tensor(E8[:, :, 1], pos[:], -float(TP), dstf[:], ALU.mult, ALU.add))
        flat = "p b c -> p (b c)"
        chain(dve, v, dve.tensor_tensor_scan(cum[:].rearrange(flat), oh[:].rearrange(flat), zero[:].rearrange(flat),
                                             0.0, ALU.add, ALU.add))
        v.up(dve.tensor_copy(cnt[:, 0:1], cum[:, 0, EC - 1:EC]))
        chain(dve, v, dve.tensor_tensor(cnt[:, 1:NT], cum[:, 1:NT, EC - 1], cum[:, 0:NT - 1, EC - 1], ALU.subtract))
        wait(pe, v, v.now())
        wait(pe, p, p.now())
        q.up(pe.matmul(g.PS[0:TP, 0, 0:NT], tri[:], cnt[:], start=True, stop=True))
        q.up(pe.matmul(g.PS[0:TP, 1, 0:NT], g.ones[0:TP, 0:TP], cnt[:], start=True, stop=True))
        wait(dve, q, q.now())
        chain(dve, v, dve.tensor_scalar(tot[:], g.PS[0:TP, 1, 0:NT], float(BLK - 1), None, ALU.add))
        chain(dve, v, dve.tensor_copy(toti[:], tot[:]))
        chain(dve, v, dve.tensor_single_scalar(toti[:], toti[:], 9, ALU.logical_shift_right))
        chain(dve, v, dve.tensor_copy(nblk[:], toti[:]))
        chain(dve, v, dve.tensor_tensor_scan(cblk[:], nblk[:], zero[:, 0, 0:NT], 0.0, ALU.add, ALU.add))
        chain(dve, v, dve.tensor_tensor(off[:], cblk[:], nblk[:], ALU.subtract))
        chain(dve, v, dve.scalar_tensor_tensor(off[:], off[:], float(BLK), g.PS[0:TP, 0, 0:NT], ALU.mult, ALU.add))
        chain(dve, v, dve.tensor_scalar(off[:], off[:], -1.0, None, ALU.add))
        chain(dve, v, dve.tensor_tensor(off[:, 1:NT], off[:, 1:NT], cum[:, 0:NT - 1, EC - 1], ALU.subtract))
        chain(dve, v, dve.tensor_tensor(cum[:], cum[:], off[:, :, None].to_broadcast([TP, NT, EC]), ALU.add))
        chain(dve, v, dve.tensor_tensor(cum[:], cum[:], oh[:], ALU.mult))
        chain(dve, v, dve.tensor_reduce(pos[:], cum[:].rearrange("p b c -> p c b"), AX, ALU.add))
        chain(dve, v, dve.tensor_copy(posi[:], pos[:]))
        chain(dve, v, dve.memset(blkb[:], 0.0))
        for b in range(NT - 1):
            chain(dve, v, dve.scalar_tensor_tensor(blkb[:], blkf[:], cblk[:, b:b + 1], blkb[:], ALU.is_ge, ALU.add))
        v.up(dve.memset(g.blk_tile[:, 0:1], 0))
        chain(dve, v, dve.tensor_copy(g.blk_tile[:, 1:NB + 1], blkb[0:1, :]))
        chain(dve, v, dve.tensor_tensor(vt[:], we[:], att[:, None, :].to_broadcast([TP, 4, D]), ALU.mult))
        chain(dve, v, dve.tensor_reduce(V[:], vt[:].rearrange("p k (h c) -> p (k h) c", h=4), AX, ALU.add))
        for h in range(4):
            chain(dve, v, dve.tensor_scalar(E8[:, :, 2 + h], ea[:, :, 0], V[:, h:h + 1], None, ALU.mult))
            for k in range(1, 4):
                chain(dve, v, dve.scalar_tensor_tensor(E8[:, :, 2 + h], ea[:, :, k], V[:, 4 * k + h:4 * k + h + 1],
                                                       E8[:, :, 2 + h], ALU.mult, ALU.add))
        chain(dve, v, dve.tensor_reduce(am[:], E8[:, :, 2:6].rearrange("p c h -> p h c"), AX, ALU.add))
        wait(pe, v, v.now())
        q.up(pe.matmul(g.PS[0:TP, 2, 0:4], g.ones[0:TP, 0:TP], am[:], start=True, stop=True))
        wait(dve, q, q.now())
        chain(dve, v, dve.tensor_scalar(g.ae_mean[:], g.PS[0:TP, 2, 0:4], 1.0 / E, None, ALU.mult))
        GC = 16
        sc, f, go = s.dma_cnt("scattered"), s.cnt("copied", dve, 2), s.cnt("go", dve, 4)
        idx = [s.sb(f"idx{u}", [TP, GC], I32) for u in range(2)]
        rec = [s.sb(f"rec{u}", [TP, GC, 8]) for u in range(2)]
        wait(pool, pd, pd.now())
        with loop(nc, EC // GC // 2, {sc: 32 * GC, f: 4, go: 4}) as i:
            for u in range(2):
                wait(dve, go, go.ago(2 * u + 2))
                f.up(dve.tensor_copy(idx[u][:], posi[:, ds(i * 2 * GC + u * GC, GC)]))
                f.up(dve.tensor_copy(rec[u][:], E8[:, ds(i * 2 * GC + u * GC, GC), :]))
                wait(pool, f, f.now())
                go.up_now(pool)
                for c in range(GC):
                    ins = pool.indirect_dma_start(out=g.recd, out_offset=bass.IndirectOffsetOnAxis(
                        ap=idx[u][:, c:c + 1], axis=0), in_=rec[u][:, c, :], in_offset=None)
                    sc.up(ins, 16)
                wait(pool, sc, sc.now())
                go.up_now(pool)
        wait(sp, pd, pd.now())
        wait(sp, sc, sc.now())
        d.up(sp.dma_start(g.rec[:], g.recd.rearrange("(c p) k -> p c k", p=128)), 16)
        wait(dve, d, d.now())
        v.up(dve.memset(g.srcidx[:, NB * CH:], 0))
        chain(dve, v, dve.tensor_copy(g.srcidx[:, 0:NB * CH], g.rec[:, :, 0]))


def count_matrix(nc, g):
    dve, pe, pool, sp, act = nc.vector, nc.tensor, nc.gpsimd, nc.sync, nc.scalar
    with stage(nc, g) as s:
        C = s.sb("C", [TP, NT, N])
        Dh = [s.sb(f"Dh{u}", [128, CH, TP], BF16) for u in range(2)]
        Sh = [s.sb(f"Sh{u}", [128, CH, N], BF16) for u in range(2)]
        iob = g.iota_tp[:, None, :].to_broadcast([128, CH, TP])
        v = s.cnt("v", dve, 1)
        one, mm, add = s.cnt("onehots"), s.cnt("products"), s.cnt("added", dve, 2)
        kv = s.cnt("dve_steps")
        chain(dve, v, dve.memset(C[:], 0.0))

        def onehots(j, u):
            kv.up(dve.tensor_tensor(Dh[u][:], iob, g.rec[:, ds(j * CH, CH), 1:2].to_broadcast([128, CH, TP]),
                                    ALU.is_equal))
            for c in range(CH):
                ins = dve.tensor_scalar(Sh[u][:, c, :], g.iota[:],
                                        g.rec[:, ds(j * CH + c, 1), 0:1].rearrange("p a k -> p (a k)"),
                                        None, ALU.is_equal)
                (one if c == CH - 1 else kv).up(ins)

        def products(j, u):
            wait(pe, one, j + 1)
            wait(pe, kv, kv.now())
            wait(pe, add, j + 1)
            for c in range(CH):
                for w, (a, b) in enumerate(((0, 512), (512, 1024), (1024, N))):
                    ins = pe.matmul(g.PS[0:TP, 3 * u + w, 0:b - a], Dh[u][:, c, :], Sh[u][:, c, a:b],
                                    start=(c == 0), stop=(c == CH - 1))
            mm.up(ins)

        def add_block(j, u):
            b = dve.value_load(g.blk_tile[0:1, ds(j + 1, 1)], min_val=0, max_val=NT - 1)
            wait(dve, mm, j + 1)
            wait(dve, add, j + 2)
            ps = g.PS[0:TP, 3 * u:3 * u + 3, :].rearrange("p w n -> p (w n)")[:, 0:N]
            add.up(dve.tensor_tensor(row(C, b), ps, row(C, b), ALU.add))

        onehots(0, 0)
        assert NB % 2 == 1
        with loop(nc, NB // 2, {one: 2, mm: 2, add: 2, kv: 2 * CH}) as i:
            for u in range(2):
                j = i * 2 + u
                products(j, u)
                onehots(j + 1, 1 - u)
                add_block(j, u)
        products(NB - 1, 0)
        add_block(NB - 1, 0)
        wait(dve, add, add.now())
        chain(dve, v, dve.tensor_reduce(g.deg[:], C[:], AX, ALU.add))

        for t in range(NT):
            v.up(dve.tensor_tensor(C[:, t, t * TP:(t + 1) * TP], C[:, t, t * TP:(t + 1) * TP],
                                   g.ident[0:TP, 0:TP], ALU.add))
        zr, dz = s.sb("zr", [128 - TP, NT, N]), s.cnt("dz")
        chain(dve, v, dve.memset(zr[:], 0.0))
        wait(sp, v, v.now())
        wait(act, v, v.now())
        dz.up(sp.dma_start(g.CT.rearrange("(k s) d -> s k d", s=128)[TP:128], zr[:]), 16)
        cin = [s.sb(f"cin{u}", [TP, N]) for u in range(2)]
        ct = [s.sb(f"ct{u}", [TP, NT, TP]) for u in range(2)]
        mask = [s.sb(f"mask{u}", [TP, N], BF16) for u in range(2)]
        ci, t, cc, mk = s.cnt("cin_copied", dve, 2), s.cnt("transposed", dve, 2), s.cnt("ct_copied", dve, 2), s.cnt("masks", dve, 2)
        st = [s.cnt(f"stored{u}", sp, 16) for u in range(2)]
        sm = [s.cnt(f"mask_stored{u}", sp, 16) for u in range(2)]
        go = s.cnt("ct_stores_begun")
        with loop(nc, NT // 2, {go: 2, ci: 2, t: 2, cc: 2, mk: 2, st[0]: 16, st[1]: 16, sm[0]: 16, sm[1]: 16}) as i:
            for u in range(2):
                n = i * 2 + u
                wait(act, t, t.ago(u + 1))
                wait(act, mk, mk.ago(u + 1))
                ci.up(act.activation(cin[u][:], row(C, n), ACT.Copy))
                wait(pe, ci, ci.now())
                wait(pe, cc, cc.ago(u + 1))
                for k in range(NT):
                    ins = pe.transpose(g.PS[0:TP, 3 * u + k // 4, (k % 4) * 128:(k % 4) * 128 + TP],
                                       cin[u][:, k * TP:(k + 1) * TP], g.ident[0:TP, 0:TP])
                t.up(ins)
                wait(dve, ci, ci.now())
                wait(dve, sm[u], sm[u].ago(16))
                mk.up(dve.tensor_scalar(mask[u][:], cin[u][:], 0.0, NEG, ALU.is_equal, ALU.mult))
                wait(sp, mk, mk.now())
                sm[u].up(sp.dma_start(g.MASK[ds(n * TP, TP), :], mask[u][:]), 16)
                wait(dve, t, t.now())
                wait(dve, st[u], st[u].ago(16))
                for k in range(3):
                    m = min(4, NT - 4 * k)
                    ins = dve.tensor_copy(ct[u][:, 4 * k:4 * k + m, :],
                                          g.PS[0:TP, 3 * u + k, 0:m * 128].rearrange("p (a b) -> p a b", b=128)[:, :, 0:TP])
                cc.up(ins)
                wait(sp, cc, cc.now())
                go.up_now(sp)
                st[u].up(sp.dma_start(g.CT.rearrange("(k s) d -> s k d", s=128)[0:TP, :, ds(n * TP, TP)], ct[u][:]), 16)
        for c in (*st, *sm, dz):
            wait(sp, c, c.now())


def norm_tiles(nc, g, s, consume, per, XT=None, XN=None, dram=None):
    dve, pe, act, sp = nc.vector, nc.tensor, nc.scalar, nc.sync
    st = s.sb("ln_st", [TP, NT, 6])
    mv = s.sb("ln_mv", [TP, NT, 2])
    rs = s.sb("ln_rs", [TP, NT])
    xn = [s.sb(f"ln_xn{u}", [TP, D]) for u in range(2)]
    xT = [s.sb(f"ln_xT{u}", [128, KC, TP]) for u in range(2)]
    v = s.cnt("ln_v", dve, 1)
    for t in range(NT):
        v.up(dve.bn_stats(st[:, t, :], g.X[:, t, :]))
    wait(dve, v, v.now())
    for t in range(NT):
        v.up(dve.bn_aggr(mv[:, t, :], st[:, t, :]))
    wait(dve, v, v.now())
    chain(dve, v, dve.tensor_scalar(rs[:], mv[:, :, 1], EPS, None, ALU.add))
    wait(act, v, v.now())
    a = s.cnt("ln_a", dve, 2)
    a.up(act.activation(rs[:], rs[:], ACT.Sqrt))
    wait(dve, a, a.now())
    chain(dve, v, dve.reciprocal(rs[:], rs[:]))
    t, w = s.cnt("ln_t", dve, 2), [s.cnt(f"ln_w{u}", sp, 16) for u in range(2)]
    used = s.cnt("ln_used", dve, 2)
    keep = {v: 2, a: 2, t: 2, used: 2, **per}
    if dram is not None:
        keep.update({w[0]: 16, w[1]: 16})
    with loop(nc, NT // 2, keep) as i:
        for u in range(2):
            k = i * 2 + u
            wait(dve, t, t.ago(u + 1))
            if dram is not None:
                wait(dve, w[u], w[u].ago(16))
            if XN is not None:
                wait(dve, a, a.ago(u + 1))
            v.up(dve.tensor_scalar(xn[u][:], row(g.X, k), mv[:, ds(k, 1), 0:1].rearrange("p a b -> p (a b)"),
                                   rs[:, ds(k, 1)], ALU.subtract, ALU.mult))
            if dram is not None:
                wait(sp, v, v.now())
                w[u].up(sp.dma_start(dram[ds(k * TP, TP), :], xn[u][:]), 16)
            wait(pe, v, v.now())
            wait(pe, a, a.ago(u + 1))
            for c in range(KC):
                ins = pe.transpose(g.PS[:, u, c * 128:c * 128 + TP], xn[u][:, c * 128:(c + 1) * 128],
                                   g.ident[0:TP, 0:TP])
            t.up(ins)
            wait(act, t, t.now())
            wait(act, used, used.ago(u + 1))
            pt = g.PS[:, u, :].rearrange("p (c n) -> p c n", n=128)[:, :, 0:TP]
            if XN is not None:
                wait(act, v, v.now())
            ins = act.activation(xT[u][:], pt, ACT.Copy)
            if XT is not None:
                ins = act.activation(XT[:, :, ds(k * TP, TP)], pt, ACT.Copy)
            if XN is not None:
                ins = act.activation(row(XN, k), xn[u][:], ACT.Copy)
            a.up(ins)
            wait(pe, a, a.now())
            consume(k, u, xT[u], used)
    if dram is not None:
        for c in w:
            wait(sp, c, c.now())
            wait(nc.gpsimd, c, c.now())


def aggregate(nc, g, s, CT, H, finish):
    dve, pe, sp = nc.vector, nc.tensor, nc.sync
    ct = [s.sb(f"ag_ct{u}", [128, N]) for u in range(2)]
    ld = [s.cnt(f"ag_ld{u}") for u in range(2)]
    rd = s.cnt("ag_rd", dve, 2)
    out = s.cnt("ag_out", dve, 1)
    for half in range(2):
        wait(pe, out, out.now())
        for b in range(5):
            pe.matmul(g.PS[0:TP, b, :], g.zeros[0:1, 0:TP], g.zeros[0:1, :], start=True, stop=True)
        with loop(nc, NT // 2, {ld[0]: 16, ld[1]: 16, rd: 2}) as i:
            for u in range(2):
                k = i * 2 + u
                wait(sp, rd, rd.ago(u + 1))
                ld[u].up(sp.dma_start(ct[u][:], CT[ds(k * 128, 128), :]), 16)
                wait(pe, ld[u], ld[u].now())
                for t in range(NT):
                    ins = pe.matmul(g.PS[0:TP, t // 2, (t % 2) * 256:(t % 2) * 256 + 256],
                                    ct[u][0:TP, t * TP:(t + 1) * TP],
                                    H[:, ds(k, 1), half * 256:half * 256 + 256].rearrange("p a n -> p (a n)"),
                                    start=False, stop=True, skip_group_check=True)
                rd.up(ins)
        wait(dve, rd, rd.now())
        out.up(finish(half, g.PS[0:TP, 0:5, :].rearrange("p b (a n) -> p (b a) n", n=256)))
    return out


def gnn0(nc, g, W, b):
    dve, pe, act, sp = nc.vector, nc.tensor, nc.scalar, nc.sync
    with stage(nc, g) as s:
        Wt = s.sb("W", [128, KC, D])
        bb = s.sb("b", [TP, D])
        H = s.sb("H", [TP, NT, D])
        di = s.sb("dinv", [TP, NT])
        y = s.sb("y", [TP, NT, 256])
        d, v, a = s.cnt("d"), s.cnt("v"), s.cnt("a")
        d.up(sp.dma_start(Wt[:], W.rearrange("(c p) n -> p c n", p=128)), 16)
        d.up(sp.dma_start(bb[:], bcast(b, TP)), 16)
        chain(dve, v, dve.tensor_scalar(di[:], g.deg[:], 1.0, None, ALU.add))
        wait(act, v, v.now())
        a.up(act.activation(di[:], di[:], ACT.Sqrt))
        wait(dve, a, a.now())
        chain(dve, v, dve.reciprocal(di[:], di[:]))
        ev = s.cnt("ev", dve, 2)
        wait(pe, d, d.now())

        def consume(k, u, xT, used):
            wait(pe, ev, ev.ago(u + 1))
            for c in range(KC):
                ins = pe.matmul(g.PS[0:TP, 2 + u, :], xT[:, c, :], Wt[:, c, :], start=(c == 0), stop=(c == KC - 1))
            wait(dve, used, used.up(ins))
            ev.up(dve.tensor_scalar(row(H, k), g.PS[0:TP, 2 + u, :], di[:, ds(k, 1)], None, ALU.mult))

        norm_tiles(nc, g, s, consume, {ev: 2})
        wait(pe, ev, ev.now())
        wait(dve, d, d.now())
        dib = di[:, :, None].to_broadcast([TP, NT, 256])

        def finish(half, ps):
            c = slice(half * 256, half * 256 + 256)
            chain(dve, v, dve.tensor_tensor(y[:], ps, dib, ALU.mult))
            last = v.now()
            chain(dve, v, dve.tensor_tensor(y[:], y[:], bb[:, None, c].to_broadcast([TP, NT, 256]), ALU.add))
            return dve.scalar_tensor_tensor(g.X[:, :, c], y[:], 0.0, g.X[:, :, c], ALU.max, ALU.add)

        aggregate(nc, g, s, g.CT, H, finish)


def to_experts(nc, g, s, T, WT, ne, v, q):
    wait(nc.tensor, v, v.now())
    for t in range(NT):
        ins = nc.tensor.transpose(g.PS[0:ne, t // 4, (t % 4) * TP:(t % 4 + 1) * TP], T[:, t, :],
                                  g.ident[0:TP, 0:TP])
    wait(nc.vector, q, q.up(ins))
    for k in range(3):
        n = min(4, NT - 4 * k) * TP
        v.up(nc.vector.tensor_copy(WT[:, 4 * k * TP:4 * k * TP + n], g.PS[0:ne, k, 0:n]))
    wait(nc.vector, v, v.now())


def top_slots(nc, g, s, WT, ne, slots, keep, v, q, ahead=1):
    dve, pe = nc.vector, nc.tensor
    parts = -(-slots // 128)
    part = slots // parts
    mx = s.sb("top_value", [ne, 8])
    ix = s.sb("top_index", [ne, 8], U32)
    turn = s.sb("turn", [ne, 1])
    val = s.sb("slot_value", [ne, slots])
    idf = s.sb("slot_token", [ne, slots])
    chain(dve, v, dve.max(mx[:], WT[:]))
    with loop(nc, slots // 8, {v: 6}) as i:
        wait(dve, v, v.now())
        v.up(dve.tensor_copy(val[:, ds(i * 8, 8)], mx[:]))
        v.up(dve.max_index(ix[:], mx[:], WT[:]))
        wait(dve, v, v.now())
        v.up(dve.tensor_copy(idf[:, ds(i * 8, 8)], ix[:]))
        v.up(dve.match_replace(WT[:], mx[:], WT[:], -2.0))
        wait(dve, v, v.now())
        v.up(dve.tensor_copy(turn[:], g.ident[0:ne, 0:1]))
        v.up(dve.max(mx[:], WT[:]))
    chain(dve, v, dve.tensor_scalar(val[:], val[:], 0.0, None, ALU.max))
    if keep < slots:
        chain(dve, v, dve.memset(val[:, keep:slots], 0.0))
    sw = s.sb("slot_w", [part, parts, ne])
    si = s.sb("slot_i", [part, parts, ne + ahead], I32)
    wait(pe, v, v.now())
    for k in range(parts):
        pe.transpose(g.PS[0:part, 0, k * 128:k * 128 + ne], val[:, k * part:(k + 1) * part], g.ident[0:ne, 0:ne])
        ins = pe.transpose(g.PS[0:part, 1, k * 128:k * 128 + ne], idf[:, k * part:(k + 1) * part],
                           g.ident[0:ne, 0:ne])
    wait(dve, q, q.up(ins))
    chain(dve, v, dve.memset(si[:], 0))
    for k in range(parts):
        v.up(dve.tensor_copy(sw[:, k, :], g.PS[0:part, 0, k * 128:k * 128 + ne]))
        v.up(dve.tensor_copy(si[:, k, 0:ne], g.PS[0:part, 1, k * 128:k * 128 + ne]))
    wait(dve, v, v.now())
    return sw, si


def softmax_rows(nc, s, L, ne, v, a):
    dve, act = nc.vector, nc.scalar
    m = s.sb("sm_m", [TP, NT])
    chain(dve, v, dve.tensor_reduce(m[:], L[:], AX, ALU.max))
    chain(dve, v, dve.tensor_tensor(L[:], L[:], m[:, :, None].to_broadcast([TP, NT, ne]), ALU.subtract))
    wait(act, v, v.now())
    a.up(act.activation(L[:], L[:], ACT.Exp))
    wait(dve, a, a.now())
    chain(dve, v, dve.tensor_reduce(m[:], L[:], AX, ALU.add))
    chain(dve, v, dve.reciprocal(m[:], m[:]))
    chain(dve, v, dve.tensor_tensor(L[:], L[:], m[:, :, None].to_broadcast([TP, NT, ne]), ALU.mult))


def logits(nc, g, s, W_ap, b_ap, ne, XT=None, XN=None, dram=None):
    dve, pe, sp = nc.vector, nc.tensor, nc.sync
    Wt, bb, L = s.sb("router_w", [128, KC, ne]), s.sb("router_b", [TP, ne]), s.sb("logits", [TP, NT, ne])
    d = s.cnt("router_d")
    d.up(sp.dma_start(Wt[:], W_ap), 16)
    d.up(sp.dma_start(bb[:], bcast(b_ap, TP)), 16)
    wait(pe, d, d.now())
    wait(dve, d, d.now())
    ev = s.cnt("router_ev", dve, 2)

    def consume(k, u, xT, used):
        wait(pe, ev, ev.ago(u + 1))
        for c in range(KC):
            ins = pe.matmul(g.PS[0:TP, 2 + u, 0:ne], xT[:, c, :], Wt[:, c, :], start=(c == 0), stop=(c == KC - 1))
        wait(dve, used, used.up(ins))
        ev.up(dve.tensor_tensor(row(L, k), g.PS[0:TP, 2 + u, 0:ne], bb[:], ALU.add))

    norm_tiles(nc, g, s, consume, {ev: 2}, XT=XT, XN=XN, dram=dram)
    wait(dve, ev, ev.now())
    return L


def ffn0(nc, g, gate_w, gate_b, w1, b1, w2, b2):
    dve, pe, act, sp, pool = nc.vector, nc.tensor, nc.scalar, nc.sync, nc.gpsimd
    NE, HID = w1.shape[0], w1.shape[2]
    CAP = int(1.2 * N / NE)
    SL = -(-CAP // 16) * 16
    HS, Q = SL // 2, HID // 512
    with stage(nc, g) as s:
        v, a, q, d = s.cnt("v"), s.cnt("a"), s.cnt("q"), s.cnt("d")
        W1 = [s.sb(f"w1_{k}", [128, KC, 512]) for k in range(Q)]
        W2 = [s.sb(f"w2_{k}", [128, 4, 512]) for k in range(Q)]
        b2b = s.sb("b2b", [HS, NE, D])
        b1r, b1T = s.sb("b1r", [128, 128]), s.sb("b1T", [128, NE, HID // 128])
        d.up(sp.dma_start(g.Y.rearrange("(t p) d -> p t d", p=TP), g.X[:]), 16)
        d.up(sp.dma_start(b1r[:], b1.rearrange("e (m p) -> (e m) p", p=128)), 16)
        d.up(sp.dma_start(b2b[:], bcast(b2, HS)), 16)
        L = logits(nc, g, s, gate_w.rearrange("(c p) e -> p c e", p=128), gate_b, NE, dram=g.XND)
        wait(pe, d, d.now())
        q.up(pe.transpose(g.PS[:, 7, 0:128], b1r[:], g.ident[:]))
        wait(dve, q, q.now())
        v.up(dve.tensor_copy(b1T[:].rearrange("p e m -> p (e m)"), g.PS[:, 7, 0:128]))
        softmax_rows(nc, s, L, NE, v, a)
        rank = ranks(nc, s, L, NE, v)
        chain(dve, v, dve.tensor_scalar(rank[:], rank[:], 2.0, None, ALU.is_lt))
        chain(dve, v, dve.tensor_tensor(L[:], L[:], rank[:], ALU.mult))
        chain(dve, v, dve.tensor_scalar(rank[:], rank[:], -1.0, None, ALU.add))
        chain(dve, v, dve.tensor_tensor(L[:], L[:], rank[:], ALU.add))
        WT = s.sb("WT", [NE, N])
        to_experts(nc, g, s, L, WT, NE, v, q)
        sw, si = top_slots(nc, g, s, WT, NE, SL, CAP, v, q)

        xg = [s.sb(f"xg{u}", [HS, 2, D]) for u in range(2)]
        xgT = [s.sb(f"xgT{u}", [128, KC, SL]) for u in range(2)]
        hT = [s.sb(f"hT{k}", [128, 4, SL]) for k in range(2)]
        wo = [s.sb(f"wo{u}", [HS, 2, D]) for u in range(2)]
        gi = [s.sb(f"gi{u}", [HS, 2], I32) for u in range(2)]
        ci = s.sb("ci", [HS, 2], I32)
        ld1 = [s.cnt(f"ld1_{k}") for k in range(Q)]
        ld2 = [s.cnt(f"ld2_{k}") for k in range(Q)]
        mm1, mm2 = s.cnt("mm1", dve, 8 * Q), s.cnt("mm2", dve, 2 * Q)
        gs = [s.dma_cnt(f"gathered{u}") for u in range(2)]
        po = s.cnt("pool_steps", dve, 1)
        tr, tc = s.cnt("transposed", dve, 2), s.cnt("transposed_copied", dve, 2)
        ge = s.cnt("gelu", dve, 8 * Q)
        ev = s.cnt("weighted", dve, 8)
        sc, sd = s.dma_cnt("scattered"), s.cnt("scatter_over", dve, 4)

        def gather(e, u):
            wait(pool, tr, gather_free(u))
            po.up(pool.tensor_copy(gi[u][:], si[:, :, ds(e, 1)].rearrange("p k e -> p (k e)")))
            wait(pool, po, po.now())
            po.up_now(pool)
            for k in range(2):
                gs[u].up(pool.indirect_dma_start(out=xg[u][:, k, :], out_offset=None, in_=g.XND,
                                                 in_offset=bass.IndirectOffsetOnAxis(ap=gi[u][:, k:k + 1], axis=0)), 16)
        wait(pool, v, v.now())
        gather_free = lambda u: 1
        gather(0, 0)
        per = {mm1: 8 * Q, mm2: 2 * Q, gs[0]: 32, gs[1]: 32, po: 6, tr: 2, tc: 2, ge: 8 * Q, ev: 8, sc: 64, sd: 4}
        per.update({c: 32 for c in ld1 + ld2})
        gather_free = lambda u: tr.now() if u == 0 else tr.ago(2)
        with loop(nc, NE // 2, per) as i:
            for u in range(2):
                e = i * 2 + u
                for k in range(Q):
                    wait(sp, mm1, mm1.ago(4 * Q + 4 * k + 4) if u == 0 else mm1.base + 4 * (k + 1))
                    ld1[k].up(sp.dma_start(W1[k][:], w1[ds(e, 1), :, k * 512:(k + 1) * 512].rearrange(
                        "a (c p) n -> p (a c) n", p=128)), 16)
                    wait(sp, mm2, mm2.ago(Q + k + 1) if u == 0 else mm2.base + k + 1)
                    ld2[k].up(sp.dma_start(W2[k][:], w2[ds(e, 1), k * 512:(k + 1) * 512, :].rearrange(
                        "a (m p) n -> p (a m) n", p=128)), 16)
                wait(pe, gs[u], gs[u].now())
                wait(pe, ge, ge.now())
                for c in range(KC):
                    for k in range(2):
                        ins = pe.transpose(g.PS[:, c // 2, (c % 2) * SL + k * HS:(c % 2) * SL + (k + 1) * HS],
                                           xg[u][:, k, c * 128:(c + 1) * 128], g.ident[0:HS, 0:HS])
                tr.up(ins)
                wait(dve, tr, tr.now())
                wait(dve, mm1, mm1.ago(4 * Q * (u + 1)))
                tc.up(dve.tensor_copy(xgT[u][:].rearrange("p (b c) n -> p b (c n)", b=2), g.PS[:, 0:2, 0:2 * SL]))

                def up_proj(k):
                    wait(pe, ld1[k], ld1[k].now())
                    for m in range(4):
                        if k == 0:
                            wait(pe, tc, tc.now())
                        else:
                            wait(pe, ge, ge.now() - 3 + m)
                        for c in range(KC):
                            ins = pe.matmul(g.PS[:, m, 0:SL], W1[k][:, c, m * 128:(m + 1) * 128], xgT[u][:, c, :],
                                            start=(c == 0), stop=(c == KC - 1))
                        mm1.up(ins)

                def gelu(k):
                    wait(act, mm2, mm2_before[k])
                    for m in range(4):
                        wait(act, mm1, mm1.now() - 3 + m)
                        ge.up(act.activation(hT[k % 2][:, m, :], g.PS[:, m, 0:SL], ACT.Gelu,
                                             bias=b1T[:, ds(e, 1), 4 * k + m:4 * k + m + 1].rearrange("p a b -> p (a b)")))

                def down_proj(k, upto):
                    wait(pe, ge, upto)
                    wait(pe, ld2[k], ld2[k].now())
                    for h in range(2):
                        for m in range(4):
                            ins = pe.matmul(g.PS[0:HS, 4 + 2 * u + h, :], hT[k % 2][:, m, h * HS:(h + 1) * HS],
                                            W2[k][:, m, :], start=(k == 0 and m == 0), stop=(k == Q - 1 and m == 3))
                    mm2.up(ins)

                m2 = mm2.base + u * Q
                mm2_before = [m2 + k - 1 for k in range(Q)]
                wait(pe, ev, ev.ago(4 * u + 4))
                done = []
                for k in range(Q):
                    up_proj(k)
                    gelu(k)
                    done.append(ge.now())
                    if k:
                        down_proj(k - 1, done[k - 1])
                down_proj(Q - 1, done[Q - 1])
                wait(dve, mm2, mm2.now())
                wait(dve, sd, sd.ago(2 * u + 2))
                for h in range(2):
                    chain(dve, ev, dve.tensor_tensor(wo[u][:, h, :], g.PS[0:HS, 4 + 2 * u + h, :],
                                                     row(b2b, e), ALU.add))
                    ev.up(dve.tensor_scalar(wo[u][:, h, :], wo[u][:, h, :], sw[:, h, ds(e, 1)], None, ALU.mult))
                gather(e + 1, 1 - u)
                po.up(pool.tensor_copy(ci[:], si[:, :, ds(e, 1)].rearrange("p k e -> p (k e)")))
                wait(pool, po, po.now())
                wait(pool, ev, ev.now())
                sd.up_now(pool)
                for h in range(2):
                    sc.up(pool.indirect_dma_start(out=g.Y, out_offset=bass.IndirectOffsetOnAxis(
                        ap=ci[:, h:h + 1], axis=0), in_=wo[u][:, h, :], in_offset=None, compute_op=ALU.add), 16)
                wait(pool, sc, sc.now())
                sd.up_now(pool)
        wait(sp, sc, sc.now())
        wait(sp, gs[0], gs[0].now())
        wait(sp, gs[1], gs[1].now())
        d.up(sp.dma_start(g.X[:], g.Y.rearrange("(t p) d -> p t d", p=TP)), 16)
        wait(sp, d, d.now())


def gnn1(nc, g, W, att_src, att_dst, bias, gamma, beta):
    dve, pe, act, sp, pool = nc.vector, nc.tensor, nc.scalar, nc.sync, nc.gpsimd
    NH, DH = 4, D // 4
    HW = NH * (DH + 1)
    with stage(nc, g) as s:
        v, a, q, d = s.cnt("v", dve, 1), s.cnt("a"), s.cnt("q"), s.cnt("d")
        ACC = s.sb("ACC", [TP, NT, HW])
        M, AD = s.sb("M", [TP, NT, NH]), s.sb("AD", [TP, NT, NH])
        Wt = s.sb("W", [128, KC, D])
        ats, atd = s.sb("ats", [TP, D]), s.sb("atd", [TP, D])
        tb = [s.sb(f"tb{u}", [TP, HW + NH]) for u in range(2)]
        tmp = s.sb("tmp", [TP, 2, D])
        d.up(sp.dma_start(Wt[:], W.rearrange("(c p) n -> p c n", p=128)), 16)
        d.up(sp.dma_start(ats[:], bcast(att_src.rearrange("h c -> (h c)"), TP)), 16)
        d.up(sp.dma_start(atd[:], bcast(att_dst.rearrange("h c -> (h c)"), TP)), 16)
        for u in range(2):
            v.up(dve.memset(tb[u][:], 1.0))
        wait(dve, v, v.now())
        wait(dve, d, d.now())
        wait(pe, d, d.now())
        ev = s.cnt("ev", dve, 14)
        tw = [s.cnt(f"table_w{u}", sp, 16) for u in range(2)]

        def consume(k, u, xT, used):
            wait(pe, ev, ev.ago(7 * u + 7))
            for c in range(KC):
                ins = pe.matmul(g.PS[0:TP, 2 + u, :], xT[:, c, :], Wt[:, c, :], start=(c == 0), stop=(c == KC - 1))
            wait(dve, used, used.up(ins))
            ph = g.PS[0:TP, 2 + u, :]
            head = tb[u][:, 0:HW].rearrange("p (h c) -> p h c", c=DH + 1)
            wait(dve, tw[u], tw[u].ago(16))
            ev.up(dve.tensor_copy(head[:, :, 0:DH], ph.rearrange("p (h c) -> p h c", c=DH)))
            ev.up(dve.tensor_tensor(tmp[:, 0, :], ph, ats[:], ALU.mult))
            chain(dve, ev, dve.tensor_tensor(tmp[:, 1, :], ph, atd[:], ALU.mult))
            sums = tmp[:].rearrange("p k (h c) -> p k h c", c=DH)
            ev.up(dve.tensor_reduce(tb[u][:, HW:HW + NH], sums[:, 0], AX, ALU.add))
            chain(dve, ev, dve.tensor_reduce(row(AD, k), sums[:, 1], AX, ALU.add))
            chain(dve, ev, dve.tensor_scalar(row(ACC, k), tb[u][:, 0:HW], 1.0, None, ALU.mult))
            chain(dve, ev, dve.tensor_tensor(row(M, k), row(AD, k), tb[u][:, HW:HW + NH], ALU.add))
            wait(sp, ev, ev.now())
            tw[u].up(sp.dma_start(g.HT[ds(k * TP, TP), :], tb[u][:]), 16)

        norm_tiles(nc, g, s, consume, {ev: 14, tw[0]: 16, tw[1]: 16})
        wait(dve, ev, ev.now())
        chain(dve, v, dve.tensor_tensor(M[:], M[:], g.ae_mean[:, None, :].to_broadcast([TP, NT, NH]), ALU.add))
        chain(dve, v, dve.scalar_tensor_tensor(M[:], M[:], 0.2, M[:], ALU.mult, ALU.max))
        for c in tw:
            wait(pool, c, c.now())
        sel = s.sb("sel", [CH * 5, CH * 5, TP])
        chain(dve, v, dve.tensor_copy(sel[:], g.ident[0:CH * 5, 0:CH * 5, None].to_broadcast([CH * 5, CH * 5, TP])))
        RING = 3
        gi = [s.sb(f"gi{u}", [128, CH], I32) for u in range(RING)]
        hg = [s.sb(f"hg{u}", [128, CH, HW + NH]) for u in range(RING)]
        Dh = [s.sb(f"Dh{u}", [128, CH, TP]) for u in range(RING)]
        DT = [s.sb(f"DT{u}", [TP, BLK]) for u in range(RING)]
        q5 = [s.sb(f"q5{u}", [128, CH, 5]) for u in range(RING)]
        qm = [s.sb(f"qm{u}", [TP, NH]) for u in range(RING)]
        mb, qT = s.sb("mb", [TP, BLK]), s.sb("qT", [CH * 5, 128])
        junk = s.sb("junk", [TP, NH, BLK])
        adm, r = s.sb("adm", [TP, 2, NH]), s.sb("r", [TP, NH])
        al, ex = s.sb("al", [128, CH, NH]), s.sb("ex", [128, CH, NH])
        gs, po = [s.dma_cnt(f"gathered{u}") for u in range(RING)], s.cnt("pool_steps")
        kv = s.cnt("dve_steps")
        rows, turned, rowsT, spread, top = [s.cnt(n) for n in ("rows", "turned", "rowsT", "spread", "top")]
        newmax, looked = s.cnt("newmax"), s.cnt("looked")
        alpha, expd, scaled = s.cnt("alpha", dve, 1), s.cnt("expd"), s.cnt("scaled", dve, 1)
        scaled2 = s.cnt("scaled_by_act")
        summed, added = s.cnt("summed"), s.cnt("added")
        events = (rows, turned, rowsT, spread, top, newmax, looked, alpha, expd, scaled, scaled2, summed, added)
        iob = g.iota_tp[:, None, :].to_broadcast([128, CH, TP])
        bank = lambda k: g.PS[0:TP, k, :]

        def of(c, j):
            return j + (1 if c not in (alpha, scaled, summed, added) else 2)

        def gather(j, u):
            po.up(pool.tensor_copy(gi[u][:], g.srcidx[:, ds(j * CH, CH)]))
            wait(pool, po, po.now())
            po.up_now(pool)
            for c in range(CH):
                gs[u].up(pool.indirect_dma_start(out=hg[u][:, c, :], out_offset=None, in_=g.HT,
                                                 in_offset=bass.IndirectOffsetOnAxis(ap=gi[u][:, c:c + 1], axis=0)), 16)

        def slot_terms(j, u):
            rec = g.rec[:, ds(j * CH, CH), :]
            wait(dve, gs[u], gs[u].now())
            kv.up(dve.tensor_tensor(q5[u][:, :, 0:4], hg[u][:, :, HW:HW + NH], rec[:, :, 2:6], ALU.add))
            rows.up(dve.tensor_copy(q5[u][:, :, 4:5], rec[:, :, 1:2]))

        def turn(j, u, first=False):
            wait(pe, rows, of(rows, j))
            wait(pe, kv, kv.now())
            if not first:
                wait(pe, top, of(top, j - 1))
            turned.up(pe.transpose(g.PS[0:CH * 5, 0, 0:128], q5[u][:].rearrange("p c k -> p (c k)"), g.ident[:]))
            wait(act, turned, of(turned, j))
            if not first:
                wait(act, spread, of(spread, j - 1))
            rowsT.up(act.activation(qT[:], g.PS[0:CH * 5, 0, 0:128], ACT.Copy))

        def spread_rows(j, u):
            wait(pe, rowsT, of(rowsT, j))
            for k in (4, 0, 1, 2, 3):
                for c in range(CH):
                    ins = pe.matmul(bank(k)[:, c * 128:(c + 1) * 128], sel[:, c * 5 + k, :], qT[:], start=True, stop=True)
            spread.up(ins)

        def block_max(j, u):
            rec = g.rec[:, ds(j * CH, CH), :]
            wait(dve, spread, of(spread, j))
            chain(dve, kv, dve.tensor_scalar(DT[u][:], bank(4), g.pcol[0:TP, :], None, ALU.is_equal))
            chain(dve, kv, dve.tensor_scalar(mb[:], DT[u][:], 1.0, -NEG, ALU.subtract, ALU.mult))
            kv.up(dve.tensor_tensor(Dh[u][:], iob, rec[:, :, 1:2].to_broadcast([128, CH, TP]), ALU.is_equal))
            for h in range(NH):
                ins = dve.tensor_tensor_reduce(junk[:, h, :], mb[:], bank(h), 1.0, NEG, ALU.add, ALU.max, qm[u][:, h:h + 1])
                (top if h == NH - 1 else kv).up(ins)

        def new_max(j, u, b):
            wait(dve, top, of(top, j))
            wait(dve, kv, kv.now())
            chain(dve, kv, dve.tensor_tensor(qm[u][:], qm[u][:], row(AD, b), ALU.add))
            chain(dve, kv, dve.scalar_tensor_tensor(qm[u][:], qm[u][:], 0.2, qm[u][:], ALU.mult, ALU.max))
            kv.up(dve.tensor_scalar(adm[:, 0, :], row(AD, b), 0.0, None, ALU.add))
            chain(dve, kv, dve.tensor_tensor(adm[:, 1, :], qm[u][:], row(M, b), ALU.max))
            chain(dve, kv, dve.tensor_tensor(r[:], row(M, b), adm[:, 1, :], ALU.subtract))
            newmax.up(dve.tensor_scalar(row(M, b), adm[:, 1, :], 0.0, None, ALU.add))

        def look_up(j, u):
            wait(pe, newmax, of(newmax, j))
            wait(pe, alpha, of(alpha, j - 1))
            for c in range(CH):
                ins = pe.matmul(g.PS[:, 5, c * 8:c * 8 + 8], DT[u][:, c * 128:(c + 1) * 128],
                                adm[:].rearrange("p k h -> p (k h)"), start=True, stop=True)
            looked.up(ins)
            wait(dve, looked, of(looked, j))
            look = g.PS[:, 5, 0:CH * 8].rearrange("p (c k h) -> p c k h", c=CH, k=2)
            chain(dve, kv, dve.tensor_tensor(al[:], q5[u][:, :, 0:4], look[:, :, 0, :], ALU.add))
            chain(dve, kv, dve.scalar_tensor_tensor(al[:], al[:], 0.2, al[:], ALU.mult, ALU.max))
            chain(dve, kv, dve.tensor_tensor(al[:], al[:], look[:, :, 1, :], ALU.subtract))
            alpha.up(dve.tensor_scalar(al[:], al[:], 0.0, None, ALU.min))
            wait(act, alpha, of(alpha, j))
            wait(act, scaled, of(scaled, j - 1))
            act.activation(r[:], r[:], ACT.Exp)
            expd.up(act.activation(ex[:], al[:], ACT.Exp))

        def add_sums(j, b):
            wait(dve, summed, of(summed, j))
            acc2 = ACC[:, ds(b, 1), :].rearrange("p a (w c) -> p (a w) c", w=2)
            added.up(dve.tensor_tensor(acc2, acc2, g.PS[0:TP, 6:8, 0:HW // 2], ALU.add))

        def scale_rows(j, u, b):
            wait(dve, expd, of(expd, j))
            hrow = lambda c: hg[u][:, c, 0:HW].rearrange("p (h c) -> p h c", c=DH + 1)
            for c in range(2):
                ins = dve.tensor_tensor(hrow(c), hrow(c), ex[:, c, :, None].to_broadcast([128, NH, DH + 1]), ALU.mult)
                (scaled if c == 1 else kv).up(ins)
            wait(act, expd, of(expd, j))
            for c in range(2, CH):
                for h in range(NH):
                    ins = act.activation(hrow(c)[:, h, :], hrow(c)[:, h, :], ACT.Copy, scale=ex[:, c, h:h + 1])
            scaled2.up(ins)
            acc = ACC[:, ds(b, 1), :].rearrange("p a (h c) -> p (a h) c", c=DH + 1)
            wait(dve, added, of(added, j - 1))
            chain(dve, kv, dve.tensor_tensor(acc, acc, r[:, :, None].to_broadcast([TP, NH, DH + 1]), ALU.mult))

        def sum_rows(j, u):
            wait(pe, scaled, of(scaled, j))
            wait(pe, scaled2, of(scaled2, j))
            wait(pe, added, of(added, j - 1))
            for c in range(CH):
                for w in range(2):
                    ins = pe.matmul(bank(6 + w)[:, 0:HW // 2], Dh[u][:, c, :], hg[u][:, c, w * (HW // 2):(w + 1) * (HW // 2)],
                                    start=(c == 0), stop=(c == CH - 1))
            summed.up(ins)

        def tile_of(j):
            return dve.value_load(g.blk_tile[0:1, ds(j + 1, 1)], min_val=0, max_val=NT - 1)

        for k in (6, 7):
            ins = pe.matmul(bank(k), g.zeros[0:1, 0:TP], g.zeros[0:1, :], start=True, stop=True)
        summed.up(ins)
        wait(pe, v, v.now())
        gather(0, 0)
        slot_terms(0, 0)
        turn(0, 0, first=True)
        spread_rows(0, 0)
        block_max(0, 0)
        gather(1, 1)
        kvn = 17
        per = {c: RING for c in events}
        per.update({c: 64 for c in gs})
        per.update({po: 2 * RING, kv: RING * kvn})
        assert NB % RING == 1
        with loop(nc, NB // RING, per) as i:
            for u in range(RING):
                j, u1, u2 = i * RING + u, (u + 1) % RING, (u + 2) % RING
                b_last, b = tile_of(j - 1), tile_of(j)
                wait(pool, summed, of(summed, j - 1))
                gather(j + 2, u2)
                new_max(j, u, b)
                slot_terms(j + 1, u1)
                turn(j + 1, u1)
                look_up(j, u)
                spread_rows(j + 1, u1)
                add_sums(j - 1, b_last)
                scale_rows(j, u, b)
                block_max(j + 1, u1)
                sum_rows(j, u)
        j = NB - 1
        b_last, b = tile_of(j - 1), tile_of(j)
        new_max(j, 0, b)
        look_up(j, 0)
        add_sums(j - 1, b_last)
        scale_rows(j, 0, b)
        sum_rows(j, 0)
        add_sums(j, b)
        wait(dve, added, added.now())
        for c in gs:
            wait(pool, c, c.now())

        O = s.sb("O", [TP, NT, D])
        sq = s.sb("sq", [TP, NT, D])
        mu, rstd = s.sb("mu", [TP, D]), s.sb("rstd", [TP, D])
        cst = s.sb("cst", [TP, 3, D])
        den = s.sb("den", [TP, NT * NH])
        for k, w in enumerate((bias, gamma, beta)):
            d.up(sp.dma_start(cst[:, k, :], bcast(w, TP)), 16)
        acc = ACC[:].rearrange("p t (h c) -> p (t h) c", c=DH + 1)
        full = [TP, NT, D]
        chain(dve, v, dve.tensor_scalar(den[:], acc[:, :, DH], 1e-16, None, ALU.add))
        chain(dve, v, dve.reciprocal(den[:], den[:]))
        chain(dve, v, dve.tensor_tensor(O[:].rearrange("p t (h c) -> p (t h) c", c=DH), acc[:, :, 0:DH],
                                        den[:, :, None].to_broadcast([TP, NT * NH, DH]), ALU.mult))
        wait(dve, d, d.now())
        chain(dve, v, dve.tensor_tensor(O[:], O[:], cst[:, 0:1, :].to_broadcast(full), ALU.add))
        wait(pe, v, v.now())
        for t in range(NT):
            ins = pe.matmul(bank(0), g.ones[0:TP, 0:TP], O[:, t, :], start=(t == 0), stop=(t == NT - 1))
        wait(dve, q, q.up(ins))
        chain(dve, v, dve.tensor_scalar(mu[:], bank(0), 1.0 / N, None, ALU.mult))
        chain(dve, v, dve.tensor_tensor(O[:], O[:], mu[:, None, :].to_broadcast(full), ALU.subtract))
        chain(dve, v, dve.tensor_tensor(sq[:], O[:], O[:], ALU.mult))
        wait(pe, v, v.now())
        for t in range(NT):
            ins = pe.matmul(bank(1), g.ones[0:TP, 0:TP], sq[:, t, :], start=(t == 0), stop=(t == NT - 1))
        wait(dve, q, q.up(ins))
        chain(dve, v, dve.tensor_scalar(rstd[:], bank(1), 1.0 / N, EPS, ALU.mult, ALU.add))
        wait(act, v, v.now())
        a.up(act.activation(rstd[:], rstd[:], ACT.Sqrt))
        wait(dve, a, a.now())
        chain(dve, v, dve.reciprocal(rstd[:], rstd[:]))
        chain(dve, v, dve.tensor_tensor(rstd[:], rstd[:], cst[:, 1, :], ALU.mult))
        chain(dve, v, dve.tensor_tensor(O[:], O[:], rstd[:, None, :].to_broadcast(full), ALU.mult))
        chain(dve, v, dve.tensor_tensor(O[:], O[:], cst[:, 2:3, :].to_broadcast(full), ALU.add))
        chain(dve, v, dve.tensor_tensor(g.X[:], g.X[:], O[:], ALU.add))


PIECES = ((0, 417), (417, 834), (834, N))


def ranks(nc, s, L, ne, v):
    dve = nc.vector
    big = [TP, NT, ne, ne]
    cmp = s.sb("cmp", big)
    low = s.sb("low", [TP, ne, ne])
    rank, rank2 = s.sb("rank", [TP, NT, ne]), s.sb("rank2", [TP, NT, ne])
    chain(dve, v, dve.memset(low[:], 1.0))
    for e in range(ne):
        v.up(dve.memset(low[:, e, e:ne], 0.0))
    other, own = L[:, :, None, :].to_broadcast(big), L[:, :, :, None].to_broadcast(big)
    chain(dve, v, dve.tensor_tensor(cmp[:], other, own, ALU.is_gt))
    chain(dve, v, dve.tensor_reduce(rank[:], cmp[:], AX, ALU.add))
    chain(dve, v, dve.tensor_tensor(cmp[:], other, own, ALU.is_equal))
    chain(dve, v, dve.tensor_tensor(cmp[:], cmp[:], low[:, None, :, :].to_broadcast(big), ALU.mult))
    chain(dve, v, dve.tensor_reduce(rank2[:], cmp[:], AX, ALU.add))
    chain(dve, v, dve.tensor_tensor(rank[:], rank[:], rank2[:], ALU.add))
    return rank


def ffn1(nc, g, Wr, br, W1, b1, W2, b2):
    dve, pe, act, sp, pool = nc.vector, nc.tensor, nc.scalar, nc.sync, nc.gpsimd
    NE, F = W1.shape[0], W1.shape[2]
    FC = F // 128
    with stage(nc, g) as s:
        v, a, q, d = s.cnt("v"), s.cnt("a"), s.cnt("q"), s.cnt("d")
        XT = s.sb("XT", [128, KC, N])
        b1r, b1T = s.sb("b1r", [NE * FC, 128]), s.sb("b1T", [128, NE, FC])
        b2r = s.sb("b2r", [NE, D])
        w1 = [s.sb(f"w1_{u}", [128, KC, F]) for u in range(2)]
        w2 = [s.sb(f"w2_{u}", [128, FC, D]) for u in range(2)]
        hT = [s.sb(f"hT_{u}", [128, FC, N]) for u in range(2)]
        d.up(sp.dma_start(b1r[:], b1.rearrange("e (m p) -> (e m) p", p=128)), 16)
        d.up(sp.dma_start(b2r[:], b2), 16)
        L = logits(nc, g, s, Wr.rearrange("(c p) e -> p c e", p=128), br, NE, XT=XT)
        wait(pe, d, d.now())
        q.up(pe.transpose(g.PS[:, 7, 0:NE * FC], b1r[:], g.ident[0:NE * FC, 0:NE * FC]))
        wait(dve, q, q.now())
        v.up(dve.tensor_copy(b1T[:].rearrange("p e m -> p (e m)"), g.PS[:, 7, 0:NE * FC]))
        rank = ranks(nc, s, L, NE, v)
        top, gate = s.sb("top", [TP, NT]), s.sb("gate", [TP, NT])
        chain(dve, v, dve.tensor_reduce(top[:], L[:], AX, ALU.max))
        chain(dve, v, dve.tensor_tensor(top[:], top[:], top[:], ALU.subtract))
        wait(act, v, v.now())
        a.up(act.activation(top[:], top[:], ACT.Exp))
        wait(dve, a, a.now())
        chain(dve, v, dve.reciprocal(gate[:], top[:]))
        chain(dve, v, dve.tensor_tensor(gate[:], gate[:], top[:], ALU.mult))
        mask = s.sb("mask", [TP, NT, NE])
        chain(dve, v, dve.tensor_scalar(rank[:], rank[:], 1.0, None, ALU.is_lt))
        chain(dve, v, dve.tensor_tensor(mask[:], rank[:], gate[:, :, None].to_broadcast([TP, NT, NE]), ALU.mult))
        mT = s.sb("mT", [NE, N])
        to_experts(nc, g, s, mask, mT, NE, v, q)
        wait(pe, v, v.now())
        for t in range(NT):
            if t >= 2:
                wait(pe, v, v.now() - 1)
            q.up(pe.matmul(g.PS[0:TP, 6 + t % 2, :], mT[:, t * TP:(t + 1) * TP], b2r[:], start=True, stop=True))
            wait(dve, q, q.now())
            v.up(dve.tensor_tensor(g.X[:, t, :], g.X[:, t, :], g.PS[0:TP, 6 + t % 2, :], ALU.add))
        wait(dve, v, v.now())
        wait(pool, v, v.now())
        ld = [s.cnt(f"ld{u}") for u in range(2)]
        up, rl = s.cnt("up", dve, 12), s.cnt("relu", dve, 12)
        bc, bcol = s.cnt("bias_columns"), [s.sb(f"bcol{u}", [128, FC]) for u in range(2)]
        dn, ad = s.cnt("down", dve, 2 * NT), s.cnt("added", dve, 2 * NT)
        with loop(nc, NE // 2, {bc: 2, ld[0]: 32, ld[1]: 32, up: 12, rl: 12, dn: 2 * NT, ad: 2 * NT}) as i:
            for u in range(2):
                e = i * 2 + u
                wait(sp, dn, dn.ago(NT * (u + 1)))
                ld[u].up(sp.dma_start(w1[u][:], W1[ds(e, 1)].rearrange("a (c p) n -> p (a c) n", p=128)), 16)
                ld[u].up(sp.dma_start(w2[u][:], W2[ds(e, 1)].rearrange("a (c p) n -> p (a c) n", p=128)), 16)
                wait(pool, rl, rl.ago(6 * (u + 1)))
                bc.up(pool.tensor_copy(bcol[u][:], b1T[:, ds(e, 1), :].rearrange("p a m -> p (a m)")))
                wait(act, bc, bc.now())
                wait(pe, ld[u], ld[u].now())
                wait(act, dn, dn.ago(NT * (u + 1)))
                first = rl.now()
                for f in range(FC):
                    for k, (x0, x1) in enumerate(PIECES):
                        bk = 3 * f + k
                        wait(pe, rl, first - 5 + bk)
                        for c in range(KC):
                            ins = pe.matmul(g.PS[:, bk, 0:x1 - x0], w1[u][:, c, f * 128:(f + 1) * 128],
                                            XT[:, c, x0:x1], start=(c == 0), stop=(c == KC - 1))
                        up.up(ins)
                        wait(act, up, up.now())
                        rl.up(act.activation(hT[u][:, f, x0:x1], g.PS[:, bk, 0:x1 - x0], ACT.Relu,
                                             bias=bcol[u][:, f:f + 1]))
                wait(pe, rl, rl.now())
                for t in range(NT):
                    wait(pe, ad, ad.now() - 1)
                    for f in range(FC):
                        ins = pe.matmul(g.PS[0:TP, 6 + t % 2, :], hT[u][:, f, t * TP:(t + 1) * TP], w2[u][:, f, :],
                                        start=(f == 0), stop=(f == FC - 1))
                    dn.up(ins)
                    wait(dve, dn, dn.now())
                    ad.up(dve.scalar_tensor_tensor(g.X[:, t, :], g.PS[0:TP, 6 + t % 2, :],
                                                   mask[:, t, ds(e, 1)], g.X[:, t, :], ALU.mult, ALU.add))
                wait(dve, ad, ad.now())


def head_sums(nc, g, s, ev, ps, att_s, att_d, tmp, AS, AD, k):
    dve = nc.vector
    nh, w = AS.shape[2], tmp.shape[2]
    ev.up(dve.tensor_tensor(tmp[:, 0, :], ps, att_s[:], ALU.mult))
    chain(dve, ev, dve.tensor_tensor(tmp[:, 1, :], ps, att_d[:], ALU.mult))
    v4 = tmp[:].rearrange("p k (h c) -> p k h c", h=nh)
    ev.up(dve.tensor_reduce(row(AS, k), v4[:, 0], AX, ALU.add))
    ev.up(dve.tensor_reduce(row(AD, k), v4[:, 1], AX, ALU.add))


def to_rows(nc, g, T, R, n, v, q):
    wait(nc.tensor, v, v.now())
    for t in range(NT):
        ins = nc.tensor.transpose(g.PS[0:n, 5 + t // 4, (t % 4) * TP:(t % 4 + 1) * TP], T[:, t, :],
                                  g.ident[0:TP, 0:TP])
    wait(nc.vector, q, q.up(ins))
    for k in range(3):
        m = min(4, NT - 4 * k) * TP
        v.up(nc.vector.tensor_copy(R[:, 4 * k * TP:4 * k * TP + m], g.PS[0:n, 5 + k, 0:m]))
    wait(nc.vector, v, v.now())


def attention(nc, g, HH, OUT, AS, AD, b):
    dve, pe, act, sp, pool = nc.vector, nc.tensor, nc.scalar, nc.sync, nc.gpsimd
    NH, W = 4, HH.shape[2]
    DH = W // NH
    with stage(nc, g) as s:
        v, a, q, d = s.cnt("v"), s.cnt("a"), s.cnt("q"), s.cnt("d")
        MKF = s.sb("MK", [128, 5, N])
        MK = MKF[0:TP, :, :].rearrange("p a n -> p (a n)").bitcast(BF16).rearrange("p (t n) -> p t n", t=NT)
        bb = s.sb("bb", [TP, W])
        d.up(sp.dma_start(MK, g.MASK.rearrange("(t p) n -> p t n", p=TP)), 16)
        d.up(sp.dma_start(bb[:], bcast(b, TP)), 16)
        sel = s.sb("sel", [2 * NH, 2 * NH, TP])
        R = s.sb("R", [NH, N])
        MX, AB = s.sb("MX", [TP, NT, NH]), s.sb("AB", [TP, NT, 2 * NH])
        junk = s.sb("junk", [TP, N], BF16)
        AS2 = s.sb("AS2", [TP, NT, NH])
        v.up(dve.tensor_copy(sel[:], g.ident[0:2 * NH, 0:2 * NH, None].to_broadcast([2 * NH, 2 * NH, TP])))
        v.up(dve.tensor_scalar(AS2[:], AS[:], 0.2, None, ALU.mult))
        to_rows(nc, g, AS, R, NH, v, q)
        wait(pe, v, v.now())
        wait(dve, d, d.now())
        wait(sp, v, v.now())
        for h in range(NH):
            if h:
                wait(pe, v, v.now())
            for k in range(3):
                x0, x1 = 512 * k, min(512 * (k + 1), N)
                ins = pe.matmul(g.PS[0:TP, k, 0:x1 - x0], sel[0:NH, h, :], R[:, x0:x1], start=True, stop=True)
            wait(dve, q, q.up(ins))
            bc = g.PS[0:TP, 0:3, :].rearrange("p b n -> p (b n)")[:, 0:N]
            for t in range(NT):
                chain(dve, v, dve.tensor_tensor_reduce(junk[:], MK[:, t, :], bc, 1.0, NEG, ALU.add, ALU.max,
                                                       MX[:, t, h:h + 1]))
        chain(dve, v, dve.tensor_tensor(MX[:], MX[:], AD[:], ALU.add))
        chain(dve, v, dve.scalar_tensor_tensor(MX[:], MX[:], 0.2, MX[:], ALU.mult, ALU.max))
        v.up(dve.tensor_tensor(AB[:, :, 0:NH], AD[:], MX[:], ALU.subtract))
        chain(dve, v, dve.scalar_tensor_tensor(AB[:, :, NH:2 * NH], AD[:], 0.2, MX[:], ALU.mult, ALU.subtract))
        R8 = s.sb("R8", [2 * NH, N])
        to_rows(nc, g, AB, R8, 2 * NH, v, q)
        RA, RB = s.sb("RA", [TP, N]), s.sb("RB", [TP, N])
        ct, P = [MKF[:, u, :] for u in range(2)], [MKF[0:TP, 2 + u, :] for u in range(2)]
        z1 = [s.sb(f"z1{u}", [TP, N]) for u in range(2)]
        z2 = [s.sb(f"z2{u}", [TP, N]) for u in range(2)]
        den = s.sb("den", [TP, NT])
        ld = [s.cnt(f"ld{u}") for u in range(2)]
        lin, mx, ex, pm = s.cnt("lin"), s.cnt("mx", dve, 2), s.cnt("ex"), s.cnt("pm", dve, 2)
        mm = s.cnt("mm", dve, 2)
        for h in range(NH):
            wait(pe, v, v.now())
            for k, dst in enumerate((RA, RB)):
                for w in range(3):
                    x0, x1 = 512 * w, min(512 * (w + 1), N)
                    ins = pe.matmul(g.PS[0:TP, 3 * k + w, 0:x1 - x0], sel[:, k * NH + h, :], R8[:, x0:x1],
                                    start=True, stop=True)
            wait(dve, q, q.up(ins))
            for k, dst in enumerate((RA, RB)):
                v.up(dve.tensor_copy(dst[:], g.PS[0:TP, 3 * k:3 * k + 3, :].rearrange("p b n -> p (b n)")[:, 0:N]))
            for e in (pe, act, dve, sp, pool):
                wait(e, v, v.now())
            for k in range(6):
                pe.matmul(g.PS[0:TP, k, :], g.zeros[0:1, 0:TP], g.zeros[0:1, :], start=True, stop=True)
            with loop(nc, NT // 2, {ld[0]: 16, ld[1]: 16, lin: 2, mx: 2, ex: 2, pm: 2, mm: 2}) as i:
                for u in range(2):
                    k = i * 2 + u
                    wait(sp, pm, pm.ago(u + 1))
                    ld[u].up(sp.dma_start(ct[u], g.CT[ds(k * 128, 128), :]), 16)
                    wait(act, mx, mx.ago(u + 1))
                    lin.up(act.activation(z1[u][:], RB[:], ACT.Identity,
                                          bias=AS2[:, ds(k, 1), h:h + 1].rearrange("p a b -> p (a b)")))
                    wait(dve, lin, lin.now())
                    wait(dve, pm, pm.ago(u + 1))
                    mx.up(dve.scalar_tensor_tensor(z2[u][:], RA[:], AS[:, ds(k, 1), h:h + 1].rearrange("p a b -> p (a b)"),
                                                   z1[u][:], ALU.add, ALU.max))
                    wait(act, mx, mx.now())
                    ex.up(act.activation(z2[u][:], z2[u][:], ACT.Exp))
                    wait(pool, ex, ex.now())
                    wait(pool, ld[u], ld[u].now())
                    wait(pool, mm, mm.ago(u + 1))
                    pm.up(pool.tensor_tensor(P[u], z2[u][:], ct[u][0:TP], ALU.mult))
                    wait(pe, pm, pm.now())
                    for t in range(NT):
                        pe.matmul(g.PS[0:TP, t // 2, (t % 2) * 256:(t % 2) * 256 + 256], P[u][:, t * TP:(t + 1) * TP],
                                  HH[:, ds(k, 1), h * DH:(h + 1) * DH].rearrange("p a n -> p (a n)"),
                                  start=False, stop=True, skip_group_check=True)
                    for t in range(NT):
                        ins = pe.matmul(g.PS[0:TP, 5, t:t + 1], P[u][:, t * TP:(t + 1) * TP], g.ones[0:TP, 0:1],
                                        start=False, stop=True, skip_group_check=True)
                    mm.up(ins)
            wait(dve, mm, mm.now())
            wait(dve, v, v.now())
            chain(dve, v, dve.tensor_scalar(den[:], g.PS[0:TP, 5, 0:NT], 1e-16, None, ALU.add))
            chain(dve, v, dve.reciprocal(den[:], den[:]))
            o = OUT[:, :, h * DH:(h + 1) * DH]
            full = [TP, NT, DH]
            chain(dve, v, dve.tensor_tensor(o, g.PS[0:TP, 0:5, :].rearrange("p b (a n) -> p (b a) n", n=256),
                                            den[:, :, None].to_broadcast(full), ALU.mult))
            chain(dve, v, dve.tensor_tensor(o, o, bb[:, None, h * DH:(h + 1) * DH].to_broadcast(full), ALU.add))
            chain(dve, v, dve.tensor_scalar(o, o, 0.0, None, ALU.max))


def tiles_linear(nc, g, s, IN, Wt, halves, take, per):
    dve, pe, act = nc.vector, nc.tensor, nc.scalar
    C8 = IN.shape[2] // 128
    xi = [s.sb(f"xi{u}", [TP, IN.shape[2]]) for u in range(2)]
    xT = [s.sb(f"xT{u}", [128, C8, TP]) for u in range(2)]
    ci, t, a, mm = s.cnt("tl_ci", dve, 2), s.cnt("tl_t", dve, 2), s.cnt("tl_a", dve, 2), s.cnt("tl_mm", dve, 2)
    with loop(nc, NT // 2, {ci: 2, t: 2, a: 2, mm: 2, **per}) as i:
        for u in range(2):
            k = i * 2 + u
            wait(nc.gpsimd, t, t.ago(u + 1))
            ci.up(nc.gpsimd.tensor_copy(xi[u][:], row(IN, k)))
            wait(pe, ci, ci.now())
            wait(pe, a, a.ago(2) if u == 0 else a.now())
            for c in range(C8):
                ins = pe.transpose(g.PS[:, c // 4, (c % 4) * 128:(c % 4) * 128 + TP], xi[u][:, c * 128:(c + 1) * 128],
                                   g.ident[0:TP, 0:TP])
            t.up(ins)
            wait(act, t, t.now())
            wait(act, mm, mm.ago(u + 1))
            a.up(act.activation(xT[u][:].rearrange("p (b c) n -> p b c n", b=2),
                                g.PS[:, 0:2, :].rearrange("p b (c n) -> p b c n", n=128)[:, :, :, 0:TP], ACT.Copy))
            wait(pe, a, a.now())
            take(k, u, xT[u], mm)


def gnn2(nc, g, W1, as1, ad1, b1, W2, as2, ad2, b2, fcW, fcb):
    dve, pe, act, sp, pool = nc.vector, nc.tensor, nc.scalar, nc.sync, nc.gpsimd
    WD = W1.shape[1]
    NH = 4
    flat = lambda ap: ap.rearrange("h c -> (h c)")
    with stage(nc, g) as o:
        HH, OUT = o.sb("HH", [TP, NT, WD]), o.sb("OUT", [TP, NT, WD])
        AS, AD = o.sb("AS", [TP, NT, NH]), o.sb("AD", [TP, NT, NH])

        def parts(s, W, att_s, att_d):
            kc = W.shape[0] // 128
            Wt, sa, sd = s.sb("W", [128, kc, WD]), s.sb("att_s", [TP, WD]), s.sb("att_d", [TP, WD])
            tmp = s.sb("tmp", [TP, 2, WD])
            d = s.cnt("d")
            d.up(sp.dma_start(Wt[:], W.rearrange("(c p) n -> p c n", p=128)), 16)
            d.up(sp.dma_start(sa[:], bcast(flat(att_s), TP)), 16)
            d.up(sp.dma_start(sd[:], bcast(flat(att_d), TP)), 16)
            wait(pe, d, d.now())
            wait(dve, d, d.now())
            ev = s.cnt("ev", dve, 10)

            def take(k, u, xT, used):
                wait(pe, ev, ev.ago(5 * u + 5))
                for w in range(2):
                    for c in range(kc):
                        ins = pe.matmul(g.PS[0:TP, 2 + 2 * u + w, :], xT[:, c, :], Wt[:, c, w * 512:(w + 1) * 512],
                                        start=(c == 0), stop=(c == kc - 1))
                wait(dve, used, used.up(ins))
                ps = g.PS[0:TP, 2 + 2 * u:4 + 2 * u, :].rearrange("p b n -> p (b n)")
                ev.up(dve.tensor_scalar(row(HH, k), ps, 1.0, None, ALU.mult))
                wait(dve, ev, ev.now())
                head_sums(nc, g, s, ev, ps, sa, sd, tmp, AS, AD, k)
                wait(dve, ev, ev.now())
            return take, {ev: 10}

        with stage(nc, g) as s:
            take, per = parts(s, W1, as1, ad1)
            norm_tiles(nc, g, s, take, per)
        attention(nc, g, HH, OUT, AS, AD, b1)
        with stage(nc, g) as s:
            take, per = parts(s, W2, as2, ad2)
            tiles_linear(nc, g, s, OUT, None, 2, take, per)
        attention(nc, g, HH, OUT, AS, AD, b2)
        with stage(nc, g) as s:
            Wt, fb = s.sb("fcW", [128, WD // 128, D]), s.sb("fcb", [TP, D])
            d = s.cnt("d")
            d.up(sp.dma_start(Wt[:], fcW.rearrange("(c p) n -> p c n", p=128)), 16)
            d.up(sp.dma_start(fb[:], bcast(fcb, TP)), 16)
            wait(pe, d, d.now())
            wait(dve, d, d.now())
            ev = s.cnt("ev", dve, 4)

            def take(k, u, xT, used):
                wait(pe, ev, ev.ago(2 * u + 2))
                for c in range(WD // 128):
                    ins = pe.matmul(g.PS[0:TP, 2 + u, :], xT[:, c, :], Wt[:, c, :], start=(c == 0),
                                    stop=(c == WD // 128 - 1))
                wait(dve, used, used.up(ins))
                chain(dve, ev, dve.tensor_tensor(row(g.X, k), row(g.X, k), g.PS[0:TP, 2 + u, :], ALU.add))
                chain(dve, ev, dve.tensor_tensor(row(g.X, k), row(g.X, k), fb[:], ALU.add))

            tiles_linear(nc, g, s, OUT, None, 1, take, {ev: 4})


def norm_all(nc, s, T, v, a):
    dve, act = nc.vector, nc.scalar
    st, mv, rs = s.sb("na_st", [TP, NT, 6]), s.sb("na_mv", [TP, NT, 2]), s.sb("na_rs", [TP, NT])
    for t in range(NT):
        v.up(dve.bn_stats(st[:, t, :], T[:, t, :]))
    wait(dve, v, v.now())
    for t in range(NT):
        v.up(dve.bn_aggr(mv[:, t, :], st[:, t, :]))
    wait(dve, v, v.now())
    chain(dve, v, dve.tensor_scalar(rs[:], mv[:, :, 1], EPS, None, ALU.add))
    wait(act, v, v.now())
    a.up(act.activation(rs[:], rs[:], ACT.Sqrt))
    wait(dve, a, a.now())
    chain(dve, v, dve.reciprocal(rs[:], rs[:]))
    for t in range(NT):
        v.up(dve.tensor_scalar(T[:, t, :], T[:, t, :], mv[:, t, 0:1], rs[:, t:t + 1], ALU.subtract, ALU.mult))
    wait(dve, v, v.now())


def ffn2(nc, g, gfc1, gfc1_b, gfc2, gfc2_b, W1, b1, W2, b2, ln_g, ln_b, tW1, tb1, tW2, tb2, tg, tb):
    dve, pe, act, sp, pool = nc.vector, nc.tensor, nc.scalar, nc.sync, nc.gpsimd
    NE, F = tb1.shape
    FC = F // 128
    with stage(nc, g) as s:
        v, a, q, d = s.cnt("v"), s.cnt("a"), s.cnt("q"), s.cnt("d")
        XT, XN = s.sb("XT", [128, KC, N]), s.sb("XN", [TP, NT, D])
        G1, G2 = s.sb("G1", [128, KC, D]), s.sb("G2", [128, KC, NE])
        g1b, g2b = s.sb("g1b", [128, KC]), s.sb("g2b", [NE, 1])
        w1, w2 = s.sb("w1", [128, KC, F]), s.sb("w2", [128, FC, D])
        t1, t2 = s.sb("t1", [128, NE, KC * F]), s.sb("t2", [128, 2, FC * D])
        b1c, tb1r, tb2r = s.sb("b1c", [128, FC]), s.sb("tb1r", [NE, F]), s.sb("tb2r", [NE, D])
        b2m, lng, lnb = s.sb("b2m", [TP, D]), s.sb("lng", [TP, D]), s.sb("lnb", [TP, D])
        tl, l8 = s.sb("tl", [NE, 2, D]), s.sb("l8", [NE, 2, D])
        loads = [(G1[:], gfc1.rearrange("(c p) n -> p c n", p=128)), (G2[:], gfc2.rearrange("(c p) n -> p c n", p=128)),
                 (g1b[:], gfc1_b), (g2b[:], gfc2_b.rearrange("(e a) -> e a", a=1)),
                 (w1[:], W1.rearrange("(c p) n -> p c n", p=128)), (w2[:], W2.rearrange("(c p) n -> p c n", p=128)),
                 (b1c[:], b1), (tb1r[:], tb1), (tb2r[:], tb2), (b2m[:], bcast(b2, TP)), (lng[:], bcast(ln_g, TP)),
                 (lnb[:], bcast(ln_b, TP)), (tl[:, 0, :], tg), (tl[:, 1, :], tb), (l8[:, 0, :], bcast(ln_g, NE)),
                 (l8[:, 1, :], bcast(ln_b, NE))]
        for e in range(NE):
            loads.append((t1[:, e, :].rearrange("p (c n) -> p c n", n=F), tW1[e].rearrange("(c p) n -> p c n", p=128)))
        for dst, src in loads:
            d.up(sp.dma_start(dst, src), 16)

        def consume(k, u, xT, used):
            used.up_now(pe)
        norm_tiles(nc, g, s, consume, {}, XT=XT, XN=XN)
        nc.all_engine_barrier()
        for e in (pe, act, dve):
            wait(e, d, d.now())
        gsum, gh, gsr = s.sb("gsum", [128, KC, 3]), s.sb("gh", [128, 2, 512]), s.sb("gsr", [128, KC])
        n = 0
        for m in range(KC):
            for k, (x0, x1) in enumerate(PIECES):
                if n >= 4:
                    wait(pe, a, a.now() - 3)
                for c in range(KC):
                    ins = pe.matmul(g.PS[:, n % 4, 0:x1 - x0], G1[:, c, m * 128:(m + 1) * 128], XT[:, c, x0:x1],
                                    start=(c == 0), stop=(c == KC - 1))
                wait(act, q, q.up(ins))
                if n >= 2:
                    wait(act, a, a.now() - 1)
                a.up(act.activation(gh[:, n % 2, 0:x1 - x0], g.PS[:, n % 4, 0:x1 - x0], ACT.Relu,
                                    bias=g1b[:, m:m + 1], accum_out=gsum[:, m, k:k + 1]))
                n += 1
        wait(dve, a, a.now())
        chain(dve, v, dve.tensor_reduce(gsr[:], gsum[:], AX, ALU.add))
        wait(pe, v, v.now())
        for c in range(KC):
            ins = pe.matmul(g.PS[0:NE, 4, 0:1], G2[:, c, :], gsr[:, c:c + 1], start=(c == 0), stop=(c == KC - 1))
        wait(dve, q, q.up(ins))
        gc, gd, gb = s.sb("gc", [NE, 1]), s.sb("gd", [NE, NE]), s.sb("gb", [128, NE])
        g8 = s.sb("g8", [NE, TP])
        chain(dve, v, dve.scalar_tensor_tensor(gc[:], g.PS[0:NE, 4, 0:1], 1.0 / N, g2b[:], ALU.mult, ALU.add))
        v.up(dve.tensor_scalar(gd[:], g.ident[0:NE, 0:NE], gc[:, 0:1], None, ALU.mult))
        v.up(dve.tensor_scalar(g8[:], g.ones[0:NE, 0:TP], gc[:, 0:1], None, ALU.mult))
        chain(dve, v, dve.tensor_tensor(tl[:], tl[:], l8[:], ALU.subtract))
        wait(pe, v, v.now())
        pe.matmul(g.PS[:, 5, 0:NE], g.ones[0:NE, :], gd[:], start=True, stop=True)
        for f in range(FC):
            pe.matmul(g.PS[:, 4, 8 + f:9 + f], tb1r[:, f * 128:(f + 1) * 128], gc[:], start=True, stop=True)
        pe.matmul(g.PS[0:TP, 6, :], g8[:], tb2r[:], start=True, stop=True)
        pe.matmul(g.PS[0:TP, 7, :], g.ones[0:NE, 0:TP], tl[:, 0, :], start=True, stop=True)
        ins = pe.matmul(g.PS[0:TP, 0, :], g.ones[0:NE, 0:TP], tl[:, 1, :], start=True, stop=True)
        wait(dve, q, q.up(ins))
        v.up(dve.tensor_copy(gb[:], g.PS[:, 5, 0:NE]))
        v.up(dve.tensor_tensor(b1c[:], b1c[:], g.PS[:, 4, 8:8 + FC], ALU.add))
        v.up(dve.tensor_tensor(b2m[:], b2m[:], g.PS[0:TP, 6, :], ALU.add))
        v.up(dve.scalar_tensor_tensor(lng[:], g.PS[0:TP, 7, :], 0.03, lng[:], ALU.mult, ALU.add))
        chain(dve, v, dve.scalar_tensor_tensor(lnb[:], g.PS[0:TP, 0, :], 0.03, lnb[:], ALU.mult, ALU.add))
        lt = [s.cnt(f"lt{u}") for u in range(2)]
        w1f, w2f = w1[:].rearrange("p c n -> p (c n)"), w2[:].rearrange("p c n -> p (c n)")
        for e in range(NE):
            chain(dve, v, dve.scalar_tensor_tensor(w1f, t1[:, e, :], gb[:, e:e + 1], w1f, ALU.mult, ALU.add))
        for e in range(NE):
            u = e % 2
            if e >= 2:
                wait(sp, v, v.now() - 1)
            lt[u].up(sp.dma_start(t2[:, u, :].rearrange("p (c n) -> p c n", n=D), tW2[e].rearrange("(c p) n -> p c n", p=128)), 16)
            wait(dve, lt[u], lt[u].now())
            chain(dve, v, dve.scalar_tensor_tensor(w2f, t2[:, u, :], gb[:, e:e + 1], w2f, ALU.mult, ALU.add))
        hT = s.sb("hT", [128, FC, N])
        wait(pe, v, v.now())
        wait(act, v, v.now())
        for f in range(FC):
            for k, (x0, x1) in enumerate(PIECES):
                for c in range(KC):
                    ins = pe.matmul(g.PS[:, 1 + 3 * f + k, 0:x1 - x0], w1[:, c, f * 128:(f + 1) * 128], XT[:, c, x0:x1],
                                    start=(c == 0), stop=(c == KC - 1))
                wait(act, q, q.up(ins))
                a.up(act.activation(hT[:, f, x0:x1], g.PS[:, 1 + 3 * f + k, 0:x1 - x0], ACT.Relu, bias=b1c[:, f:f + 1]))
        wait(pe, a, a.now())
        for t in range(NT):
            if t >= 2:
                wait(pe, v, v.now() - 1)
            for f in range(FC):
                ins = pe.matmul(g.PS[0:TP, t % 2, :], hT[:, f, t * TP:(t + 1) * TP], w2[:, f, :],
                                start=(f == 0), stop=(f == FC - 1))
            wait(dve, q, q.up(ins))
            v.up(dve.tensor_tensor(XN[:, t, :], XN[:, t, :], g.PS[0:TP, t % 2, :], ALU.add))
        wait(dve, v, v.now())
        full = [TP, NT, D]
        chain(dve, v, dve.tensor_tensor(XN[:], XN[:], b2m[:, None, :].to_broadcast(full), ALU.add))
        norm_all(nc, s, XN, v, a)
        chain(dve, v, dve.tensor_tensor(XN[:], XN[:], lng[:, None, :].to_broadcast(full), ALU.mult))
        chain(dve, v, dve.tensor_tensor(XN[:], XN[:], lnb[:, None, :].to_broadcast(full), ALU.add))
        chain(dve, v, dve.tensor_tensor(g.X[:], g.X[:], XN[:], ALU.add))


def gnn3(nc, g, Ws, Wn, bias, gamma, beta):
    dve, pe, act, sp = nc.vector, nc.tensor, nc.scalar, nc.sync
    with stage(nc, g) as s:
        v, a, d = s.cnt("v"), s.cnt("a"), s.cnt("d")
        Wt = [s.sb(f"W{w}", [128, KC, D]) for w in range(2)]
        S, H = s.sb("S", [TP, NT, D]), s.sb("H", [TP, NT, D])
        cst, inv, y = s.sb("cst", [TP, 3, D]), s.sb("inv", [TP, NT]), s.sb("y", [TP, NT, 256])
        for w, src in enumerate((Ws, Wn)):
            d.up(sp.dma_start(Wt[w][:], src.rearrange("(c p) n -> p c n", p=128)), 16)
        for k, w in enumerate((bias, gamma, beta)):
            d.up(sp.dma_start(cst[:, k, :], bcast(w, TP)), 16)
        chain(dve, v, dve.tensor_scalar(inv[:], g.deg[:], 1.0, None, ALU.max))
        chain(dve, v, dve.reciprocal(inv[:], inv[:]))
        wait(pe, d, d.now())
        wait(dve, d, d.now())
        ev = s.cnt("ev", dve, 4)

        def consume(k, u, xT, used):
            wait(pe, ev, ev.ago(2 * u + 2))
            for w in range(2):
                for c in range(KC):
                    ins = pe.matmul(g.PS[0:TP, 2 + 2 * u + w, :], xT[:, c, :], Wt[w][:, c, :],
                                    start=(c == 0), stop=(c == KC - 1))
            wait(dve, used, used.up(ins))
            ev.up(dve.tensor_tensor(row(S, k), g.PS[0:TP, 2 + 2 * u, :], cst[:, 0, :], ALU.add))
            ev.up(dve.tensor_scalar(row(H, k), g.PS[0:TP, 3 + 2 * u, :], 1.0, None, ALU.mult))

        norm_tiles(nc, g, s, consume, {ev: 4})
        wait(pe, ev, ev.now())
        wait(dve, ev, ev.now())

        def finish(half, ps):
            c = slice(half * 256, half * 256 + 256)
            chain(dve, v, dve.tensor_tensor(y[:], ps, H[:, :, c], ALU.subtract))
            chain(dve, v, dve.tensor_tensor(y[:], y[:], inv[:, :, None].to_broadcast([TP, NT, 256]), ALU.mult))
            ins = dve.tensor_tensor(S[:, :, c], S[:, :, c], y[:], ALU.add)
            return ins

        out = aggregate(nc, g, s, g.CT, H, finish)
        wait(dve, out, out.now())
        norm_all(nc, s, S, v, a)
        full = [TP, NT, D]
        chain(dve, v, dve.tensor_tensor(S[:], S[:], cst[:, 1:2, :].to_broadcast(full), ALU.mult))
        chain(dve, v, dve.tensor_tensor(S[:], S[:], cst[:, 2:3, :].to_broadcast(full), ALU.add))
        chain(dve, v, dve.tensor_tensor(g.X[:], g.X[:], S[:], ALU.add))


def ffn3(nc, g, Wr, br, Wu, bu, Wd, bd):
    dve, pe, act, sp, pool = nc.vector, nc.tensor, nc.scalar, nc.sync, nc.gpsimd
    NE, F = Wd.shape[0], Wd.shape[1]
    NG = Wu.shape[0]
    GS = NE // NG
    K = N // NE
    SL = -(-K // 8) * 8
    FP = 105
    FM = F // FP
    SG = GS * SL
    with stage(nc, g) as s:
        v, a, q, d = s.cnt("v"), s.cnt("a"), s.cnt("q"), s.cnt("d")
        WU = [s.sb(f"wu{u}", [128, KC, F]) for u in range(1)]
        WD_ = [s.sb(f"wd{u}", [FP, FM, D]) for u in range(GS)]
        bdb = [s.sb(f"bdb{u}", [SL, D]) for u in range(GS)]
        buT = [s.sb(f"buT{u}", [FP, FM]) for u in range(1)]
        d.up(sp.dma_start(g.Y.rearrange("(t p) d -> p t d", p=TP), g.X[:]), 16)
        L = logits(nc, g, s, Wr.rearrange("(c p) e -> p c e", p=128), br, NE, dram=g.XND)
        softmax_rows(nc, s, L, NE, v, a)
        WT = s.sb("WT", [NE, N])
        to_experts(nc, g, s, L, WT, NE, v, q)
        sw, si = top_slots(nc, g, s, WT, NE, SL, K, v, q, GS)
        wait(pool, v, v.now())
        wait(pool, d, d.now())
        wait(dve, d, d.now())
        xg = s.sb("xg", [SL, GS, D])
        xgT = s.sb("xgT", [128, KC, SG])
        hT = s.sb("hT", [FP, FM, SG])
        wo = g.X[0:SL, 0:GS, :]
        gi, ci = s.sb("gi", [SL, GS], I32), s.sb("ci", [SL, GS], I32)
        lu, lw = s.cnt("lu"), [s.cnt(f"lw{k}") for k in range(GS)]
        gs, po = s.dma_cnt("gathered"), s.cnt("pool_steps", dve, 1)
        tr, tc = s.cnt("transposed", dve, 1), s.cnt("transposed_copied", dve, 1)
        mu, sl = s.cnt("up", dve, FM), s.cnt("silu", dve, FM)
        md, ev = s.cnt("down", dve, GS), s.cnt("weighted", dve, 2 * GS)
        sc, sd = s.dma_cnt("scattered"), s.cnt("scatter_over", dve, 2 * GS)
        go = s.cnt("go")
        per = {go: 1, lu: 32, gs: 16 * GS, po: 4, tr: 1, tc: 1, mu: FM, sl: FM, md: GS, ev: 2 * GS,
               sc: 16 * GS, sd: 2 * GS}
        per.update({c: 32 for c in lw})

        def gather(e):
            po.up(pool.tensor_copy(gi[:], si[:, 0, ds(e, GS)]))
            wait(pool, po, po.now())
            po.up_now(pool)
            for k in range(GS):
                gs.up(pool.indirect_dma_start(out=xg[:, k, :], out_offset=None, in_=g.XND,
                                              in_offset=bass.IndirectOffsetOnAxis(ap=gi[:, k:k + 1], axis=0)), 16)

        gather(0)
        with loop(nc, NG, per) as i:
            e0 = i * GS
            wait(sp, mu, mu.ago(FM))
            lu.up(sp.dma_start(WU[0][:], Wu[ds(i, 1)].rearrange("a (c p) n -> p (a c) n", p=128)), 16)
            wait(sp, sl, sl.ago(FM))
            lu.up(sp.dma_start(buT[0][:], bu[ds(i, 1)].rearrange("a (p m) -> p (a m)", m=FM)), 16)
            for k in range(GS):
                wait(sp, ev, ev.ago(2 * k + 2))
                lw[k].up(sp.dma_start(WD_[k][:], Wd[ds(e0 + k, 1)].rearrange("a (p m) n -> p (a m) n", m=FM)), 16)
                lw[k].up(sp.dma_start(bdb[k][:], bcast(bd[ds(e0 + k, 1)].rearrange("a n -> (a n)"), SL)), 16)
            wait(pe, gs, gs.now())
            wait(pe, sl, sl.ago(FM))
            go.up_now(pe)
            for c in range(KC):
                for k in range(GS):
                    ins = pe.transpose(g.PS[:, c // 2, (c % 2) * SG + k * SL:(c % 2) * SG + (k + 1) * SL],
                                       xg[:, k, c * 128:(c + 1) * 128], g.ident[0:SL, 0:SL])
            tr.up(ins)
            wait(pool, tr, tr.now())
            gather(e0 + GS)
            wait(dve, tr, tr.now())
            wait(dve, mu, mu.ago(FM))
            tc.up(dve.tensor_copy(xgT[:].rearrange("p (b c) n -> p b (c n)", b=2), g.PS[:, 0:2, 0:2 * SG]))
            wait(pe, tc, tc.now())
            wait(pe, lu, lu.now())
            wait(act, lu, lu.now())
            wait(act, md, md.ago(GS))
            first = sl.now()
            for m in range(FM):
                bk = m % 4
                wait(pe, sl, first + m - 3)
                for c in range(KC):
                    ins = pe.matmul(g.PS[0:FP, bk, 0:SG], WU[0][:, c, m:F:FM], xgT[:, c, :],
                                    start=(c == 0), stop=(c == KC - 1))
                mu.up(ins)
                wait(act, mu, mu.now())
                sl.up(act.activation(hT[:, m, :], g.PS[0:FP, bk, 0:SG], ACT.Silu, bias=buT[0][:, m:m + 1]))
            wait(pe, sl, sl.now())
            po.up(pool.tensor_copy(ci[:], si[:, 0, ds(e0, GS)]))
            wait(pool, po, po.now())
            po.up_now(pool)
            for k in range(GS):
                wait(pe, lw[k], lw[k].now())
                wait(pe, ev, ev.ago(2 * k + 2))
                for m in range(FM):
                    ins = pe.matmul(g.PS[0:SL, 4 + k, :], hT[:, m, k * SL:(k + 1) * SL], WD_[k][:, m, :],
                                    start=(m == 0), stop=(m == FM - 1))
                md.up(ins)
                wait(dve, md, md.now())
                wait(dve, lw[k], lw[k].now())
                wait(dve, sd, sd.ago(2 * k + 2))
                chain(dve, ev, dve.tensor_tensor(wo[:, k, :], g.PS[0:SL, 4 + k, :], bdb[k][:], ALU.add))
                ev.up(dve.tensor_scalar(wo[:, k, :], wo[:, k, :], sw[:, 0, ds(e0 + k, 1)], None, ALU.mult))
                wait(pool, ev, ev.now())
                sd.up_now(pool)
                sc.up(pool.indirect_dma_start(out=g.Y, out_offset=bass.IndirectOffsetOnAxis(
                    ap=ci[:, k:k + 1], axis=0), in_=wo[:, k, :], in_offset=None, compute_op=ALU.add), 16)
                wait(pool, sc, sc.now())
                sd.up_now(pool)
        wait(sp, sc, sc.now())
        wait(sp, gs, gs.now())


def program(nc, A, out):
    ctx = ExitStack()
    with ctx:
        g = Env()
        g.ctx = ctx
        g.k = 0
        def dram(name, shape, dt=F32):
            return nc.dram_tensor(name, shape, dt, kind="Internal").ap()
        g.recd = dram("recd", (NB * BLK, 8))
        g.XND, g.Y = dram("XND", (N, D)), dram("Y", (N, D))
        g.HT = dram("HT", (N, D + 8))
        g.CT, g.MASK = dram("CT", (NT * 128, N)), dram("MASK", (N, N), BF16)
        g.blk_tile = ctx.enter_context(nc.sbuf_tensor("blk_tile", [1, NB + 1], I32))
        g.srcidx = ctx.enter_context(nc.sbuf_tensor("srcidx", [128, (NB + 1) * CH], I32))
        g.ae_mean = ctx.enter_context(nc.sbuf_tensor("ae_mean", [TP, 4], F32))
        constants(nc, g, ctx, A["x"])
        group_edges(nc, g, A["src"], A["dst"], A["edge_attr_4"], A["L1_gnn_W_edge"], A["L1_gnn_att_edge"])
        count_matrix(nc, g)
        gnn0(nc, g, A["L0_gnn_W"], A["L0_gnn_b"])
        ffn0(nc, g, A["L0_ffn_gate_w"], A["L0_ffn_gate_b"], A["L0_ffn_w1"], A["L0_ffn_b1"], A["L0_ffn_w2"], A["L0_ffn_b2"])
        gnn1(nc, g, *[A["L1_gnn_" + n] for n in ("W", "att_src", "att_dst", "bias", "gamma", "beta")])
        ffn1(nc, g, *[A["L1_ffn_" + n] for n in ("Wr", "br", "W1", "b1", "W2", "b2")])
        gnn2(nc, g, *[A["L2_gnn_" + n] for n in ("W1", "att_src1", "att_dst1", "b1", "W2", "att_src2", "att_dst2", "b2",
                                                "fcW", "fcb")])
        ffn2(nc, g, *[A["L2_ffn_" + n] for n in ("gfc1_w", "gfc1_b", "gfc2_w", "gfc2_b", "W1", "b1", "W2", "b2", "ln_g",
                                                "ln_b", "tv_W1", "tv_b1", "tv_W2", "tv_b2", "tv_ln_g", "tv_ln_b")])
        gnn3(nc, g, *[A["L3_gnn_" + n] for n in ("W_self", "W_neigh", "bias", "gamma", "beta")])
        ffn3(nc, g, *[A["L3_ffn_" + n] for n in ("W_router", "b_router", "W_up", "b_up", "W_down", "b_down")])
        with stage(nc, g) as s:
            d = s.cnt("d")
            d.up(nc.sync.dma_start(out, g.Y), 16)
            wait(nc.sync, d, d.now())


_INS = (
    'x src dst edge_attr_4 '
    'L0_gnn_W L0_gnn_b L0_ffn_gate_w L0_ffn_gate_b '
    'L0_ffn_w1 L0_ffn_b1 L0_ffn_w2 L0_ffn_b2 '
    'L1_gnn_W L1_gnn_W_edge L1_gnn_att_src L1_gnn_att_dst '
    'L1_gnn_att_edge L1_gnn_bias L1_gnn_gamma L1_gnn_beta '
    'L1_ffn_Wr L1_ffn_br L1_ffn_W1 L1_ffn_b1 '
    'L1_ffn_W2 L1_ffn_b2 L2_gnn_W1 L2_gnn_att_src1 '
    'L2_gnn_att_dst1 L2_gnn_b1 L2_gnn_W2 L2_gnn_att_src2 '
    'L2_gnn_att_dst2 L2_gnn_b2 L2_gnn_fcW L2_gnn_fcb '
    'L2_ffn_gfc1_w L2_ffn_gfc1_b L2_ffn_gfc2_w L2_ffn_gfc2_b '
    'L2_ffn_W1 L2_ffn_b1 L2_ffn_W2 L2_ffn_b2 '
    'L2_ffn_ln_g L2_ffn_ln_b L2_ffn_tv_W1 L2_ffn_tv_b1 '
    'L2_ffn_tv_W2 L2_ffn_tv_b2 L2_ffn_tv_ln_g L2_ffn_tv_ln_b '
    'L3_gnn_W_self L3_gnn_W_neigh L3_gnn_bias L3_gnn_gamma '
    'L3_gnn_beta L3_ffn_W_router L3_ffn_b_router L3_ffn_W_up '
    'L3_ffn_b_up L3_ffn_W_down L3_ffn_b_down '
).split()
_TURNED = ["L0_ffn_gate_w", "L2_ffn_gfc1_w", "L2_ffn_gfc2_w", "L2_ffn_W1", "L2_ffn_W2", "L2_ffn_tv_W1", "L2_ffn_tv_W2",
           "L3_gnn_W_self", "L3_gnn_W_neigh"]
_COLUMNS = ["L2_ffn_gfc1_b", "L2_ffn_b1"]


def kernel(**inputs):
    import numpy as _np
    import concourse.bacc as _bacc
    from concourse import mybir as _mybir
    from concourse.bass_utils import run_bass_kernel_spmd as _run
    nc = _bacc.Bacc("TRN2", target_bir_lowering=False, num_devices=1)
    arrays, A = {}, {}
    for name in _INS:
        a = _np.asarray(inputs[name])
        a = a.reshape(-1, 128).T if name in _COLUMNS else a.swapaxes(-1, -2) if name in _TURNED else a
        a = _np.ascontiguousarray(a)
        arrays[f"in_{name}"] = a
        A[name] = nc.dram_tensor(f"in_{name}", a.shape, _mybir.dt.from_np(a.dtype), kind="ExternalInput").ap()
    out = nc.dram_tensor("out_0", (N, D), F32, kind="ExternalOutput").ap()
    program(nc, A, out)
    return _run(nc, [arrays], core_ids=[0]).results[0]["out_0"]
```

```python
from contextlib import ExitStack

import concourse.bass as bass
from concourse import mybir

F32 = mybir.dt.float32
BF16 = mybir.dt.bfloat16
F16 = mybir.dt.float16
I32 = mybir.dt.int32
U32 = mybir.dt.uint32
ALU = mybir.AluOpType
ACT = mybir.ActivationFunctionType
AX = mybir.AxisListType.X
ds = bass.ds

N, D, E = 1250, 512, 20000
TP, NT = 125, 10
KC = D // 128
EC = E // TP
BLK, CH = 512, 4
NB = (E + NT * (BLK - 1)) // BLK
NEG = -1.0e30
EPS = 1e-5


class Count:

    def __init__(self, nc, ctx, name, giver=None, credit=0):
        self.sem = ctx.enter_context(nc.semaphore(name))
        self.base, self.n, self.stack = credit, 0, []
        if credit:
            giver.sem_inc(self.sem, credit)

    def up(self, ins, k=1):
        ins.then_inc(self.sem, k)
        self.n += k
        return self.base + self.n

    def up_now(self, eng):
        eng.sem_inc(self.sem, 1)
        self.n += 1
        return self.base + self.n

    def now(self):
        return self.base + self.n

    def ago(self, m, turns=1):
        start, per = self.stack[-1]
        assert not isinstance(start, int) or start + m - turns * per > 0, (self.sem, "needs more credit")
        return self.base + (m - turns * per)

    def enter(self, i, per):
        self.stack.append((self.base + self.n, per))
        self.base, self.n = self.base + self.n + i * per, 0

    def leave(self, trips):
        start, per = self.stack.pop()
        assert self.n == per, (self.sem, "increments in a turn:", self.n, "declared:", per)
        self.base, self.n = start + trips * per, 0


class loop:

    def __init__(self, nc, trips, per):
        self.nc, self.trips, self.per = nc, trips, per

    def __enter__(self):
        self.f = self.nc.Fori(0, self.trips)
        i = self.f.__enter__()
        for c, k in self.per.items():
            c.enter(i, k)
        return i

    def __exit__(self, *a):
        r = self.f.__exit__(*a)
        if a[0] is None:
            for c in self.per:
                c.leave(self.trips)
        return r


def wait(eng, c, v):
    eng.wait_ge(c.sem, v)


def chain(eng, c, ins):
    wait(eng, c, c.up(ins))


def row(t, i):
    return t[:, ds(i, 1), :].rearrange("p a n -> p (a n)")


def selector(nc, g, s, n, v):
    dve = nc.vector
    one, sel = s.sb(f"sel_one_{n}", [3 * n, n]), s.sb(f"sel_{n}", [3 * n, n, TP], BF16)
    chain(dve, v, dve.tensor_reduce(one[:], g.ident[0:3 * n, 0:3 * n].rearrange("r (p j) -> r j p", j=n), AX, ALU.add))
    chain(dve, v, dve.tensor_copy(sel[:], one[:, :, None].to_broadcast([3 * n, n, TP])))
    return sel


def split(dve, c, x, parts, rest):
    chain(dve, c, dve.tensor_copy(parts[0], x))
    chain(dve, c, dve.tensor_tensor(rest, x, parts[0], ALU.subtract))
    chain(dve, c, dve.tensor_copy(parts[1], rest))
    chain(dve, c, dve.tensor_tensor(rest, rest, parts[1], ALU.subtract))
    return dve.tensor_copy(parts[2], rest)


class Env:
    pass


def stage(nc, g):
    class S(ExitStack):
        def __exit__(self, *a):
            if a[0] is None:
                nc.all_engine_barrier()
                if self.counts:
                    nums = sorted(c.sem.num for c in self.counts)
                    first = [n for n in nums if n - 1 not in nums]
                    last = [n for n in nums if n + 1 not in nums]
                    for m, n in zip(first, last):
                        nc.gpsimd.sem_clear(range(m, n + 1))
                    nc.all_engine_barrier()
            return super().__exit__(*a)
    s = S()
    g.k += 1
    k = g.k
    s.sb = lambda name, shape, dt=F32: s.enter_context(nc.sbuf_tensor(f"{name}_{k}", shape, dt))
    s.counts = []

    def cnt(name, giver=None, credit=0):
        s.counts.append(Count(nc, s, f"{name}_{k}", giver, credit))
        return s.counts[-1]
    s.cnt = cnt
    s.dma_cnt = lambda name: Count(nc, g.ctx, f"{name}_{k}")
    return s


def bcast(ap, p):
    return ap.partition_broadcast(p)


def constants(nc, g, ctx, x):
    def sb(name, shape, dt=F32):
        return ctx.enter_context(nc.sbuf_tensor(name, shape, dt))
    g.X = sb("x_res", [TP, NT, D])
    g.ident = sb("ident", [128, 128])
    g.identb = sb("ident_bf", [128, 128], BF16)
    g.iota = sb("iota_nodes", [128, N], F16)
    g.iota_tp = sb("iota_tp", [128, TP])
    g.pcol = sb("partition_number", [128, 1])
    g.ones = sb("ones", [128, 128])
    g.zeros = sb("zeros_bf", [1, 512], BF16)
    g.deg = sb("degree", [TP, NT])
    g.PS = ctx.enter_context(nc.psum_tensor("psum", [128, 8, 512], F32))
    g.rec = sb("records", [128, NB * CH, 8])
    with stage(nc, g) as s:
        cp, cd = s.cnt("c_pool"), s.cnt("c_dma")
        cd.up(nc.sync.dma_start(g.X[:], x.rearrange("(t p) d -> p t d", p=TP)), 16)
        chain(nc.gpsimd, cp, nc.gpsimd.memset(g.ident[:], 0.0))
        cp.up(nc.gpsimd.affine_select(out=g.ident[:], in_=g.ident[:], compare_op=ALU.not_equal, fill=1.0,
                                      base=0, pattern=[[-1, 128]], channel_multiplier=1))
        cp.up(nc.gpsimd.iota(g.iota[:], [[1, N]], base=0, channel_multiplier=0,
                             allow_small_or_imprecise_dtypes=True))
        cp.up(nc.gpsimd.iota(g.iota_tp[:], [[1, TP]], base=0, channel_multiplier=0,
                             allow_small_or_imprecise_dtypes=True))
        cp.up(nc.gpsimd.iota(g.pcol[:], [[1, 1]], base=0, channel_multiplier=1,
                             allow_small_or_imprecise_dtypes=True))
        cp.up(nc.gpsimd.memset(g.ones[:], 1.0))
        cp.up(nc.gpsimd.memset(g.zeros[:], 0.0))
        wait(nc.gpsimd, cp, cp.now())
        cp.up(nc.gpsimd.tensor_copy(g.identb[:], g.ident[:]))
        wait(nc.gpsimd, cp, cp.now())
        wait(nc.sync, cd, cd.now())


def group_edges(nc, g, src, dst, edge_attr, W_edge, att_edge, H, W0):
    dve, pe, pool, sp, act = nc.vector, nc.tensor, nc.gpsimd, nc.sync, nc.scalar
    with stage(nc, g) as s:
        v, d, p, q = s.cnt("v"), s.cnt("d"), s.cnt("p"), s.cnt("q")
        srci, dsti = s.sb("srci", [TP, EC], I32), s.sb("dsti", [TP, EC], I32)
        ea = s.sb("ea", [TP, EC, 4])
        we = s.sb("we", [TP, 4, D])
        att = s.sb("att", [TP, D])
        E8 = s.sb("edge_records", [TP, EC, 8])
        dstf = s.sb("dstf", [TP, EC])
        ge = s.sb("ge", [TP, NT + 1, EC])
        oh = s.sb("oh", [TP, NT, EC])
        cum = s.sb("cum", [TP, NT, EC])
        zero = s.sb("zero", [TP, NT, EC])
        tri = s.sb("tri", [TP, TP])
        cnt = s.sb("cnt", [TP, NT])
        tot = s.sb("tot", [TP, NT])
        toti = s.sb("toti", [TP, NT], I32)
        nblk = s.sb("nblk", [TP, NT])
        cblk = s.sb("cblk", [TP, NT])
        off = s.sb("off", [TP, NT])
        pos = s.sb("pos", [TP, EC])
        posi = s.sb("posi", [TP, EC], I32)
        V = s.sb("V", [TP, 16])
        vt = s.sb("vt", [TP, 4, D])
        am = s.sb("am", [TP, 4])
        pad = s.sb("pad", [128, NB * CH, 8])
        blkf = s.sb("blkf", [TP, NB])
        blkb = s.sb("blkb", [TP, NB])
        Wt, wd = s.sb("W", [128, KC, D]), s.cnt("w_loaded")
        d.up(sp.dma_start(dsti[:], dst.rearrange("(p c) -> p c", c=EC)), 16)
        d.up(sp.dma_start(srci[:], src.rearrange("(p c) -> p c", c=EC)), 16)
        d.up(sp.dma_start(ea[:], edge_attr.rearrange("(p c) k -> p c k", c=EC)), 16)
        d.up(sp.dma_start(we[:], bcast(W_edge, TP)), 16)
        d.up(sp.dma_start(att[:], bcast(att_edge.rearrange("h c -> (h c)"), TP)), 16)
        wd.up(sp.dma_start(Wt[:], W0.rearrange("(c p) n -> p c n", p=128)), 16)
        chain(pool, p, pool.memset(tri[:], 1.0))
        p.up(pool.affine_select(out=tri[:], in_=tri[:], compare_op=ALU.is_gt, fill=0.0, base=0,
                                pattern=[[1, TP]], channel_multiplier=-1))
        chain(pool, p, pool.memset(pad[:], 0.0))
        p.up(pool.memset(pad[:, :, 1:2], -1.0))
        p.up(pool.iota(blkf[:], [[1, NB]], base=0, channel_multiplier=0, allow_small_or_imprecise_dtypes=True))
        wait(sp, p, p.now())
        pd = s.cnt("pads")
        pd.up(sp.dma_start(g.recd.rearrange("(c p) k -> p c k", p=128), pad[:]), 16)
        wait(dve, d, d.now())
        wait(dve, p, p.now())
        v.up(dve.memset(zero[:], 0.0))
        chain(dve, v, dve.tensor_copy(dstf[:], dsti[:]))
        chain(dve, v, dve.memset(E8[:], 0.0))
        v.up(dve.tensor_copy(E8[:, :, 0], srci[:]))
        for b in range(NT + 1):
            v.up(dve.tensor_scalar(ge[:, b, :], dstf[:], float(TP * b), None, ALU.is_ge))
        wait(dve, v, v.now())
        chain(dve, v, dve.tensor_tensor(oh[:], ge[:, 0:NT, :], ge[:, 1:NT + 1, :], ALU.subtract))
        chain(dve, v, dve.tensor_reduce(pos[:], ge[:, 1:NT, :].rearrange("p b c -> p c b"), AX, ALU.add))
        v.up(dve.scalar_tensor_tensor(E8[:, :, 1], pos[:], -float(TP), dstf[:], ALU.mult, ALU.add))
        flat = "p b c -> p (b c)"
        chain(dve, v, dve.tensor_tensor_scan(cum[:].rearrange(flat), oh[:].rearrange(flat), zero[:].rearrange(flat),
                                             0.0, ALU.add, ALU.add))
        v.up(dve.tensor_copy(cnt[:, 0:1], cum[:, 0, EC - 1:EC]))
        chain(dve, v, dve.tensor_tensor(cnt[:, 1:NT], cum[:, 1:NT, EC - 1], cum[:, 0:NT - 1, EC - 1], ALU.subtract))
        wait(pe, v, v.now())
        wait(pe, p, p.now())
        q.up(pe.matmul(g.PS[0:TP, 0, 0:NT], tri[:], cnt[:], start=True, stop=True))
        q.up(pe.matmul(g.PS[0:TP, 1, 0:NT], g.ones[0:TP, 0:TP], cnt[:], start=True, stop=True))
        wait(dve, q, q.now())
        chain(dve, v, dve.tensor_scalar(tot[:], g.PS[0:TP, 1, 0:NT], float(BLK - 1), None, ALU.add))
        chain(dve, v, dve.tensor_copy(toti[:], tot[:]))
        chain(dve, v, dve.tensor_single_scalar(toti[:], toti[:], 9, ALU.logical_shift_right))
        chain(dve, v, dve.tensor_copy(nblk[:], toti[:]))
        chain(dve, v, dve.tensor_tensor_scan(cblk[:], nblk[:], zero[:, 0, 0:NT], 0.0, ALU.add, ALU.add))
        chain(dve, v, dve.tensor_tensor(off[:], cblk[:], nblk[:], ALU.subtract))
        chain(dve, v, dve.scalar_tensor_tensor(off[:], off[:], float(BLK), g.PS[0:TP, 0, 0:NT], ALU.mult, ALU.add))
        chain(dve, v, dve.tensor_scalar(off[:], off[:], -1.0, None, ALU.add))
        chain(dve, v, dve.tensor_tensor(off[:, 1:NT], off[:, 1:NT], cum[:, 0:NT - 1, EC - 1], ALU.subtract))
        chain(dve, v, dve.tensor_tensor(cum[:], cum[:], off[:, :, None].to_broadcast([TP, NT, EC]), ALU.add))
        chain(dve, v, dve.tensor_tensor(cum[:], cum[:], oh[:], ALU.mult))
        chain(dve, v, dve.tensor_reduce(pos[:], cum[:].rearrange("p b c -> p c b"), AX, ALU.add))
        chain(dve, v, dve.tensor_copy(posi[:], pos[:]))
        chain(dve, v, dve.memset(blkb[:], 0.0))
        for b in range(NT - 1):
            chain(dve, v, dve.scalar_tensor_tensor(blkb[:], blkf[:], cblk[:, b:b + 1], blkb[:], ALU.is_ge, ALU.add))
        v.up(dve.memset(g.blk_tile[:, 0:1], 0))
        chain(dve, v, dve.tensor_copy(g.blk_tile[:, 1:NB + 1], blkb[0:1, :]))
        chain(dve, v, dve.tensor_tensor(vt[:], we[:], att[:, None, :].to_broadcast([TP, 4, D]), ALU.mult))
        chain(dve, v, dve.tensor_reduce(V[:], vt[:].rearrange("p k (h c) -> p (k h) c", h=4), AX, ALU.add))
        for h in range(4):
            chain(dve, v, dve.tensor_scalar(E8[:, :, 2 + h], ea[:, :, 0], V[:, h:h + 1], None, ALU.mult))
            for k in range(1, 4):
                chain(dve, v, dve.scalar_tensor_tensor(E8[:, :, 2 + h], ea[:, :, k], V[:, 4 * k + h:4 * k + h + 1],
                                                       E8[:, :, 2 + h], ALU.mult, ALU.add))
        chain(dve, v, dve.tensor_reduce(am[:], E8[:, :, 2:6].rearrange("p c h -> p h c"), AX, ALU.add))
        wait(pe, v, v.now())
        q.up(pe.matmul(g.PS[0:TP, 2, 0:4], g.ones[0:TP, 0:TP], am[:], start=True, stop=True))
        wait(dve, q, q.now())
        chain(dve, v, dve.tensor_scalar(g.ae_mean[:], g.PS[0:TP, 2, 0:4], 1.0 / E, None, ALU.mult))
        GC = EC // NT
        assert GC * NT == EC
        sc, f, go = s.dma_cnt("scattered"), s.cnt("copied"), s.cnt("go", dve, 4)
        idx = [s.sb(f"idx{u}", [TP, GC], I32) for u in range(2)]
        rec = [s.sb(f"rec{u}", [TP, GC, 8]) for u in range(2)]
        wait(pool, pd, pd.now())
        wait(pe, wd, wd.now())
        ev = s.cnt("ev", dve, 2)

        def consume(k, u, xT, used):
            wait(pe, ev, ev.now() - 1)
            for c in range(KC):
                ins = pe.matmul(g.PS[0:TP, 2 + u, :], xT[:, c, :], Wt[:, c, :], start=(c == 0), stop=(c == KC - 1))
            wait(dve, used, used.up(ins))
            ev.up(dve.tensor_scalar(row(H, k), g.PS[0:TP, 2 + u, :], 1.0, None, ALU.mult))
            wait(dve, go, go.now() - 2)
            f.up(dve.tensor_copy(idx[u][:], posi[:, ds(k * GC, GC)]))
            f.up(dve.tensor_copy(rec[u][:], E8[:, ds(k * GC, GC), :]))
            wait(pool, f, f.now())
            go.up_now(pool)
            for c in range(GC):
                sc.up(pool.indirect_dma_start(out=g.recd, out_offset=bass.IndirectOffsetOnAxis(
                    ap=idx[u][:, c:c + 1], axis=0), in_=rec[u][:, c, :], in_offset=None), 16)
            wait(pool, sc, sc.now())
            go.up_now(pool)

        norm_tiles(nc, g, s, consume, {ev: 2, sc: 32 * GC, f: 4, go: 4})
        wait(sp, pd, pd.now())
        wait(sp, sc, sc.now())
        d.up(sp.dma_start(g.rec[:], g.recd.rearrange("(c p) k -> p c k", p=128)), 16)
        wait(dve, d, d.now())
        v.up(dve.memset(g.srcidx[:, NB * CH:], 0))
        chain(dve, v, dve.tensor_copy(g.srcidx[:, 0:NB * CH], g.rec[:, :, 0]))


def count_matrix(nc, g):
    dve, pe, pool, sp, act = nc.vector, nc.tensor, nc.gpsimd, nc.sync, nc.scalar
    with stage(nc, g) as s:
        NW = N + 2
        C = s.sb("C", [TP, NT, NW])
        Dh = [s.sb(f"Dh{u}", [128, CH, TP], BF16) for u in range(2)]
        Sh = [s.sb(f"Sh{u}", [128, CH, NW], BF16) for u in range(2)]
        zr, dz, p = s.sb("zr", [128 - TP, NT, N]), s.cnt("dz"), s.cnt("p")
        iob = g.iota_tp[:, None, :].to_broadcast([128, CH, TP])
        v = s.cnt("v", dve, 1)
        one, mm, add = s.cnt("onehots"), s.cnt("products"), s.cnt("added", dve, 2)
        kv = s.cnt("dve_steps")
        for u in range(2):
            p.up(pool.memset(Sh[u][:, :, N:NW], 1.0))
        p.up(pool.memset(C[:, 0:4, :], 0.0))
        v.up(dve.memset(C[:, 4:NT, :], 0.0))
        p.up(pool.memset(zr[:], 0.0))
        wait(pe, p, p.now() - 2)
        wait(dve, p, p.now() - 1)
        wait(dve, v, v.now())

        def onehots(j, u):
            kv.up(dve.tensor_tensor(Dh[u][:], iob, g.rec[:, ds(j * CH, CH), 1:2].to_broadcast([128, CH, TP]),
                                    ALU.is_equal))
            for c in range(CH):
                ins = dve.tensor_scalar(Sh[u][:, c, 0:N], g.iota[:],
                                        g.rec[:, ds(j * CH + c, 1), 0:1].rearrange("p a k -> p (a k)"),
                                        None, ALU.is_equal)
                (one if c == CH - 1 else kv).up(ins)

        def products(j, u):
            wait(pe, one, j + 1)
            wait(pe, kv, kv.now())
            wait(pe, add, j + 1)
            for c in range(CH):
                for w, (a, b) in enumerate(((0, 512), (512, 1024), (1024, NW))):
                    ins = pe.matmul(g.PS[0:TP, 3 * u + w, 0:b - a], Dh[u][:, c, :], Sh[u][:, c, a:b],
                                    start=(c == 0), stop=(c == CH - 1))
            mm.up(ins)

        def add_block(j, u):
            b = dve.value_load(g.blk_tile[0:1, ds(j + 1, 1)], min_val=0, max_val=NT - 1)
            wait(dve, mm, j + 1)
            wait(dve, add, j + 2)
            ps = g.PS[0:TP, 3 * u:3 * u + 3, :].rearrange("p w n -> p (w n)")[:, 0:NW]
            add.up(dve.tensor_tensor(row(C, b), ps, row(C, b), ALU.add))

        onehots(0, 0)
        assert NB % 2 == 1
        with loop(nc, NB // 2, {one: 2, mm: 2, add: 2, kv: 2 * CH}) as i:
            for u in range(2):
                j = i * 2 + u
                products(j, u)
                onehots(j + 1, 1 - u)
                add_block(j, u)
        products(NB - 1, 0)
        add_block(NB - 1, 0)
        wait(dve, add, add.now())
        chain(dve, v, dve.tensor_copy(g.deg[:], C[:, :, N]))

        for t in range(NT):
            v.up(dve.tensor_tensor(C[:, t, t * TP:(t + 1) * TP], C[:, t, t * TP:(t + 1) * TP],
                                   g.ident[0:TP, 0:TP], ALU.add))
        wait(sp, p, p.now())
        wait(act, v, v.now())
        dz.up(sp.dma_start(g.CT.rearrange("(k s) d -> s k d", s=128)[TP:128], zr[:]), 16)
        cin = [s.sb(f"cin{u}", [TP, N]) for u in range(2)]
        ct = [s.sb(f"ct{u}", [TP, NT, TP]) for u in range(2)]
        mask = [s.sb(f"mask{u}", [TP, N], BF16) for u in range(2)]
        ci, t, cc, mk = s.cnt("cin_copied", dve, 2), s.cnt("transposed", dve, 2), s.cnt("ct_copied", dve, 2), s.cnt("masks", dve, 2)
        st = [s.cnt(f"stored{u}", sp, 16) for u in range(2)]
        sm = [s.cnt(f"mask_stored{u}", sp, 16) for u in range(2)]
        go = s.cnt("ct_stores_begun")
        with loop(nc, NT // 2, {go: 2, ci: 2, t: 2, cc: 2, mk: 2, st[0]: 16, st[1]: 16, sm[0]: 16, sm[1]: 16}) as i:
            for u in range(2):
                n = i * 2 + u
                wait(act, t, t.ago(u + 1))
                wait(act, mk, mk.ago(u + 1))
                ci.up(act.activation(cin[u][:], row(C, n)[:, 0:N], ACT.Copy))
                wait(pe, ci, ci.now())
                wait(pe, cc, cc.ago(u + 1))
                for k in range(NT):
                    ins = pe.transpose(g.PS[0:TP, 3 * u + k // 4, (k % 4) * 128:(k % 4) * 128 + TP],
                                       cin[u][:, k * TP:(k + 1) * TP], g.ident[0:TP, 0:TP])
                t.up(ins)
                wait(dve, ci, ci.now())
                wait(dve, sm[u], sm[u].ago(16))
                mk.up(dve.tensor_scalar(mask[u][:], cin[u][:], 0.0, NEG, ALU.is_equal, ALU.mult))
                wait(sp, mk, mk.now())
                sm[u].up(sp.dma_start(g.MASK[ds(n * TP, TP), :], mask[u][:]), 16)
                wait(dve, t, t.now())
                wait(dve, st[u], st[u].ago(16))
                for k in range(3):
                    m = min(4, NT - 4 * k)
                    ins = dve.tensor_copy(ct[u][:, 4 * k:4 * k + m, :],
                                          g.PS[0:TP, 3 * u + k, 0:m * 128].rearrange("p (a b) -> p a b", b=128)[:, :, 0:TP])
                cc.up(ins)
                wait(sp, cc, cc.now())
                go.up_now(sp)
                st[u].up(sp.dma_start(g.CT.rearrange("(k s) d -> s k d", s=128)[0:TP, :, ds(n * TP, TP)], ct[u][:]), 16)
        for c in (*st, *sm, dz):
            wait(sp, c, c.now())


def one_ahead(nc, per, load, turn, products):
    load(0, 0)
    turn(0, 0)
    with loop(nc, NT // 2 - 1, per) as i:
        for u in range(2):
            k = i * 2 + u
            load(k + 1, 1 - u)
            products(k, u)
            turn(k + 1, 1 - u)
    load(NT - 1, 1)
    products(NT - 2, 0)
    turn(NT - 1, 1)
    products(NT - 1, 1)


def norm_tiles(nc, g, s, consume, per, XT=None, XN=None, dram=None, loaded=()):
    dve, pe, act, sp = nc.vector, nc.tensor, nc.scalar, nc.sync
    st = s.sb("ln_st", [TP, NT, 6])
    mv = s.sb("ln_mv", [TP, NT, 2])
    rs = s.sb("ln_rs", [TP, NT])
    xn = [s.sb(f"ln_xn{u}", [TP, D]) for u in range(2)]
    xT = [s.sb(f"ln_xT{u}", [128, KC, TP]) for u in range(2)]
    v = s.cnt("ln_v", dve, 1)
    for t in range(NT):
        v.up(dve.bn_stats(st[:, t, :], g.X[:, t, :]))
    wait(dve, v, v.now())
    for t in range(NT):
        v.up(dve.bn_aggr(mv[:, t, :], st[:, t, :]))
    wait(dve, v, v.now())
    chain(dve, v, dve.tensor_scalar(rs[:], mv[:, :, 1], EPS, None, ALU.add))
    wait(act, v, v.now())
    a = s.cnt("ln_a", dve, 2)
    a.up(act.activation(rs[:], rs[:], ACT.Sqrt))
    wait(dve, a, a.now())
    chain(dve, v, dve.reciprocal(rs[:], rs[:]))
    t, w = s.cnt("ln_t", dve, 2), [s.cnt(f"ln_w{u}", sp, 16) for u in range(2)]
    used = s.cnt("ln_used", dve, 2)
    for c in loaded:
        wait(pe, c, c.now())
        wait(dve, c, c.now())
    keep = {v: 2, a: 2, t: 2, used: 2, **per}
    if dram is not None:
        keep.update({w[0]: 16, w[1]: 16})

    def load(k, u):
        wait(dve, t, t.now() - 1)
        if dram is not None:
            wait(dve, w[u], w[u].now())
        if XN is not None:
            wait(dve, a, a.now() - 1)
        v.up(dve.tensor_scalar(xn[u][:], row(g.X, k), mv[:, ds(k, 1), 0:1].rearrange("p a b -> p (a b)"),
                               rs[:, ds(k, 1)], ALU.subtract, ALU.mult))
        if dram is not None:
            wait(sp, v, v.now())
            w[u].up(sp.dma_start(dram[ds(k * TP, TP), :], xn[u][:]), 16)

    def turn(k, u):
        wait(pe, v, v.now())
        wait(pe, a, a.now() - 1)
        for c in range(KC):
            ins = pe.transpose(g.PS[:, u, c * 128:c * 128 + TP], xn[u][:, c * 128:(c + 1) * 128],
                               g.ident[0:TP, 0:TP])
        t.up(ins)
        wait(act, t, t.now())
        wait(act, used, used.now() - 1)
        pt = g.PS[:, u, :].rearrange("p (c n) -> p c n", n=128)[:, :, 0:TP]
        if XN is not None:
            wait(act, v, v.now())
        ins = act.activation(xT[u][:], pt, ACT.Copy)
        if XT is not None:
            ins = act.activation(XT[:, :, ds(k * TP, TP)], pt, ACT.Copy)
        if XN is not None:
            ins = act.activation(row(XN, k), xn[u][:], ACT.Copy)
        a.up(ins)

    def products(k, u):
        wait(pe, a, a.now())
        consume(k, u, xT[u], used)

    one_ahead(nc, keep, load, turn, products)
    if dram is not None:
        for c in w:
            wait(sp, c, c.now())
            wait(nc.gpsimd, c, c.now())


def aggregate(nc, g, s, CT, H, finish):
    dve, pe, sp = nc.vector, nc.tensor, nc.sync
    ct = [s.sb(f"ag_ct{u}", [128, N]) for u in range(2)]
    ld = [s.cnt(f"ag_ld{u}") for u in range(2)]
    rd = s.cnt("ag_rd", dve, 2)
    out = s.cnt("ag_out", dve, 1)
    for half in range(2):
        wait(pe, out, out.now())
        for b in range(5):
            pe.matmul(g.PS[0:TP, b, :], g.zeros[0:1, 0:TP], g.zeros[0:1, :], start=True, stop=True)
        with loop(nc, NT // 2, {ld[0]: 16, ld[1]: 16, rd: 2}) as i:
            for u in range(2):
                k = i * 2 + u
                wait(sp, rd, rd.ago(u + 1))
                ld[u].up(sp.dma_start(ct[u][:], CT[ds(k * 128, 128), :]), 16)
                wait(pe, ld[u], ld[u].now())
                for t in range(NT):
                    ins = pe.matmul(g.PS[0:TP, t // 2, (t % 2) * 256:(t % 2) * 256 + 256],
                                    ct[u][0:TP, t * TP:(t + 1) * TP],
                                    H[:, ds(k, 1), half * 256:half * 256 + 256].rearrange("p a n -> p (a n)"),
                                    start=False, stop=True, skip_group_check=True)
                rd.up(ins)
        wait(dve, rd, rd.now())
        finish(half, g.PS[0:TP, 0:5, :].rearrange("p b (a n) -> p (b a) n", n=256), out)


def gnn0(nc, g, H, b):
    dve, pe, act, sp = nc.vector, nc.tensor, nc.scalar, nc.sync
    with stage(nc, g) as s:
        bb = s.sb("b", [TP, D])
        di = s.sb("dinv", [TP, NT])
        y = s.sb("y", [TP, NT, 256])
        d, v, a = s.cnt("d"), s.cnt("v"), s.cnt("a")
        d.up(sp.dma_start(bb[:], bcast(b, TP)), 16)
        chain(dve, v, dve.tensor_scalar(di[:], g.deg[:], 1.0, None, ALU.add))
        wait(act, v, v.now())
        a.up(act.activation(di[:], di[:], ACT.Sqrt))
        wait(dve, a, a.now())
        chain(dve, v, dve.reciprocal(di[:], di[:]))
        v.up(dve.tensor_tensor(H[:], H[:], di[:, :, None].to_broadcast([TP, NT, D]), ALU.mult))
        wait(pe, v, v.now())
        wait(dve, d, d.now())
        dib = di[:, :, None].to_broadcast([TP, NT, 256])

        def finish(half, ps, out):
            c = slice(half * 256, half * 256 + 256)
            chain(dve, out, dve.tensor_tensor(y[:], ps, dib, ALU.mult))
            chain(dve, v, dve.tensor_tensor(y[:], y[:], bb[:, None, c].to_broadcast([TP, NT, 256]), ALU.add))
            chain(dve, v, dve.scalar_tensor_tensor(g.X[:, :, c], y[:], 0.0, g.X[:, :, c], ALU.max, ALU.add))

        aggregate(nc, g, s, g.CT, H, finish)


def to_experts(nc, g, s, T, WT, ne, v, q):
    wait(nc.tensor, v, v.now())
    for t in range(NT):
        ins = nc.tensor.transpose(g.PS[0:ne, t // 4, (t % 4) * TP:(t % 4 + 1) * TP], T[:, t, :],
                                  g.ident[0:TP, 0:TP])
    wait(nc.vector, q, q.up(ins))
    for k in range(3):
        n = min(4, NT - 4 * k) * TP
        v.up(nc.vector.tensor_copy(WT[:, 4 * k * TP:4 * k * TP + n], g.PS[0:ne, k, 0:n]))
    wait(nc.vector, v, v.now())


def top_slots(nc, g, s, WT, ne, slots, keep, v, q, ahead=1):
    dve, pe = nc.vector, nc.tensor
    parts = -(-slots // 128)
    part = slots // parts
    mx = s.sb("top_value", [ne, 8])
    ix = s.sb("top_index", [ne, 8], U32)
    turn = s.sb("turn", [ne, 1])
    val = s.sb("slot_value", [ne, slots])
    idf = s.sb("slot_token", [ne, slots])
    chain(dve, v, dve.max(mx[:], WT[:]))
    with loop(nc, slots // 8, {v: 6}) as i:
        wait(dve, v, v.now())
        v.up(dve.tensor_copy(val[:, ds(i * 8, 8)], mx[:]))
        v.up(dve.max_index(ix[:], mx[:], WT[:]))
        wait(dve, v, v.now())
        v.up(dve.tensor_copy(idf[:, ds(i * 8, 8)], ix[:]))
        v.up(dve.match_replace(WT[:], mx[:], WT[:], -2.0))
        wait(dve, v, v.now())
        v.up(dve.tensor_copy(turn[:], g.ident[0:ne, 0:1]))
        v.up(dve.max(mx[:], WT[:]))
    chain(dve, v, dve.tensor_scalar(val[:], val[:], 0.0, None, ALU.max))
    if keep < slots:
        chain(dve, v, dve.memset(val[:, keep:slots], 0.0))
    sw = s.sb("slot_w", [part, parts, ne])
    si = s.sb("slot_i", [part, parts, ne + ahead], I32)
    wait(pe, v, v.now())
    for k in range(parts):
        pe.transpose(g.PS[0:part, 0, k * 128:k * 128 + ne], val[:, k * part:(k + 1) * part], g.ident[0:ne, 0:ne])
        ins = pe.transpose(g.PS[0:part, 1, k * 128:k * 128 + ne], idf[:, k * part:(k + 1) * part],
                           g.ident[0:ne, 0:ne])
    wait(dve, q, q.up(ins))
    chain(dve, v, dve.memset(si[:], 0))
    for k in range(parts):
        v.up(dve.tensor_copy(sw[:, k, :], g.PS[0:part, 0, k * 128:k * 128 + ne]))
        v.up(dve.tensor_copy(si[:, k, 0:ne], g.PS[0:part, 1, k * 128:k * 128 + ne]))
    wait(dve, v, v.now())
    return sw, si


def softmax_rows(nc, s, L, ne, v, a):
    dve, act = nc.vector, nc.scalar
    m = s.sb("sm_m", [TP, NT])
    chain(dve, v, dve.tensor_reduce(m[:], L[:], AX, ALU.max))
    chain(dve, v, dve.tensor_tensor(L[:], L[:], m[:, :, None].to_broadcast([TP, NT, ne]), ALU.subtract))
    wait(act, v, v.now())
    a.up(act.activation(L[:], L[:], ACT.Exp))
    wait(dve, a, a.now())
    chain(dve, v, dve.tensor_reduce(m[:], L[:], AX, ALU.add))
    chain(dve, v, dve.reciprocal(m[:], m[:]))
    chain(dve, v, dve.tensor_tensor(L[:], L[:], m[:, :, None].to_broadcast([TP, NT, ne]), ALU.mult))


def logits(nc, g, s, W_ap, b_ap, ne, XT=None, XN=None, dram=None):
    dve, pe, sp = nc.vector, nc.tensor, nc.sync
    Wt, bb, L = s.sb("router_w", [128, KC, ne]), s.sb("router_b", [TP, ne]), s.sb("logits", [TP, NT, ne])
    d = s.cnt("router_d")
    d.up(sp.dma_start(Wt[:], W_ap), 16)
    d.up(sp.dma_start(bb[:], bcast(b_ap, TP)), 16)
    ev = s.cnt("router_ev", dve, 2)

    def consume(k, u, xT, used):
        wait(pe, ev, ev.now() - 1)
        for c in range(KC):
            ins = pe.matmul(g.PS[0:TP, 2 + u, 0:ne], xT[:, c, :], Wt[:, c, :], start=(c == 0), stop=(c == KC - 1))
        wait(dve, used, used.up(ins))
        ev.up(dve.tensor_tensor(row(L, k), g.PS[0:TP, 2 + u, 0:ne], bb[:], ALU.add))

    norm_tiles(nc, g, s, consume, {ev: 2}, XT=XT, XN=XN, dram=dram, loaded=(d,))
    wait(dve, ev, ev.now())
    return L


def ffn0(nc, g, gate_w, gate_b, w1, b1, w2, b2):
    dve, pe, act, sp, pool = nc.vector, nc.tensor, nc.scalar, nc.sync, nc.gpsimd
    NE, HID = w1.shape[0], w1.shape[2]
    CAP = int(1.2 * N / NE)
    SL = -(-CAP // 16) * 16
    HS, Q = SL // 2, HID // 512
    with stage(nc, g) as s:
        v, a, q, d = s.cnt("v"), s.cnt("a"), s.cnt("q"), s.cnt("d")
        W1 = [s.sb(f"w1_{k}", [128, KC, 512]) for k in range(Q)]
        W2 = [s.sb(f"w2_{k}", [128, 4, 512]) for k in range(Q)]
        b2b = s.sb("b2b", [HS, NE, D])
        b1r, b1T = s.sb("b1r", [128, 128]), s.sb("b1T", [128, NE, HID // 128])
        d.up(sp.dma_start(b1r[:], b1.rearrange("e (m p) -> (e m) p", p=128)), 16)
        d.up(sp.dma_start(b2b[:], bcast(b2, HS)), 16)
        L = logits(nc, g, s, gate_w.rearrange("(c p) e -> p c e", p=128), gate_b, NE, dram=g.XND)
        d.up(sp.dma_start(g.Y.rearrange("(t p) d -> p t d", p=TP), g.X[:]), 16)
        wait(pe, d, d.now())
        q.up(pe.transpose(g.PS[:, 7, 0:128], b1r[:], g.ident[:]))
        wait(dve, q, q.now())
        v.up(dve.tensor_copy(b1T[:].rearrange("p e m -> p (e m)"), g.PS[:, 7, 0:128]))
        softmax_rows(nc, s, L, NE, v, a)
        rank = ranks(nc, s, L, NE, v)
        chain(dve, v, dve.tensor_scalar(rank[:], rank[:], 2.0, None, ALU.is_lt))
        chain(dve, v, dve.tensor_tensor(L[:], L[:], rank[:], ALU.mult))
        chain(dve, v, dve.tensor_scalar(rank[:], rank[:], -1.0, None, ALU.add))
        chain(dve, v, dve.tensor_tensor(L[:], L[:], rank[:], ALU.add))
        WT = s.sb("WT", [NE, N])
        to_experts(nc, g, s, L, WT, NE, v, q)
        sw, si = top_slots(nc, g, s, WT, NE, SL, CAP, v, q)

        xg = [s.sb(f"xg{u}", [HS, 2, D]) for u in range(2)]
        xgT = [s.sb(f"xgT{u}", [128, KC, SL]) for u in range(2)]
        hT = [s.sb(f"hT{k}", [128, 4, SL]) for k in range(2)]
        wo = [s.sb(f"wo{u}", [HS, 2, D]) for u in range(2)]
        oT, oc, ot = s.sb("oT", [128, KC, SL]), s.cnt("sums_copied"), s.cnt("sums_transposed")
        gi = [s.sb(f"gi{u}", [HS, 2], I32) for u in range(2)]
        ci = s.sb("ci", [HS, 2], I32)
        ld1 = [s.cnt(f"ld1_{k}") for k in range(Q)]
        ld2 = [s.cnt(f"ld2_{k}") for k in range(Q)]
        mm1, mm2 = s.cnt("mm1", dve, 8 * Q), s.cnt("mm2", dve, 2 * Q)
        gs = [s.dma_cnt(f"gathered{u}") for u in range(2)]
        po = s.cnt("pool_steps", dve, 1)
        tr, tc = s.cnt("transposed", dve, 2), s.cnt("transposed_copied", dve, 2)
        ge = s.cnt("gelu", dve, 8 * Q)
        ev = s.cnt("weighted", dve, 8)
        sc, sd = s.dma_cnt("scattered"), s.cnt("scatter_over", dve, 4)

        def gather(e, u):
            wait(pool, tr, gather_free(u))
            po.up(pool.tensor_copy(gi[u][:], si[:, :, ds(e, 1)].rearrange("p k e -> p (k e)")))
            wait(pool, po, po.now())
            po.up_now(pool)
            for k in range(2):
                gs[u].up(pool.indirect_dma_start(out=xg[u][:, k, :], out_offset=None, in_=g.XND,
                                                 in_offset=bass.IndirectOffsetOnAxis(ap=gi[u][:, k:k + 1], axis=0)), 16)
        wait(pool, v, v.now())
        gather_free = lambda u: 1
        gather(0, 0)
        per = {oc: 2, ot: 2, mm1: 8 * Q, mm2: 2 * Q, gs[0]: 32, gs[1]: 32, po: 6, tr: 2, tc: 2, ge: 8 * Q, ev: 8, sc: 64, sd: 4}
        per.update({c: 32 for c in ld1 + ld2})
        gather_free = lambda u: tr.now() if u == 0 else tr.ago(2)
        with loop(nc, NE // 2, per) as i:
            for u in range(2):
                e = i * 2 + u
                for k in range(Q):
                    wait(sp, mm1, mm1.ago(4 * Q + 4 * k + 4) if u == 0 else mm1.base + 4 * (k + 1))
                    ld1[k].up(sp.dma_start(W1[k][:], w1[ds(e, 1), :, k * 512:(k + 1) * 512].rearrange(
                        "a (c p) n -> p (a c) n", p=128)), 16)
                    wait(sp, mm2, mm2.ago(Q + k + 1) if u == 0 else mm2.base + k + 1)
                    ld2[k].up(sp.dma_start(W2[k][:], w2[ds(e, 1), k * 512:(k + 1) * 512, :].rearrange(
                        "a (m p) n -> p (a m) n", p=128)), 16)
                wait(pe, gs[u], gs[u].now())
                wait(pe, ge, ge.now())
                for c in range(KC):
                    for k in range(2):
                        ins = pe.transpose(g.PS[:, c // 2, (c % 2) * SL + k * HS:(c % 2) * SL + (k + 1) * HS],
                                           xg[u][:, k, c * 128:(c + 1) * 128], g.ident[0:HS, 0:HS])
                tr.up(ins)
                wait(dve, tr, tr.now())
                wait(dve, mm1, mm1.ago(4 * Q * (u + 1)))
                tc.up(dve.tensor_copy(xgT[u][:].rearrange("p (b c) n -> p b (c n)", b=2), g.PS[:, 0:2, 0:2 * SL]))

                def up_proj(k):
                    wait(pe, ld1[k], ld1[k].now())
                    for m in range(4):
                        if k == 0:
                            wait(pe, tc, tc.now())
                        else:
                            wait(pe, ge, ge.now() - 3 + m)
                        for c in range(KC):
                            ins = pe.matmul(g.PS[:, m, 0:SL], W1[k][:, c, m * 128:(m + 1) * 128], xgT[u][:, c, :],
                                            start=(c == 0), stop=(c == KC - 1))
                        mm1.up(ins)

                def gelu(k):
                    wait(act, mm2, mm2_before[k])
                    for m in range(4):
                        wait(act, mm1, mm1.now() - 3 + m)
                        ge.up(act.activation(hT[k % 2][:, m, :], g.PS[:, m, 0:SL], ACT.Gelu,
                                             bias=b1T[:, ds(e, 1), 4 * k + m:4 * k + m + 1].rearrange("p a b -> p (a b)")))

                def down_proj(k, upto):
                    wait(pe, ge, upto)
                    wait(pe, ld2[k], ld2[k].now())
                    for c in range(KC):
                        for m in range(4):
                            ins = pe.matmul(g.PS[:, 4 + 2 * u + c // 2, (c % 2) * SL:(c % 2 + 1) * SL],
                                            W2[k][:, m, c * 128:(c + 1) * 128], hT[k % 2][:, m, :],
                                            start=False, stop=True, skip_group_check=True)
                    mm2.up(ins)

                m2 = mm2.base + u * Q
                mm2_before = [m2 + k - 1 for k in range(Q)]
                wait(pe, ev, ev.ago(4 * u + 4))
                for b in range(2):
                    pe.matmul(g.PS[:, 4 + 2 * u + b, :], g.zeros[0:1, 0:128], g.zeros[0:1, :], start=True, stop=True)
                done = []
                for k in range(Q):
                    up_proj(k)
                    gelu(k)
                    done.append(ge.now())
                    if k:
                        down_proj(k - 1, done[k - 1])
                down_proj(Q - 1, done[Q - 1])
                wait(dve, mm2, mm2.now())
                oc.up(dve.tensor_copy(oT[:].rearrange("p (b c) n -> p b (c n)", b=2),
                                      g.PS[:, 4 + 2 * u:6 + 2 * u, 0:2 * SL]))
                wait(pe, oc, oc.now())
                for h in range(2):
                    for c in range(KC):
                        ins = pe.transpose(g.PS[0:HS, 4 + 2 * u + h, c * 128:(c + 1) * 128],
                                           oT[:, c, h * HS:(h + 1) * HS], g.ident[:])
                ot.up(ins)
                wait(dve, ot, ot.now())
                wait(dve, sd, sd.ago(2 * u + 2))
                for h in range(2):
                    chain(dve, ev, dve.tensor_tensor(wo[u][:, h, :], g.PS[0:HS, 4 + 2 * u + h, :],
                                                     row(b2b, e), ALU.add))
                    ev.up(dve.tensor_scalar(wo[u][:, h, :], wo[u][:, h, :], sw[:, h, ds(e, 1)], None, ALU.mult))
                gather(e + 1, 1 - u)
                po.up(pool.tensor_copy(ci[:], si[:, :, ds(e, 1)].rearrange("p k e -> p (k e)")))
                wait(pool, po, po.now())
                wait(pool, ev, ev.now())
                sd.up_now(pool)
                for h in range(2):
                    sc.up(pool.indirect_dma_start(out=g.Y, out_offset=bass.IndirectOffsetOnAxis(
                        ap=ci[:, h:h + 1], axis=0), in_=wo[u][:, h, :], in_offset=None, compute_op=ALU.add), 16)
                wait(pool, sc, sc.now())
                sd.up_now(pool)
        wait(sp, sc, sc.now())
        wait(sp, gs[0], gs[0].now())
        wait(sp, gs[1], gs[1].now())
        d.up(sp.dma_start(g.X[:], g.Y.rearrange("(t p) d -> p t d", p=TP)), 16)
        wait(sp, d, d.now())


def gnn1(nc, g, W, att_src, att_dst, bias, gamma, beta):
    dve, pe, act, sp, pool = nc.vector, nc.tensor, nc.scalar, nc.sync, nc.gpsimd
    NH, DH = 4, D // 4
    HW = NH * (DH + 1)
    with stage(nc, g) as s:
        v, a, q, d = s.cnt("v", dve, 1), s.cnt("a"), s.cnt("q"), s.cnt("d")
        ACC = s.sb("ACC", [TP, NT, HW])
        M, AD = s.sb("M", [TP, NT, NH]), s.sb("AD", [TP, NT, NH])
        Wt = s.sb("W", [128, KC, D])
        ats, atd = s.sb("ats", [TP, D]), s.sb("atd", [TP, D])
        tb = [s.sb(f"tb{u}", [TP, HW + NH]) for u in range(2)]
        tmp = s.sb("tmp", [TP, 2, D])
        cst = s.sb("cst", [TP, 3, D])
        d.up(sp.dma_start(Wt[:], W.rearrange("(c p) n -> p c n", p=128)), 16)
        for k, w in enumerate((bias, gamma, beta)):
            d.up(sp.dma_start(cst[:, k, :], bcast(w, TP)), 16)
        d.up(sp.dma_start(ats[:], bcast(att_src.rearrange("h c -> (h c)"), TP)), 16)
        d.up(sp.dma_start(atd[:], bcast(att_dst.rearrange("h c -> (h c)"), TP)), 16)
        for u in range(2):
            v.up(dve.memset(tb[u][:], 1.0))
        wait(dve, v, v.now())
        ev = s.cnt("ev", dve, 14)
        tw = [s.cnt(f"table_w{u}", sp, 16) for u in range(2)]

        def consume(k, u, xT, used):
            wait(pe, ev, ev.now() - 7)
            for c in range(KC):
                ins = pe.matmul(g.PS[0:TP, 2 + u, :], xT[:, c, :], Wt[:, c, :], start=(c == 0), stop=(c == KC - 1))
            wait(dve, used, used.up(ins))
            ph = g.PS[0:TP, 2 + u, :]
            head = tb[u][:, 0:HW].rearrange("p (h c) -> p h c", c=DH + 1)
            wait(dve, tw[u], tw[u].now())
            ev.up(dve.tensor_copy(head[:, :, 0:DH], ph.rearrange("p (h c) -> p h c", c=DH)))
            ev.up(dve.tensor_tensor(tmp[:, 0, :], ph, ats[:], ALU.mult))
            chain(dve, ev, dve.tensor_tensor(tmp[:, 1, :], ph, atd[:], ALU.mult))
            sums = tmp[:].rearrange("p k (h c) -> p k h c", c=DH)
            ev.up(dve.tensor_reduce(tb[u][:, HW:HW + NH], sums[:, 0], AX, ALU.add))
            chain(dve, ev, dve.tensor_reduce(row(AD, k), sums[:, 1], AX, ALU.add))
            chain(dve, ev, dve.tensor_scalar(row(ACC, k), tb[u][:, 0:HW], 1.0, None, ALU.mult))
            chain(dve, ev, dve.tensor_tensor(row(M, k), row(AD, k), tb[u][:, HW:HW + NH], ALU.add))
            wait(sp, ev, ev.now())
            tw[u].up(sp.dma_start(g.HT[ds(k * TP, TP), :], tb[u][:]), 16)

        norm_tiles(nc, g, s, consume, {ev: 14, tw[0]: 16, tw[1]: 16}, loaded=(d,))
        wait(dve, ev, ev.now())
        chain(dve, v, dve.tensor_tensor(M[:], M[:], g.ae_mean[:, None, :].to_broadcast([TP, NT, NH]), ALU.add))
        chain(dve, v, dve.scalar_tensor_tensor(M[:], M[:], 0.2, M[:], ALU.mult, ALU.max))
        for c in tw:
            wait(pool, c, c.now())
        sel = selector(nc, g, s, CH * 5, v)
        RING = 3
        gi = [s.sb(f"gi{u}", [128, CH], I32) for u in range(RING)]
        hg = [s.sb(f"hg{u}", [128, CH, HW + NH]) for u in range(RING)]
        Dh = [s.sb(f"Dh{u}", [128, CH, TP]) for u in range(RING)]
        DT = [s.sb(f"DT{u}", [TP, BLK]) for u in range(RING)]
        q5 = [s.sb(f"q5{u}", [128, CH, 5]) for u in range(RING)]
        qm = [s.sb(f"qm{u}", [TP, NH]) for u in range(RING)]
        mb, qT = s.sb("mb", [TP, BLK]), s.sb("qT", [3 * CH * 5, 128], BF16)
        q_parts, q_rest = s.sb("q_parts", [128, 3, CH * 5], BF16), s.sb("q_rest", [128, CH * 5])
        junk = s.sb("junk", [TP, NH, BLK])
        adm, r = s.sb("adm", [TP, 2, NH]), s.sb("r", [TP, NH])
        al, ex = s.sb("al", [128, CH, NH]), s.sb("ex", [128, CH, NH])
        gs, po = [s.dma_cnt(f"gathered{u}") for u in range(RING)], s.cnt("pool_steps")
        kv = s.cnt("dve_steps")
        rows, turned, rowsT, spread, top = [s.cnt(n) for n in ("rows", "turned", "rowsT", "spread", "top")]
        newmax, looked = s.cnt("newmax"), s.cnt("looked")
        alpha, expd, scaled = s.cnt("alpha", dve, 1), s.cnt("expd"), s.cnt("scaled", dve, 1)
        scaled2 = s.cnt("scaled_by_act")
        summed, added = s.cnt("summed"), s.cnt("added")
        events = (rows, turned, rowsT, spread, top, newmax, looked, alpha, expd, scaled, scaled2, summed, added)
        iob = g.iota_tp[:, None, :].to_broadcast([128, CH, TP])
        bank = lambda k: g.PS[0:TP, k, :]

        def of(c, j):
            return j + (1 if c not in (alpha, scaled, summed, added) else 2)

        def gather(j, u):
            po.up(pool.tensor_copy(gi[u][:], g.srcidx[:, ds(j * CH, CH)]))
            wait(pool, po, po.now())
            po.up_now(pool)
            for c in range(CH):
                gs[u].up(pool.indirect_dma_start(out=hg[u][:, c, :], out_offset=None, in_=g.HT,
                                                 in_offset=bass.IndirectOffsetOnAxis(ap=gi[u][:, c:c + 1], axis=0)), 16)

        def slot_terms(j, u):
            rec = g.rec[:, ds(j * CH, CH), :]
            wait(dve, gs[u], gs[u].now())
            kv.up(dve.tensor_tensor(q5[u][:, :, 0:4], hg[u][:, :, HW:HW + NH], rec[:, :, 2:6], ALU.add))
            chain(dve, kv, dve.tensor_copy(q5[u][:, :, 4:5], rec[:, :, 1:2]))
            rows.up(split(dve, kv, q5[u][:].rearrange("p c k -> p (c k)"), [q_parts[:, k, :] for k in range(3)],
                          q_rest[:]))

        def turn(j, u, first=False):
            wait(pe, rows, of(rows, j))
            wait(pe, kv, kv.now())
            if not first:
                wait(pe, top, of(top, j - 1))
            turned.up(pe.matmul(g.PS[0:3 * CH * 5, 0, 0:128], q_parts[:].rearrange("p k n -> p (k n)"), g.identb[:],
                                start=True, stop=True))
            wait(act, turned, of(turned, j))
            if not first:
                wait(act, spread, of(spread, j - 1))
            rowsT.up(act.activation(qT[:], g.PS[0:3 * CH * 5, 0, 0:128], ACT.Copy))

        def spread_rows(j, u):
            wait(pe, rowsT, of(rowsT, j))
            for k in (4, 0, 1, 2, 3):
                for c in range(CH):
                    ins = pe.matmul(bank(k)[:, c * 128:(c + 1) * 128], sel[:, c * 5 + k, :], qT[:], start=True, stop=True)
            spread.up(ins)

        def block_max(j, u):
            rec = g.rec[:, ds(j * CH, CH), :]
            wait(dve, spread, of(spread, j))
            chain(dve, kv, dve.tensor_scalar(DT[u][:], bank(4), g.pcol[0:TP, :], None, ALU.is_equal))
            chain(dve, kv, dve.tensor_scalar(mb[:], DT[u][:], 1.0, -NEG, ALU.subtract, ALU.mult))
            kv.up(dve.tensor_tensor(Dh[u][:], iob, rec[:, :, 1:2].to_broadcast([128, CH, TP]), ALU.is_equal))
            for h in range(NH):
                ins = dve.tensor_tensor_reduce(junk[:, h, :], mb[:], bank(h), 1.0, NEG, ALU.add, ALU.max, qm[u][:, h:h + 1])
                (top if h == NH - 1 else kv).up(ins)

        def new_max(j, u, b):
            wait(dve, top, of(top, j))
            wait(dve, kv, kv.now())
            chain(dve, kv, dve.tensor_tensor(qm[u][:], qm[u][:], row(AD, b), ALU.add))
            chain(dve, kv, dve.scalar_tensor_tensor(qm[u][:], qm[u][:], 0.2, qm[u][:], ALU.mult, ALU.max))
            kv.up(dve.tensor_scalar(adm[:, 0, :], row(AD, b), 0.0, None, ALU.add))
            chain(dve, kv, dve.tensor_tensor(adm[:, 1, :], qm[u][:], row(M, b), ALU.max))
            chain(dve, kv, dve.tensor_tensor(r[:], row(M, b), adm[:, 1, :], ALU.subtract))
            newmax.up(dve.tensor_scalar(row(M, b), adm[:, 1, :], 0.0, None, ALU.add))

        def look_up(j, u):
            wait(pe, newmax, of(newmax, j))
            wait(pe, alpha, of(alpha, j - 1))
            for c in range(CH):
                ins = pe.matmul(g.PS[:, 5, c * 8:c * 8 + 8], DT[u][:, c * 128:(c + 1) * 128],
                                adm[:].rearrange("p k h -> p (k h)"), start=True, stop=True)
            looked.up(ins)
            wait(dve, looked, of(looked, j))
            look = g.PS[:, 5, 0:CH * 8].rearrange("p (c k h) -> p c k h", c=CH, k=2)
            chain(dve, kv, dve.tensor_tensor(al[:], q5[u][:, :, 0:4], look[:, :, 0, :], ALU.add))
            chain(dve, kv, dve.scalar_tensor_tensor(al[:], al[:], 0.2, al[:], ALU.mult, ALU.max))
            chain(dve, kv, dve.tensor_tensor(al[:], al[:], look[:, :, 1, :], ALU.subtract))
            alpha.up(dve.tensor_scalar(al[:], al[:], 0.0, None, ALU.min))
            wait(act, alpha, of(alpha, j))
            wait(act, scaled, of(scaled, j - 1))
            act.activation(r[:], r[:], ACT.Exp)
            expd.up(act.activation(ex[:], al[:], ACT.Exp))

        def add_sums(j, b):
            wait(dve, summed, of(summed, j))
            acc2 = ACC[:, ds(b, 1), :].rearrange("p a (w c) -> p (a w) c", w=2)
            added.up(dve.tensor_tensor(acc2, acc2, g.PS[0:TP, 6:8, 0:HW // 2], ALU.add))

        def scale_rows(j, u, b):
            wait(dve, expd, of(expd, j))
            hrow = lambda c: hg[u][:, c, 0:HW].rearrange("p (h c) -> p h c", c=DH + 1)
            for c in range(2):
                ins = dve.tensor_tensor(hrow(c), hrow(c), ex[:, c, :, None].to_broadcast([128, NH, DH + 1]), ALU.mult)
                (scaled if c == 1 else kv).up(ins)
            wait(act, expd, of(expd, j))
            for c in range(2, CH):
                for h in range(NH):
                    ins = act.activation(hrow(c)[:, h, :], hrow(c)[:, h, :], ACT.Copy, scale=ex[:, c, h:h + 1])
            scaled2.up(ins)
            acc = ACC[:, ds(b, 1), :].rearrange("p a (h c) -> p (a h) c", c=DH + 1)
            wait(dve, added, of(added, j - 1))
            chain(dve, kv, dve.tensor_tensor(acc, acc, r[:, :, None].to_broadcast([TP, NH, DH + 1]), ALU.mult))

        def sum_rows(j, u):
            wait(pe, scaled, of(scaled, j))
            wait(pe, scaled2, of(scaled2, j))
            wait(pe, added, of(added, j - 1))
            for c in range(CH):
                for w in range(2):
                    ins = pe.matmul(bank(6 + w)[:, 0:HW // 2], Dh[u][:, c, :], hg[u][:, c, w * (HW // 2):(w + 1) * (HW // 2)],
                                    start=(c == 0), stop=(c == CH - 1))
            summed.up(ins)

        def tile_of(j):
            return dve.value_load(g.blk_tile[0:1, ds(j + 1, 1)], min_val=0, max_val=NT - 1)

        for k in (6, 7):
            ins = pe.matmul(bank(k), g.zeros[0:1, 0:TP], g.zeros[0:1, :], start=True, stop=True)
        summed.up(ins)
        wait(pe, v, v.now())
        gather(0, 0)
        slot_terms(0, 0)
        turn(0, 0, first=True)
        spread_rows(0, 0)
        block_max(0, 0)
        gather(1, 1)
        kvn = 22
        per = {c: RING for c in events}
        per.update({c: 64 for c in gs})
        per.update({po: 2 * RING, kv: RING * kvn})
        assert NB % RING == 1
        with loop(nc, NB // RING, per) as i:
            for u in range(RING):
                j, u1, u2 = i * RING + u, (u + 1) % RING, (u + 2) % RING
                b_last, b = tile_of(j - 1), tile_of(j)
                wait(pool, summed, of(summed, j - 1))
                gather(j + 2, u2)
                new_max(j, u, b)
                slot_terms(j + 1, u1)
                turn(j + 1, u1)
                look_up(j, u)
                spread_rows(j + 1, u1)
                add_sums(j - 1, b_last)
                scale_rows(j, u, b)
                block_max(j + 1, u1)
                sum_rows(j, u)
        j = NB - 1
        b_last, b = tile_of(j - 1), tile_of(j)
        new_max(j, 0, b)
        look_up(j, 0)
        add_sums(j - 1, b_last)
        scale_rows(j, 0, b)
        sum_rows(j, 0)
        add_sums(j, b)
        wait(dve, added, added.now())
        for c in gs:
            wait(pool, c, c.now())

        O = s.sb("O", [TP, NT, D])
        sq = s.sb("sq", [TP, NT, D])
        mu, shift, rstd = s.sb("mu", [TP, D]), s.sb("shift", [TP, D]), s.sb("rstd", [TP, D])
        den = s.sb("den", [TP, NT * NH])
        pb = s.cnt("beta_added")
        wait(pool, d, d.now())
        pb.up(pool.tensor_tensor(g.X[:], g.X[:], cst[:, 2:3, :].to_broadcast([TP, NT, D]), ALU.add))
        acc = ACC[:].rearrange("p t (h c) -> p (t h) c", c=DH + 1)
        full = [TP, NT, D]
        chain(dve, v, dve.tensor_scalar(den[:], acc[:, :, DH], 1e-16, None, ALU.add))
        chain(dve, v, dve.reciprocal(den[:], den[:]))
        for t in range(NT):
            h4 = slice(t * NH, (t + 1) * NH)
            wait(pe, v, v.up(dve.tensor_tensor(
                O[:, t, :].rearrange("p (h c) -> p h c", c=DH), acc[:, h4, 0:DH],
                den[:, h4, None].to_broadcast([TP, NH, DH]), ALU.mult)))
            ins = pe.matmul(bank(0), g.ones[0:TP, 0:TP], O[:, t, :], start=(t == 0), stop=(t == NT - 1))
        wait(dve, q, q.up(ins))
        wait(dve, v, v.now())
        chain(dve, v, dve.scalar_tensor_tensor(mu[:], bank(0), 1.0 / N, cst[:, 0, :], ALU.mult, ALU.add))
        chain(dve, v, dve.tensor_tensor(shift[:], cst[:, 0, :], mu[:], ALU.subtract))
        for t in range(NT):
            wait(act, v, v.up(dve.tensor_tensor(O[:, t, :], O[:, t, :], shift[:], ALU.add)))
            wait(pe, a, a.up(act.activation(sq[:, t, :], O[:, t, :], ACT.Square)))
            ins = pe.matmul(bank(1), g.ones[0:TP, 0:TP], sq[:, t, :], start=(t == 0), stop=(t == NT - 1))
        wait(dve, q, q.up(ins))
        chain(dve, v, dve.tensor_scalar(rstd[:], bank(1), 1.0 / N, EPS, ALU.mult, ALU.add))
        wait(act, v, v.now())
        a.up(act.activation(rstd[:], rstd[:], ACT.Sqrt))
        wait(dve, a, a.now())
        chain(dve, v, dve.reciprocal(rstd[:], rstd[:]))
        chain(dve, v, dve.tensor_tensor(rstd[:], rstd[:], cst[:, 1, :], ALU.mult))
        chain(dve, v, dve.tensor_tensor(O[:], O[:], rstd[:, None, :].to_broadcast(full), ALU.mult))
        wait(dve, pb, pb.now())
        chain(dve, v, dve.tensor_tensor(g.X[:], g.X[:], O[:], ALU.add))


PIECES = ((0, 417), (417, 834), (834, N))


def ranks(nc, s, L, ne, v):
    dve = nc.vector
    big = [TP, NT, ne, ne]
    cmp = s.sb("cmp", big)
    low = s.sb("low", [TP, ne, ne])
    rank, rank2 = s.sb("rank", [TP, NT, ne]), s.sb("rank2", [TP, NT, ne])
    chain(dve, v, dve.memset(low[:], 1.0))
    for e in range(ne):
        v.up(dve.memset(low[:, e, e:ne], 0.0))
    other, own = L[:, :, None, :].to_broadcast(big), L[:, :, :, None].to_broadcast(big)
    chain(dve, v, dve.tensor_tensor(cmp[:], other, own, ALU.is_gt))
    chain(dve, v, dve.tensor_reduce(rank[:], cmp[:], AX, ALU.add))
    chain(dve, v, dve.tensor_tensor(cmp[:], other, own, ALU.is_equal))
    chain(dve, v, dve.tensor_tensor(cmp[:], cmp[:], low[:, None, :, :].to_broadcast(big), ALU.mult))
    chain(dve, v, dve.tensor_reduce(rank2[:], cmp[:], AX, ALU.add))
    chain(dve, v, dve.tensor_tensor(rank[:], rank[:], rank2[:], ALU.add))
    return rank


def ffn1(nc, g, Wr, br, W1, b1, W2, b2):
    dve, pe, act, sp, pool = nc.vector, nc.tensor, nc.scalar, nc.sync, nc.gpsimd
    NE, F = W1.shape[0], W1.shape[2]
    FC = F // 128
    with stage(nc, g) as s:
        v, a, q, d = s.cnt("v"), s.cnt("a"), s.cnt("q"), s.cnt("d")
        XT = s.sb("XT", [128, KC, N])
        b1r, b1T = s.sb("b1r", [NE * FC, 128]), s.sb("b1T", [128, NE, FC])
        b2r = s.sb("b2r", [NE, D])
        w1 = [s.sb(f"w1_{u}", [128, KC, F]) for u in range(2)]
        w2 = [s.sb(f"w2_{u}", [128, FC, D]) for u in range(2)]
        hT = [s.sb(f"hT_{u}", [128, FC, N]) for u in range(2)]
        d.up(sp.dma_start(b1r[:], b1.rearrange("e (m p) -> (e m) p", p=128)), 16)
        d.up(sp.dma_start(b2r[:], b2), 16)
        L = logits(nc, g, s, Wr.rearrange("(c p) e -> p c e", p=128), br, NE, XT=XT)
        wait(pe, d, d.now())
        q.up(pe.transpose(g.PS[:, 7, 0:NE * FC], b1r[:], g.ident[0:NE * FC, 0:NE * FC]))
        wait(dve, q, q.now())
        v.up(dve.tensor_copy(b1T[:].rearrange("p e m -> p (e m)"), g.PS[:, 7, 0:NE * FC]))
        rank = ranks(nc, s, L, NE, v)
        top, gate = s.sb("top", [TP, NT]), s.sb("gate", [TP, NT])
        chain(dve, v, dve.tensor_reduce(top[:], L[:], AX, ALU.max))
        chain(dve, v, dve.tensor_tensor(top[:], top[:], top[:], ALU.subtract))
        wait(act, v, v.now())
        a.up(act.activation(top[:], top[:], ACT.Exp))
        wait(dve, a, a.now())
        chain(dve, v, dve.reciprocal(gate[:], top[:]))
        chain(dve, v, dve.tensor_tensor(gate[:], gate[:], top[:], ALU.mult))
        mask = s.sb("mask", [TP, NT, NE])
        chain(dve, v, dve.tensor_scalar(rank[:], rank[:], 1.0, None, ALU.is_lt))
        chain(dve, v, dve.tensor_tensor(mask[:], rank[:], gate[:, :, None].to_broadcast([TP, NT, NE]), ALU.mult))
        mT = s.sb("mT", [NE, N])
        to_experts(nc, g, s, mask, mT, NE, v, q)
        wait(pe, v, v.now())
        for t in range(NT):
            if t >= 2:
                wait(pe, v, v.now() - 1)
            q.up(pe.matmul(g.PS[0:TP, 6 + t % 2, :], mT[:, t * TP:(t + 1) * TP], b2r[:], start=True, stop=True))
            wait(dve, q, q.now())
            v.up(dve.tensor_tensor(g.X[:, t, :], g.X[:, t, :], g.PS[0:TP, 6 + t % 2, :], ALU.add))
        wait(dve, v, v.now())
        wait(pool, v, v.now())
        ld = [s.cnt(f"ld{u}") for u in range(2)]
        up, rl = s.cnt("up", dve, 12), s.cnt("relu", dve, 12)
        bc, bcol = s.cnt("bias_columns"), [s.sb(f"bcol{u}", [128, FC]) for u in range(2)]
        dn, ad = s.cnt("down", dve, 2 * NT), s.cnt("added", dve, 2 * NT)
        with loop(nc, NE // 2, {bc: 2, ld[0]: 32, ld[1]: 32, up: 12, rl: 12, dn: 2 * NT, ad: 2 * NT}) as i:
            for u in range(2):
                e = i * 2 + u
                wait(sp, dn, dn.ago(NT * (u + 1)))
                ld[u].up(sp.dma_start(w1[u][:], W1[ds(e, 1)].rearrange("a (c p) n -> p (a c) n", p=128)), 16)
                ld[u].up(sp.dma_start(w2[u][:], W2[ds(e, 1)].rearrange("a (c p) n -> p (a c) n", p=128)), 16)
                wait(pool, rl, rl.ago(6 * (u + 1)))
                bc.up(pool.tensor_copy(bcol[u][:], b1T[:, ds(e, 1), :].rearrange("p a m -> p (a m)")))
                wait(act, bc, bc.now())
                wait(pe, ld[u], ld[u].now())
                wait(act, dn, dn.ago(NT * (u + 1)))
                first = rl.now()
                for f in range(FC):
                    for k, (x0, x1) in enumerate(PIECES):
                        bk = 3 * f + k
                        wait(pe, rl, first - 5 + bk)
                        for c in range(KC):
                            ins = pe.matmul(g.PS[:, bk, 0:x1 - x0], w1[u][:, c, f * 128:(f + 1) * 128],
                                            XT[:, c, x0:x1], start=(c == 0), stop=(c == KC - 1))
                        up.up(ins)
                        wait(act, up, up.now())
                        rl.up(act.activation(hT[u][:, f, x0:x1], g.PS[:, bk, 0:x1 - x0], ACT.Relu,
                                             bias=bcol[u][:, f:f + 1]))
                wait(pe, rl, rl.now())
                for t in range(NT):
                    wait(pe, ad, ad.now() - 1)
                    for f in range(FC):
                        ins = pe.matmul(g.PS[0:TP, 6 + t % 2, :], hT[u][:, f, t * TP:(t + 1) * TP], w2[u][:, f, :],
                                        start=(f == 0), stop=(f == FC - 1))
                    dn.up(ins)
                    wait(dve, dn, dn.now())
                    ad.up(dve.scalar_tensor_tensor(g.X[:, t, :], g.PS[0:TP, 6 + t % 2, :],
                                                   mask[:, t, ds(e, 1)], g.X[:, t, :], ALU.mult, ALU.add))
                wait(dve, ad, ad.now())


def head_sums(nc, g, s, ev, ps, att_s, att_d, tmp, AS, AD, k):
    dve = nc.vector
    nh, w = AS.shape[2], tmp.shape[2]
    ev.up(dve.tensor_tensor(tmp[:, 0, :], ps, att_s[:], ALU.mult))
    chain(dve, ev, dve.tensor_tensor(tmp[:, 1, :], ps, att_d[:], ALU.mult))
    v4 = tmp[:].rearrange("p k (h c) -> p k h c", h=nh)
    ev.up(dve.tensor_reduce(row(AS, k), v4[:, 0], AX, ALU.add))
    ev.up(dve.tensor_reduce(row(AD, k), v4[:, 1], AX, ALU.add))


def to_rows(nc, g, s, T, R, n, v, q):
    dve, pe = nc.vector, nc.tensor
    parts, rest = s.sb(f"row_parts_{n}", [TP, NT, 3 * n], BF16), s.sb(f"row_rest_{n}", [TP, NT, n])
    v.up(split(dve, v, T[:], [parts[:, :, k * n:(k + 1) * n] for k in range(3)], rest[:]))
    wait(pe, v, v.now())
    for t in range(NT):
        ins = pe.matmul(g.PS[0:3 * n, 5 + t // 4, (t % 4) * TP:(t % 4 + 1) * TP], parts[:, t, :],
                        g.identb[0:TP, 0:TP], start=True, stop=True)
    wait(dve, q, q.up(ins))
    for k in range(3):
        m = min(4, NT - 4 * k) * TP
        v.up(dve.tensor_copy(R[:, 4 * k * TP:4 * k * TP + m], g.PS[0:3 * n, 5 + k, 0:m]))
    wait(dve, v, v.now())


def attention(nc, g, HH, OUT, AS, AD, MKF, mask):
    dve, pe, act, sp, pool = nc.vector, nc.tensor, nc.scalar, nc.sync, nc.gpsimd
    NH, W = 4, HH.shape[2]
    DH = W // NH
    with stage(nc, g) as s:
        v, a, q, d = s.cnt("v"), s.cnt("a"), s.cnt("q"), s.cnt("d")
        MK = MKF[0:TP, :, :].rearrange("p a n -> p (a n)").bitcast(BF16).rearrange("p (t n) -> p t n", t=NT)
        R, R8 = s.sb("R", [3 * NH, N], BF16), s.sb("R8", [6 * NH, N], BF16)
        MX, AB = s.sb("MX", [TP, NT, NH]), s.sb("AB", [TP, NT, 2 * NH])
        junk = s.sb("junk", [TP, N], BF16)
        AS2 = s.sb("AS2", [TP, NT, NH])
        sel4, sel8 = selector(nc, g, s, NH, v), selector(nc, g, s, 2 * NH, v)
        v.up(dve.tensor_scalar(AS2[:], AS[:], 0.2, None, ALU.mult))
        to_rows(nc, g, s, AS, R, NH, v, q)
        wait(pe, v, v.now())
        wait(dve, mask, mask.now())
        for h in range(NH):
            if h:
                wait(pe, v, v.now())
            for k in range(3):
                x0, x1 = 512 * k, min(512 * (k + 1), N)
                ins = pe.matmul(g.PS[0:TP, k, 0:x1 - x0], sel4[:, h, :], R[:, x0:x1], start=True, stop=True)
            wait(dve, q, q.up(ins))
            bc = g.PS[0:TP, 0:3, :].rearrange("p b n -> p (b n)")[:, 0:N]
            for t in range(NT):
                chain(dve, v, dve.tensor_tensor_reduce(junk[:], MK[:, t, :], bc, 1.0, NEG, ALU.add, ALU.max,
                                                       MX[:, t, h:h + 1]))
        chain(dve, v, dve.tensor_tensor(MX[:], MX[:], AD[:], ALU.add))
        chain(dve, v, dve.scalar_tensor_tensor(MX[:], MX[:], 0.2, MX[:], ALU.mult, ALU.max))
        v.up(dve.tensor_tensor(AB[:, :, 0:NH], AD[:], MX[:], ALU.subtract))
        chain(dve, v, dve.scalar_tensor_tensor(AB[:, :, NH:2 * NH], AD[:], 0.2, MX[:], ALU.mult, ALU.subtract))
        to_rows(nc, g, s, AB, R8, 2 * NH, v, q)
        RA, RB = s.sb("RA", [TP, N]), s.sb("RB", [TP, N])
        ct, P = [MKF[:, u, :] for u in range(2)], [MKF[0:TP, 2 + u, :] for u in range(2)]
        z1 = [s.sb(f"z1{u}", [TP, N]) for u in range(2)]
        z2 = [s.sb(f"z2{u}", [TP, N]) for u in range(2)]
        den, psum = s.sb("den", [TP, NT]), s.sb("weight_sums", [TP, N])
        ld = [s.cnt(f"ld{u}") for u in range(2)]
        lin, mx, ex, pm = s.cnt("lin"), s.cnt("mx", dve, 2), s.cnt("ex"), s.cnt("pm", dve, 2)
        mm, sm = s.cnt("mm", dve, 2), s.cnt("summed", dve, 2)
        spread, rb, cl = s.cnt("spread"), s.cnt("RB_copied"), s.cnt("cleared")
        rows = g.PS[0:TP, 5:8, :].rearrange("p b n -> p (b n)")[:, 0:N]

        def spread_row(j):
            for w in range(3):
                x0, x1 = 512 * w, min(512 * (w + 1), N)
                ins = pe.matmul(g.PS[0:TP, 5 + w, 0:x1 - x0], sel8[:, j, :], R8[:, x0:x1], start=True, stop=True)
            spread.up(ins)

        def start_head(h):
            wait(pe, v, v.now())
            spread_row(NH + h)
            wait(act, spread, spread.now())
            rb.up(act.activation(RB[:], rows, ACT.Copy))
            wait(pe, rb, rb.now())
            spread_row(h)
            cl.up(pool.memset(psum[:], 0.0))
            cl.up(pool.memset(P[1], 0.0))

        for e in (pool, sp):
            wait(e, v, v.now())
        start_head(0)
        for h in range(NH):
            wait(dve, spread, spread.now())
            chain(dve, v, dve.tensor_copy(RA[:], rows))
            wait(act, rb, rb.now())
            wait(dve, cl, cl.now())
            wait(pe, v, v.now())
            for k in range(5):
                pe.matmul(g.PS[0:TP, k, :], g.zeros[0:1, 0:TP], g.zeros[0:1, :], start=True, stop=True)
            with loop(nc, NT // 2, {ld[0]: 16, ld[1]: 16, lin: 2, mx: 2, ex: 2, pm: 2, mm: 2, sm: 2}) as i:
                for u in range(2):
                    k = i * 2 + u
                    wait(sp, pm, pm.ago(u + 1))
                    ld[u].up(sp.dma_start(ct[u], g.CT[ds(k * 128, 128), :]), 16)
                    wait(act, mx, mx.ago(u + 1))
                    lin.up(act.activation(z1[u][:], RB[:], ACT.Identity,
                                          bias=AS2[:, ds(k, 1), h:h + 1].rearrange("p a b -> p (a b)")))
                    wait(dve, lin, lin.now())
                    wait(dve, pm, pm.ago(u + 1))
                    mx.up(dve.scalar_tensor_tensor(z2[u][:], RA[:], AS[:, ds(k, 1), h:h + 1].rearrange("p a b -> p (a b)"),
                                                   z1[u][:], ALU.add, ALU.max))
                    wait(dve, pm, pm.now())
                    wait(dve, sm, sm.now())
                    added = sm.now()
                    sm.up(dve.tensor_tensor(psum[:], psum[:], P[1 - u], ALU.add))
                    wait(act, mx, mx.now())
                    ex.up(act.activation(z2[u][:], z2[u][:], ACT.Exp))
                    wait(pool, ex, ex.now())
                    wait(pool, ld[u], ld[u].now())
                    wait(pool, mm, mm.ago(u + 1))
                    wait(pool, sm, added)
                    pm.up(pool.tensor_tensor(P[u], z2[u][:], ct[u][0:TP], ALU.mult))
                    wait(pe, pm, pm.now())
                    for t in range(NT):
                        ins = pe.matmul(g.PS[0:TP, t // 2, (t % 2) * 256:(t % 2) * 256 + 256], P[u][:, t * TP:(t + 1) * TP],
                                  HH[:, ds(k, 1), h * DH:(h + 1) * DH].rearrange("p a n -> p (a n)"),
                                  start=False, stop=True, skip_group_check=True)
                    mm.up(ins)
            wait(dve, pm, pm.now())
            wait(dve, sm, sm.now())
            sm.up(dve.tensor_tensor(psum[:], psum[:], P[1], ALU.add))
            wait(pe, sm, sm.now())
            pe.matmul(g.PS[0:TP, 5, :], g.zeros[0:1, 0:TP], g.zeros[0:1, :], start=True, stop=True)
            for t in range(NT):
                ins = pe.matmul(g.PS[0:TP, 5, t:t + 1], psum[:, t * TP:(t + 1) * TP], g.ones[0:TP, 0:1],
                                start=False, stop=True, skip_group_check=True)
            wait(dve, mm, mm.now())
            wait(dve, q, q.up(ins))
            chain(dve, v, dve.tensor_scalar(den[:], g.PS[0:TP, 5, 0:NT], 1e-16, None, ALU.add))
            if h + 1 < NH:
                wait(pool, q, q.now())
                wait(pool, mm, mm.now())
                start_head(h + 1)
            chain(dve, v, dve.reciprocal(den[:], den[:]))
            o = OUT[:, :, h * DH:(h + 1) * DH]
            full = [TP, NT, DH]
            chain(dve, v, dve.tensor_tensor(o, g.PS[0:TP, 0:5, :].rearrange("p b (a n) -> p (b a) n", n=256),
                                            den[:, :, None].to_broadcast(full), ALU.mult))


def tiles_linear(nc, g, s, IN, b, take, per):
    dve, pe, act = nc.vector, nc.tensor, nc.scalar
    C8 = IN.shape[2] // 128
    xi = [s.sb(f"xi{u}", [TP, IN.shape[2]]) for u in range(2)]
    xT = [s.sb(f"xT{u}", [128, C8, TP]) for u in range(2)]
    bb, bd = s.sb("bb", [TP, IN.shape[2]]), s.cnt("bias")
    bd.up(nc.scalar.dma_start(bb[:], bcast(b, TP)), 16)
    wait(nc.gpsimd, bd, bd.now())
    ci, t, a, mm = s.cnt("tl_ci", dve, 2), s.cnt("tl_t", dve, 2), s.cnt("tl_a", dve, 2), s.cnt("tl_mm", dve, 2)

    def load(k, u):
        wait(nc.gpsimd, t, t.now() - 1)
        ci.up(nc.gpsimd.tensor_tensor(xi[u][:], row(IN, k), bb[:], ALU.add))

    def turn(k, u):
        wait(pe, ci, ci.now())
        wait(pe, a, a.now() - 1)
        for c in range(C8):
            ins = pe.transpose(g.PS[:, 6 * u + c // 4, (c % 4) * 128:(c % 4) * 128 + TP],
                               xi[u][:, c * 128:(c + 1) * 128], g.ident[0:TP, 0:TP])
        t.up(ins)
        wait(act, t, t.now())
        wait(act, mm, mm.now() - 1)
        a.up(act.activation(xT[u][:].rearrange("p (b c) n -> p b c n", b=2),
                            g.PS[:, 6 * u:6 * u + 2, :].rearrange("p b (c n) -> p b c n", n=128)[:, :, :, 0:TP],
                            ACT.Relu))

    def products(k, u):
        wait(pe, a, a.now())
        take(k, u, xT[u], mm)

    one_ahead(nc, {ci: 2, t: 2, a: 2, mm: 2, **per}, load, turn, products)


def gnn2(nc, g, W1, as1, ad1, b1, W2, as2, ad2, b2, fcW, fcb):
    dve, pe, act, sp, pool = nc.vector, nc.tensor, nc.scalar, nc.sync, nc.gpsimd
    WD = W1.shape[1]
    NH = 4
    flat = lambda ap: ap.rearrange("h c -> (h c)")
    with stage(nc, g) as o:
        HH, OUT = o.sb("HH", [TP, NT, WD]), o.sb("OUT", [TP, NT, WD])
        AS, AD = o.sb("AS", [TP, NT, NH]), o.sb("AD", [TP, NT, NH])
        MKF, mask = o.sb("MK", [128, 5, N]), o.cnt("mask_loaded")

        def parts(s, W, att_s, att_d):
            kc = W.shape[0] // 128
            Wt, sa, sd = s.sb("W", [128, kc, WD]), s.sb("att_s", [TP, WD]), s.sb("att_d", [TP, WD])
            tmp = s.sb("tmp", [TP, 2, WD])
            d = s.cnt("d")
            d.up(sp.dma_start(Wt[:], W.rearrange("(c p) n -> p c n", p=128)), 16)
            d.up(sp.dma_start(sa[:], bcast(flat(att_s), TP)), 16)
            d.up(sp.dma_start(sd[:], bcast(flat(att_d), TP)), 16)
            mask.up(sp.dma_start(MKF[0:TP, :, :].rearrange("p a n -> p (a n)").bitcast(BF16).rearrange(
                "p (t n) -> p t n", t=NT), g.MASK.rearrange("(t p) n -> p t n", p=TP)), 16)
            ev = s.cnt("ev", dve, 10)

            def take(k, u, xT, used):
                wait(pe, ev, ev.now() - 5)
                for w in range(2):
                    for c in range(kc):
                        ins = pe.matmul(g.PS[0:TP, 2 + 2 * u + w, :], xT[:, c, :], Wt[:, c, w * 512:(w + 1) * 512],
                                        start=(c == 0), stop=(c == kc - 1))
                wait(dve, used, used.up(ins))
                ps = g.PS[0:TP, 2 + 2 * u:4 + 2 * u, :].rearrange("p b n -> p (b n)")
                ev.up(dve.tensor_scalar(row(HH, k), ps, 1.0, None, ALU.mult))
                wait(dve, ev, ev.now())
                head_sums(nc, g, s, ev, ps, sa, sd, tmp, AS, AD, k)
                wait(dve, ev, ev.now())
            return take, {ev: 10}, d

        with stage(nc, g) as s:
            take, per, d = parts(s, W1, as1, ad1)
            norm_tiles(nc, g, s, take, per, loaded=(d,))
        attention(nc, g, HH, OUT, AS, AD, MKF, mask)
        with stage(nc, g) as s:
            take, per, d = parts(s, W2, as2, ad2)
            wait(pe, d, d.now())
            wait(dve, d, d.now())
            tiles_linear(nc, g, s, OUT, b1, take, per)
        attention(nc, g, HH, OUT, AS, AD, MKF, mask)
        with stage(nc, g) as s:
            Wt, fb = s.sb("fcW", [128, WD // 128, D]), s.sb("fcb", [TP, D])
            d = s.cnt("d")
            d.up(sp.dma_start(Wt[:], fcW.rearrange("(c p) n -> p c n", p=128)), 16)
            d.up(sp.dma_start(fb[:], bcast(fcb, TP)), 16)
            wait(pe, d, d.now())
            wait(dve, d, d.now())
            ev = s.cnt("ev", dve, 4)

            def take(k, u, xT, used):
                wait(pe, ev, ev.now() - 2)
                for c in range(WD // 128):
                    ins = pe.matmul(g.PS[0:TP, 2 + u, :], xT[:, c, :], Wt[:, c, :], start=(c == 0),
                                    stop=(c == WD // 128 - 1))
                wait(dve, used, used.up(ins))
                chain(dve, ev, dve.tensor_tensor(row(g.X, k), row(g.X, k), g.PS[0:TP, 2 + u, :], ALU.add))
                chain(dve, ev, dve.tensor_tensor(row(g.X, k), row(g.X, k), fb[:], ALU.add))

            tiles_linear(nc, g, s, OUT, b2, take, {ev: 4})


def norm_all(nc, s, T, v, a):
    dve, act = nc.vector, nc.scalar
    st, mv, rs = s.sb("na_st", [TP, NT, 6]), s.sb("na_mv", [TP, NT, 2]), s.sb("na_rs", [TP, NT])
    for t in range(NT):
        v.up(dve.bn_stats(st[:, t, :], T[:, t, :]))
    wait(dve, v, v.now())
    for t in range(NT):
        v.up(dve.bn_aggr(mv[:, t, :], st[:, t, :]))
    wait(dve, v, v.now())
    chain(dve, v, dve.tensor_scalar(rs[:], mv[:, :, 1], EPS, None, ALU.add))
    wait(act, v, v.now())
    a.up(act.activation(rs[:], rs[:], ACT.Sqrt))
    wait(dve, a, a.now())
    chain(dve, v, dve.reciprocal(rs[:], rs[:]))
    for t in range(NT):
        v.up(dve.tensor_scalar(T[:, t, :], T[:, t, :], mv[:, t, 0:1], rs[:, t:t + 1], ALU.subtract, ALU.mult))
    wait(dve, v, v.now())


def ffn2(nc, g, gfc1, gfc1_b, gfc2, gfc2_b, W1, b1, W2, b2, ln_g, ln_b, tW1, tb1, tW2, tb2, tg, tb):
    dve, pe, act, sp, pool = nc.vector, nc.tensor, nc.scalar, nc.sync, nc.gpsimd
    NE, F = tb1.shape
    FC = F // 128
    with stage(nc, g) as s:
        v, a, q, d = s.cnt("v"), s.cnt("a"), s.cnt("q"), s.cnt("d")
        XT, XN = s.sb("XT", [128, KC, N]), s.sb("XN", [TP, NT, D])
        G1, G2 = s.sb("G1", [128, KC, D]), s.sb("G2", [128, KC, NE])
        g1b, g2b = s.sb("g1b", [128, KC]), s.sb("g2b", [NE, 1])
        w1, w2 = s.sb("w1", [128, KC, F]), s.sb("w2", [128, FC, D])
        t1, t2 = s.sb("t1", [128, NE, KC * F]), s.sb("t2", [128, NE, FC * D])
        b1c, tb1r, tb2r = s.sb("b1c", [128, FC]), s.sb("tb1r", [NE, F]), s.sb("tb2r", [NE, D])
        b2m, lng, lnb = s.sb("b2m", [TP, D]), s.sb("lng", [TP, D]), s.sb("lnb", [TP, D])
        tl, l8 = s.sb("tl", [NE, 2, D]), s.sb("l8", [NE, 2, D])
        loads = [(G1[:], gfc1.rearrange("(c p) n -> p c n", p=128)), (G2[:], gfc2.rearrange("(c p) n -> p c n", p=128)),
                 (g1b[:], gfc1_b), (g2b[:], gfc2_b.rearrange("(e a) -> e a", a=1)),
                 (w1[:], W1.rearrange("(c p) n -> p c n", p=128)), (w2[:], W2.rearrange("(c p) n -> p c n", p=128)),
                 (b1c[:], b1), (tb1r[:], tb1), (tb2r[:], tb2), (b2m[:], bcast(b2, TP)), (lng[:], bcast(ln_g, TP)),
                 (lnb[:], bcast(ln_b, TP)), (tl[:, 0, :], tg), (tl[:, 1, :], tb), (l8[:, 0, :], bcast(ln_g, NE)),
                 (l8[:, 1, :], bcast(ln_b, NE))]
        for e in range(NE):
            loads.append((t1[:, e, :].rearrange("p (c n) -> p c n", n=F), tW1[e].rearrange("(c p) n -> p c n", p=128)))
        for e in range(NE):
            loads.append((t2[:, e, :].rearrange("p (c n) -> p c n", n=D), tW2[e].rearrange("(c p) n -> p c n", p=128)))
        for dst, src in loads:
            d.up(sp.dma_start(dst, src), 16)

        def consume(k, u, xT, used):
            used.up_now(pe)
        norm_tiles(nc, g, s, consume, {}, XT=XT, XN=XN)
        nc.all_engine_barrier()
        for e in (pe, act, dve):
            wait(e, d, d.now())
        gsum, gh, gsr = s.sb("gsum", [128, KC, 3]), s.sb("gh", [128, 2, 512]), s.sb("gsr", [128, KC])
        n = 0
        for m in range(KC):
            for k, (x0, x1) in enumerate(PIECES):
                if n >= 4:
                    wait(pe, a, a.now() - 3)
                for c in range(KC):
                    ins = pe.matmul(g.PS[:, n % 4, 0:x1 - x0], G1[:, c, m * 128:(m + 1) * 128], XT[:, c, x0:x1],
                                    start=(c == 0), stop=(c == KC - 1))
                wait(act, q, q.up(ins))
                if n >= 2:
                    wait(act, a, a.now() - 1)
                a.up(act.activation(gh[:, n % 2, 0:x1 - x0], g.PS[:, n % 4, 0:x1 - x0], ACT.Relu,
                                    bias=g1b[:, m:m + 1], accum_out=gsum[:, m, k:k + 1]))
                n += 1
        wait(dve, a, a.now())
        chain(dve, v, dve.tensor_reduce(gsr[:], gsum[:], AX, ALU.add))
        wait(pe, v, v.now())
        for c in range(KC):
            ins = pe.matmul(g.PS[0:NE, 4, 0:1], G2[:, c, :], gsr[:, c:c + 1], start=(c == 0), stop=(c == KC - 1))
        wait(dve, q, q.up(ins))
        gc, gd, gb = s.sb("gc", [NE, 1]), s.sb("gd", [NE, NE]), s.sb("gb", [128, NE])
        g8 = s.sb("g8", [NE, TP])
        chain(dve, v, dve.scalar_tensor_tensor(gc[:], g.PS[0:NE, 4, 0:1], 1.0 / N, g2b[:], ALU.mult, ALU.add))
        v.up(dve.tensor_scalar(gd[:], g.ident[0:NE, 0:NE], gc[:, 0:1], None, ALU.mult))
        v.up(dve.tensor_scalar(g8[:], g.ones[0:NE, 0:TP], gc[:, 0:1], None, ALU.mult))
        chain(dve, v, dve.tensor_tensor(tl[:], tl[:], l8[:], ALU.subtract))
        wait(pe, v, v.now())
        pe.matmul(g.PS[:, 5, 0:NE], g.ones[0:NE, :], gd[:], start=True, stop=True)
        for f in range(FC):
            pe.matmul(g.PS[:, 4, 8 + f:9 + f], tb1r[:, f * 128:(f + 1) * 128], gc[:], start=True, stop=True)
        pe.matmul(g.PS[0:TP, 6, :], g8[:], tb2r[:], start=True, stop=True)
        pe.matmul(g.PS[0:TP, 7, :], g.ones[0:NE, 0:TP], tl[:, 0, :], start=True, stop=True)
        ins = pe.matmul(g.PS[0:TP, 0, :], g.ones[0:NE, 0:TP], tl[:, 1, :], start=True, stop=True)
        wait(dve, q, q.up(ins))
        v.up(dve.tensor_copy(gb[:], g.PS[:, 5, 0:NE]))
        v.up(dve.tensor_tensor(b1c[:], b1c[:], g.PS[:, 4, 8:8 + FC], ALU.add))
        v.up(dve.tensor_tensor(b2m[:], b2m[:], g.PS[0:TP, 6, :], ALU.add))
        v.up(dve.scalar_tensor_tensor(lng[:], g.PS[0:TP, 7, :], 0.03, lng[:], ALU.mult, ALU.add))
        chain(dve, v, dve.scalar_tensor_tensor(lnb[:], g.PS[0:TP, 0, :], 0.03, lnb[:], ALU.mult, ALU.add))
        merged = v.now()
        w1f, w2f = w1[:].rearrange("p c n -> p (c n)"), w2[:].rearrange("p c n -> p (c n)")
        for e in range(NE):
            chain(dve, v, dve.scalar_tensor_tensor(w1f, t1[:, e, :], gb[:, e:e + 1], w1f, ALU.mult, ALU.add))
        wait(pe, v, v.now())
        for e in range(NE):
            chain(dve, v, dve.scalar_tensor_tensor(w2f, t2[:, e, :], gb[:, e:e + 1], w2f, ALU.mult, ALU.add))
        hT = s.sb("hT", [128, FC, N])
        p, full = s.cnt("p"), [TP, NT, D]
        wait(pool, v, merged)
        wait(pool, d, d.now())
        p.up(pool.tensor_tensor(XN[:], XN[:], b2m[:, None, :].to_broadcast(full), ALU.add))
        p.up(pool.tensor_tensor(g.X[:], g.X[:], lnb[:, None, :].to_broadcast(full), ALU.add))
        wait(act, v, merged)
        for f in range(FC):
            for k, (x0, x1) in enumerate(PIECES):
                for c in range(KC):
                    ins = pe.matmul(g.PS[:, 1 + 3 * f + k, 0:x1 - x0], w1[:, c, f * 128:(f + 1) * 128], XT[:, c, x0:x1],
                                    start=(c == 0), stop=(c == KC - 1))
                wait(act, q, q.up(ins))
                a.up(act.activation(hT[:, f, x0:x1], g.PS[:, 1 + 3 * f + k, 0:x1 - x0], ACT.Relu, bias=b1c[:, f:f + 1]))
        wait(pe, a, a.now())
        wait(pe, v, v.now())
        wait(dve, p, p.now() - 1)
        for t in range(NT):
            if t >= 2:
                wait(pe, v, v.now() - 1)
            for f in range(FC):
                ins = pe.matmul(g.PS[0:TP, t % 2, :], hT[:, f, t * TP:(t + 1) * TP], w2[:, f, :],
                                start=(f == 0), stop=(f == FC - 1))
            wait(dve, q, q.up(ins))
            v.up(dve.tensor_tensor(XN[:, t, :], XN[:, t, :], g.PS[0:TP, t % 2, :], ALU.add))
        wait(dve, v, v.now())
        norm_all(nc, s, XN, v, a)
        chain(dve, v, dve.tensor_tensor(XN[:], XN[:], lng[:, None, :].to_broadcast(full), ALU.mult))
        wait(dve, p, p.now())
        chain(dve, v, dve.tensor_tensor(g.X[:], g.X[:], XN[:], ALU.add))


def gnn3(nc, g, Ws, Wn, bias, gamma, beta):
    dve, pe, act, sp, pool = nc.vector, nc.tensor, nc.scalar, nc.sync, nc.gpsimd
    with stage(nc, g) as s:
        v, a, d = s.cnt("v"), s.cnt("a"), s.cnt("d")
        Wt = [s.sb(f"W{w}", [128, KC, D]) for w in range(2)]
        S, H = s.sb("S", [TP, NT, D]), s.sb("H", [TP, NT, D])
        cst, inv, y = s.sb("cst", [TP, 3, D]), s.sb("inv", [TP, NT]), s.sb("y", [TP, NT, 256])
        for w, src in enumerate((Ws, Wn)):
            d.up(sp.dma_start(Wt[w][:], src.rearrange("(c p) n -> p c n", p=128)), 16)
        for k, w in enumerate((bias, gamma, beta)):
            d.up(sp.dma_start(cst[:, k, :], bcast(w, TP)), 16)
        chain(dve, v, dve.tensor_scalar(inv[:], g.deg[:], 1.0, None, ALU.max))
        chain(dve, v, dve.reciprocal(inv[:], inv[:]))
        ev = s.cnt("ev", dve, 4)

        def consume(k, u, xT, used):
            wait(pe, ev, ev.now() - 2)
            for w in range(2):
                for c in range(KC):
                    ins = pe.matmul(g.PS[0:TP, 2 + 2 * u + w, :], xT[:, c, :], Wt[w][:, c, :],
                                    start=(c == 0), stop=(c == KC - 1))
            wait(dve, used, used.up(ins))
            ev.up(dve.tensor_tensor(row(S, k), g.PS[0:TP, 2 + 2 * u, :], cst[:, 0, :], ALU.add))
            ev.up(dve.tensor_scalar(row(H, k), g.PS[0:TP, 3 + 2 * u, :], 1.0, None, ALU.mult))

        norm_tiles(nc, g, s, consume, {ev: 4}, loaded=(d,))
        wait(pe, ev, ev.now())
        wait(dve, ev, ev.now())
        full = [TP, NT, D]
        own, p = s.sb("own", full), s.cnt("p")
        wait(pool, ev, ev.now())
        wait(pool, v, v.now())
        wait(pool, d, d.now())
        p.up(pool.tensor_tensor(own[:], H[:], inv[:, :, None].to_broadcast(full), ALU.mult))
        wait(pool, p, p.now())
        p.up(pool.tensor_tensor(S[:], S[:], own[:], ALU.subtract))
        p.up(pool.tensor_tensor(g.X[:], g.X[:], cst[:, 2:3, :].to_broadcast(full), ALU.add))

        def finish(half, ps, out):
            c = slice(half * 256, half * 256 + 256)
            wait(dve, p, p.now())
            chain(dve, out, dve.tensor_tensor(y[:], ps, inv[:, :, None].to_broadcast([TP, NT, 256]), ALU.mult))
            chain(dve, v, dve.tensor_tensor(S[:, :, c], S[:, :, c], y[:], ALU.add))

        aggregate(nc, g, s, g.CT, H, finish)
        norm_all(nc, s, S, v, a)
        chain(dve, v, dve.tensor_tensor(S[:], S[:], cst[:, 1:2, :].to_broadcast(full), ALU.mult))
        chain(dve, v, dve.tensor_tensor(g.X[:], g.X[:], S[:], ALU.add))


def ffn3(nc, g, Wr, br, Wu, bu, Wd, bd):
    dve, pe, act, sp, pool = nc.vector, nc.tensor, nc.scalar, nc.sync, nc.gpsimd
    NE, F = Wd.shape[0], Wd.shape[1]
    NG = Wu.shape[0]
    GS = NE // NG
    K = N // NE
    SL = -(-K // 8) * 8
    FP = 105
    FM = F // FP
    SG = GS * SL
    with stage(nc, g) as s:
        v, a, q, d = s.cnt("v"), s.cnt("a"), s.cnt("q"), s.cnt("d")
        WU = [s.sb(f"wu{u}", [128, KC, F]) for u in range(1)]
        WD_ = [s.sb(f"wd{u}", [FP, FM, D]) for u in range(GS)]
        bdb = [s.sb(f"bdb{u}", [SL, D]) for u in range(GS)]
        buT = [s.sb(f"buT{u}", [FP, FM]) for u in range(1)]
        L = logits(nc, g, s, Wr.rearrange("(c p) e -> p c e", p=128), br, NE, dram=g.XND)
        d.up(sp.dma_start(g.Y.rearrange("(t p) d -> p t d", p=TP), g.X[:]), 16)
        softmax_rows(nc, s, L, NE, v, a)
        WT = s.sb("WT", [NE, N])
        to_experts(nc, g, s, L, WT, NE, v, q)
        sw, si = top_slots(nc, g, s, WT, NE, SL, K, v, q, GS)
        wait(pool, v, v.now())
        wait(pool, d, d.now())
        wait(dve, d, d.now())
        xg = s.sb("xg", [SL, GS, D])
        xgT = s.sb("xgT", [128, KC, SG])
        hT = s.sb("hT", [FP, FM, SG])
        wo = g.X[0:SL, 0:GS, :]
        gi, ci = s.sb("gi", [SL, GS], I32), s.sb("ci", [SL, GS], I32)
        lu, lw = s.cnt("lu"), [s.cnt(f"lw{k}") for k in range(GS)]
        gs, po = s.dma_cnt("gathered"), s.cnt("pool_steps", dve, 1)
        tr, tc = s.cnt("transposed", dve, 1), s.cnt("transposed_copied", dve, 1)
        mu, sl = s.cnt("up", dve, FM), s.cnt("silu", dve, FM)
        md, ev = s.cnt("down", dve, GS), s.cnt("weighted", dve, 2 * GS)
        sc, sd = s.dma_cnt("scattered"), s.cnt("scatter_over", dve, 2 * GS)
        go = s.cnt("go")
        per = {go: 1, lu: 32, gs: 16 * GS, po: 4, tr: 1, tc: 1, mu: FM, sl: FM, md: GS, ev: 2 * GS,
               sc: 16 * GS, sd: 2 * GS}
        per.update({c: 32 for c in lw})

        def gather(e):
            po.up(pool.tensor_copy(gi[:], si[:, 0, ds(e, GS)]))
            wait(pool, po, po.now())
            po.up_now(pool)
            for k in range(GS):
                gs.up(pool.indirect_dma_start(out=xg[:, k, :], out_offset=None, in_=g.XND,
                                              in_offset=bass.IndirectOffsetOnAxis(ap=gi[:, k:k + 1], axis=0)), 16)

        gather(0)
        with loop(nc, NG, per) as i:
            e0 = i * GS
            wait(sp, mu, mu.ago(FM))
            lu.up(sp.dma_start(WU[0][:], Wu[ds(i, 1)].rearrange("a (c p) n -> p (a c) n", p=128)), 16)
            wait(sp, sl, sl.ago(FM))
            lu.up(sp.dma_start(buT[0][:], bu[ds(i, 1)].rearrange("a (p m) -> p (a m)", m=FM)), 16)
            for k in range(GS):
                wait(sp, ev, ev.ago(2 * k + 2))
                lw[k].up(sp.dma_start(WD_[k][:], Wd[ds(e0 + k, 1)].rearrange("a (p m) n -> p (a m) n", m=FM)), 16)
                lw[k].up(sp.dma_start(bdb[k][:], bcast(bd[ds(e0 + k, 1)].rearrange("a n -> (a n)"), SL)), 16)
            wait(pe, gs, gs.now())
            wait(pe, sl, sl.ago(FM))
            go.up_now(pe)
            for c in range(KC):
                for k in range(GS):
                    ins = pe.transpose(g.PS[:, c // 2, (c % 2) * SG + k * SL:(c % 2) * SG + (k + 1) * SL],
                                       xg[:, k, c * 128:(c + 1) * 128], g.ident[0:SL, 0:SL])
            tr.up(ins)
            wait(pool, tr, tr.now())
            gather(e0 + GS)
            wait(dve, tr, tr.now())
            wait(dve, mu, mu.ago(FM))
            tc.up(dve.tensor_copy(xgT[:].rearrange("p (b c) n -> p b (c n)", b=2), g.PS[:, 0:2, 0:2 * SG]))
            wait(pe, tc, tc.now())
            wait(pe, lu, lu.now())
            wait(act, lu, lu.now())
            wait(act, md, md.ago(GS))
            first = sl.now()
            for m in range(FM):
                bk = m % 4
                wait(pe, sl, first + m - 3)
                for c in range(KC):
                    ins = pe.matmul(g.PS[0:FP, bk, 0:SG], WU[0][:, c, m:F:FM], xgT[:, c, :],
                                    start=(c == 0), stop=(c == KC - 1))
                mu.up(ins)
                wait(act, mu, mu.now())
                sl.up(act.activation(hT[:, m, :], g.PS[0:FP, bk, 0:SG], ACT.Silu, bias=buT[0][:, m:m + 1]))
            wait(pe, sl, sl.now())
            po.up(pool.tensor_copy(ci[:], si[:, 0, ds(e0, GS)]))
            wait(pool, po, po.now())
            po.up_now(pool)
            for k in range(GS):
                wait(pe, lw[k], lw[k].now())
                wait(pe, ev, ev.ago(2 * k + 2))
                for m in range(FM):
                    ins = pe.matmul(g.PS[0:SL, 4 + k, :], hT[:, m, k * SL:(k + 1) * SL], WD_[k][:, m, :],
                                    start=(m == 0), stop=(m == FM - 1))
                md.up(ins)
                wait(dve, md, md.now())
                wait(dve, lw[k], lw[k].now())
                wait(dve, sd, sd.ago(2 * k + 2))
                chain(dve, ev, dve.tensor_tensor(wo[:, k, :], g.PS[0:SL, 4 + k, :], bdb[k][:], ALU.add))
                ev.up(dve.tensor_scalar(wo[:, k, :], wo[:, k, :], sw[:, 0, ds(e0 + k, 1)], None, ALU.mult))
                wait(pool, ev, ev.now())
                sd.up_now(pool)
                sc.up(pool.indirect_dma_start(out=g.Y, out_offset=bass.IndirectOffsetOnAxis(
                    ap=ci[:, k:k + 1], axis=0), in_=wo[:, k, :], in_offset=None, compute_op=ALU.add), 16)
                wait(pool, sc, sc.now())
                sd.up_now(pool)
        wait(sp, sc, sc.now())
        wait(sp, gs, gs.now())


def program(nc, A, out):
    ctx = ExitStack()
    with ctx:
        g = Env()
        g.ctx = ctx
        g.k = 0
        def dram(name, shape, dt=F32):
            return nc.dram_tensor(name, shape, dt, kind="Internal").ap()
        g.recd = dram("recd", (NB * BLK, 8))
        g.XND, g.Y = dram("XND", (N, D)), dram("Y", (N, D))
        g.HT = dram("HT", (N, D + 8))
        g.CT, g.MASK = dram("CT", (NT * 128, N)), dram("MASK", (N, N), BF16)
        g.blk_tile = ctx.enter_context(nc.sbuf_tensor("blk_tile", [1, NB + 1], I32))
        g.srcidx = ctx.enter_context(nc.sbuf_tensor("srcidx", [128, (NB + 1) * CH], I32))
        g.ae_mean = ctx.enter_context(nc.sbuf_tensor("ae_mean", [TP, 4], F32))
        constants(nc, g, ctx, A["x"])
        with stage(nc, g) as s:
            H = s.sb("H", [TP, NT, D])
            group_edges(nc, g, A["src"], A["dst"], A["edge_attr_4"], A["L1_gnn_W_edge"], A["L1_gnn_att_edge"], H,
                        A["L0_gnn_W"])
            count_matrix(nc, g)
            gnn0(nc, g, H, A["L0_gnn_b"])
        ffn0(nc, g, A["L0_ffn_gate_w"], A["L0_ffn_gate_b"], A["L0_ffn_w1"], A["L0_ffn_b1"], A["L0_ffn_w2"], A["L0_ffn_b2"])
        gnn1(nc, g, *[A["L1_gnn_" + n] for n in ("W", "att_src", "att_dst", "bias", "gamma", "beta")])
        ffn1(nc, g, *[A["L1_ffn_" + n] for n in ("Wr", "br", "W1", "b1", "W2", "b2")])
        gnn2(nc, g, *[A["L2_gnn_" + n] for n in ("W1", "att_src1", "att_dst1", "b1", "W2", "att_src2", "att_dst2", "b2",
                                                "fcW", "fcb")])
        ffn2(nc, g, *[A["L2_ffn_" + n] for n in ("gfc1_w", "gfc1_b", "gfc2_w", "gfc2_b", "W1", "b1", "W2", "b2", "ln_g",
                                                "ln_b", "tv_W1", "tv_b1", "tv_W2", "tv_b2", "tv_ln_g", "tv_ln_b")])
        gnn3(nc, g, *[A["L3_gnn_" + n] for n in ("W_self", "W_neigh", "bias", "gamma", "beta")])
        ffn3(nc, g, *[A["L3_ffn_" + n] for n in ("W_router", "b_router", "W_up", "b_up", "W_down", "b_down")])
        with stage(nc, g) as s:
            d = s.cnt("d")
            d.up(nc.sync.dma_start(out, g.Y), 16)
            wait(nc.sync, d, d.now())


_INS = (
    'x src dst edge_attr_4 '
    'L0_gnn_W L0_gnn_b L0_ffn_gate_w L0_ffn_gate_b '
    'L0_ffn_w1 L0_ffn_b1 L0_ffn_w2 L0_ffn_b2 '
    'L1_gnn_W L1_gnn_W_edge L1_gnn_att_src L1_gnn_att_dst '
    'L1_gnn_att_edge L1_gnn_bias L1_gnn_gamma L1_gnn_beta '
    'L1_ffn_Wr L1_ffn_br L1_ffn_W1 L1_ffn_b1 '
    'L1_ffn_W2 L1_ffn_b2 L2_gnn_W1 L2_gnn_att_src1 '
    'L2_gnn_att_dst1 L2_gnn_b1 L2_gnn_W2 L2_gnn_att_src2 '
    'L2_gnn_att_dst2 L2_gnn_b2 L2_gnn_fcW L2_gnn_fcb '
    'L2_ffn_gfc1_w L2_ffn_gfc1_b L2_ffn_gfc2_w L2_ffn_gfc2_b '
    'L2_ffn_W1 L2_ffn_b1 L2_ffn_W2 L2_ffn_b2 '
    'L2_ffn_ln_g L2_ffn_ln_b L2_ffn_tv_W1 L2_ffn_tv_b1 '
    'L2_ffn_tv_W2 L2_ffn_tv_b2 L2_ffn_tv_ln_g L2_ffn_tv_ln_b '
    'L3_gnn_W_self L3_gnn_W_neigh L3_gnn_bias L3_gnn_gamma '
    'L3_gnn_beta L3_ffn_W_router L3_ffn_b_router L3_ffn_W_up '
    'L3_ffn_b_up L3_ffn_W_down L3_ffn_b_down '
).split()
_TURNED = ["L0_ffn_gate_w", "L2_ffn_gfc1_w", "L2_ffn_gfc2_w", "L2_ffn_W1", "L2_ffn_W2", "L2_ffn_tv_W1", "L2_ffn_tv_W2",
           "L3_gnn_W_self", "L3_gnn_W_neigh"]
_COLUMNS = ["L2_ffn_gfc1_b", "L2_ffn_b1"]


def kernel(**inputs):
    import numpy as _np
    import concourse.bacc as _bacc
    from concourse import mybir as _mybir
    from concourse.bass_utils import run_bass_kernel_spmd as _run
    nc = _bacc.Bacc("TRN2", target_bir_lowering=False, num_devices=1)
    arrays, A = {}, {}
    for name in _INS:
        a = _np.asarray(inputs[name])
        a = a.reshape(-1, 128).T if name in _COLUMNS else a.swapaxes(-1, -2) if name in _TURNED else a
        a = _np.ascontiguousarray(a)
        arrays[f"in_{name}"] = a
        A[name] = nc.dram_tensor(f"in_{name}", a.shape, _mybir.dt.from_np(a.dtype), kind="ExternalInput").ap()
    out = nc.dram_tensor("out_0", (N, D), F32, kind="ExternalOutput").ap()
    program(nc, A, out)
    return _run(nc, [arrays], core_ids=[0]).results[0]["out_0"]
```
